# Optimizing a Trainium2 kernel written in Bass

```python
import numpy as np
import jax
import jax.numpy as jnp

def _softmax(x, axis=-1):
    return jax.nn.softmax(x, axis=axis)

def _gelu(x):
    return jax.nn.gelu(x, approximate=True)

def _silu(x):
    return jax.nn.silu(x)

def _sigmoid(x):
    return jax.nn.sigmoid(x)

def _layernorm(x, axis=-1, eps=1e-05):
    m = jnp.mean(x, axis=axis, keepdims=True)
    v = jnp.var(x, axis=axis, keepdims=True)
    return (x - m) / jnp.sqrt(v + eps)

def _scatter_add(tgt, idx, src, axis=0):
    return tgt.at[idx].add(src)

def _segment_sum(src, seg, n):
    return jax.ops.segment_sum(src, seg, n)
kernel_name = 'mk_flamingo_gated_d2_seqx_r8_e97917'

def setup_inputs(seed: int=0):
    np.random.seed(seed)
    _w = jnp.asarray

    def _rec_inputs():
        import jax
        import jax.numpy as jnp
        _rk = jax.random.key(seed)
        x = 7.22e-05 + 1 * jax.random.normal(jax.random.fold_in(_rk, 1), (32, 64, 512), jnp.float32)
        _lenS = 64 - jax.random.randint(jax.random.fold_in(_rk, 7), (32,), 0, max(1, 64 // 4) + 1, jnp.int32)
        _lenS2 = 64 - jax.random.randint(jax.random.fold_in(_rk, 8), (32,), 0, max(1, 64 // 4) + 1, jnp.int32)
        _ctx_4096P = jax.random.normal(jax.random.fold_in(_rk, 11), (32, 16, 512), jnp.float32)
        _ctx_4096c = jax.random.dirichlet(jax.random.fold_in(_rk, 511), 0.3 * jnp.ones((16,), jnp.float32), (32, 64))
        _ctx_4096t = jnp.einsum('bsk,bkd->bsd', _ctx_4096c, _ctx_4096P)
        _ctx_4096t = _ctx_4096t * jax.lax.rsqrt(jnp.mean(jnp.square(_ctx_4096t)) + 1e-12) * 0.953939
        ctx_4096 = 4.13588e-05 + 0.999923 * (_ctx_4096t + 0.3 * jax.random.normal(jax.random.fold_in(_rk, 611), (32, 64, 512), jnp.float32))
        _g = jax.random.normal(jax.random.fold_in(_rk, 9001), (2, 2), jnp.float32)
        _g = jnp.sign(_g) * jnp.maximum(jnp.abs(_g), 1.0) + (_g == 0) * 1.0
        g_xattn = _g[0]
        g_ffn = _g[1]
        return (x, ctx_4096, g_xattn, g_ffn)
    x, ctx_4096, g_xattn, g_ffn = _rec_inputs()

    def _L0_xattn_setup():
        import jax, jax.numpy as jnp
        import numpy as np
        HEADS = 8
        WINDOW = 16

        def _pointwise(W, b, t):
            return jnp.einsum('oc,bct->bot', W, t) + b[None, :, None]
        key = jax.random.key(seed)
        ks = jax.random.split(key, 10)
        B, C, T = (4, 64, 512)
        s = 0.02
        return {'x': jax.random.normal(ks[0], (B, C, T), jnp.float32), 'cond': jax.random.normal(ks[1], (B, C, T), jnp.float32), 'Wq': jax.random.normal(ks[2], (C, C), jnp.float32) * s, 'bq': jnp.zeros((C,), jnp.float32), 'Wk': jax.random.normal(ks[3], (C, C), jnp.float32) * s, 'bk': jnp.zeros((C,), jnp.float32), 'Wv': jax.random.normal(ks[4], (C, C), jnp.float32) * s, 'bv': jnp.zeros((C,), jnp.float32), 'Wo': jax.random.normal(ks[5], (C, C), jnp.float32) * s, 'bo': jnp.zeros((C,), jnp.float32)}
    _L0_xattn_all = _L0_xattn_setup()
    _L0_xattn_in = {k: v for k, v in _L0_xattn_all.items() if k in ('Wq', 'bq', 'Wk', 'bk', 'Wv', 'bv', 'Wo', 'bo')}
    del _L0_xattn_all

    def _L0_ffn_setup():
        import jax, jax.numpy as jnp
        import numpy as np
        import math
        SQRT7 = math.sqrt(7.0)
        EPS = 1e-05

        def int4_quant(x):
            beta = jnp.mean(jnp.abs(x), axis=-1, keepdims=True)
            x_q = jnp.clip(jnp.round(x * SQRT7 / (beta + EPS)), -8, 7)
            return x_q * (beta * SQRT7) / SQRT7

        def int8_quant(x):
            gamma = jnp.max(jnp.abs(x), axis=-1, keepdims=True)
            x_q = jnp.clip(jnp.round(x * 127.0 / (gamma + EPS)), -128, 127)
            return x_q * gamma / 127.0

        def bitlinear(x, w, scale):
            w_mean = jnp.mean(jnp.abs(w))
            w_q = jnp.clip(jnp.round(w / (w_mean + EPS)), -1.0, 1.0)
            w_eff = w_q * w_mean * scale
            return jnp.einsum('...i,oi->...o', x, w_eff)
        key = jax.random.key(seed)
        ks = jax.random.split(key, 4)
        H, I = (512, 1376)
        B, S = (2, 256)
        x = jax.random.normal(ks[0], (B, S, H), dtype=jnp.float32)
        w_gate = jax.random.uniform(ks[1], (I, H), jnp.float32, -1.0, 1.0) / np.sqrt(H)
        w_up = jax.random.uniform(ks[2], (I, H), jnp.float32, -1.0, 1.0) / np.sqrt(H)
        w_down = jax.random.uniform(ks[3], (H, I), jnp.float32, -1.0, 1.0) / np.sqrt(I)
        ones = jnp.ones((1,), jnp.float32)
        return {'x': x, 'w_gate': w_gate, 'w_up': w_up, 'w_down': w_down, 's_gate': ones, 's_up': ones, 's_down': ones}
    _L0_ffn_all = _L0_ffn_setup()
    _L0_ffn_in = {k: v for k, v in _L0_ffn_all.items() if k in ('w_gate', 'w_up', 'w_down', 's_gate', 's_up', 's_down')}
    del _L0_ffn_all

    def _L1_xattn_setup():
        import jax, jax.numpy as jnp
        import numpy as np
        EMBED = 512
        NUM_Q = 32
        NUM_KV = 8
        GROUPS = NUM_Q // NUM_KV
        HEAD_DIM = EMBED // NUM_Q
        KV_DIM = HEAD_DIM * NUM_KV
        key = jax.random.key(seed)
        ks = jax.random.split(key, 12)
        B, S = (2, 256)
        s = 0.02
        return {'query': jax.random.normal(ks[0], (B, S, EMBED), jnp.float32), 'key': jax.random.normal(ks[1], (B, S, EMBED), jnp.float32), 'value': jax.random.normal(ks[2], (B, S, EMBED), jnp.float32), 'Wq': jax.random.normal(ks[3], (EMBED, EMBED), jnp.float32) * s, 'bq': jnp.zeros((EMBED,), jnp.float32), 'Wk': jax.random.normal(ks[4], (EMBED, KV_DIM), jnp.float32) * s, 'bk': jnp.zeros((KV_DIM,), jnp.float32), 'Wv': jax.random.normal(ks[5], (EMBED, KV_DIM), jnp.float32) * s, 'bv': jnp.zeros((KV_DIM,), jnp.float32), 'Wo': jax.random.normal(ks[6], (EMBED, EMBED), jnp.float32) * s, 'bo': jnp.zeros((EMBED,), jnp.float32)}
    _L1_xattn_all = _L1_xattn_setup()
    _L1_xattn_in = {k: v for k, v in _L1_xattn_all.items() if k in ('Wq', 'bq', 'Wk', 'bk', 'Wv', 'bv', 'Wo', 'bo')}
    del _L1_xattn_all

    def _L1_ffn_setup():
        import jax, jax.numpy as jnp
        import numpy as np
        IN_F = 512
        OUT_F = 512
        C = 32
        NCL = 32
        SUB = IN_F // C
        CLS = OUT_F // NCL
        SIGMA = 10.0
        THRESH = 0.5

        def _expand(codes, codebooks):
            w = codebooks[jnp.arange(codes.shape[0])[:, None], codes]
            return jnp.transpose(w, (1, 0, 2)).reshape(codes.shape[1], -1)
        key = jax.random.key(seed)
        ks = jax.random.split(key, 6)
        x = jax.random.normal(ks[0], (4, 256, IN_F), dtype=jnp.float32)
        codebooks = jax.random.normal(ks[1], (C, 32, SUB), dtype=jnp.float32) * 0.025
        centroids = jax.random.randint(ks[2], (NCL, C), 0, 32, dtype=jnp.int32)
        codes = jnp.repeat(centroids, CLS, axis=0)
        n_pert = max(1, round(0.25 * C))
        psel = jax.random.randint(ks[3], (OUT_F, n_pert), 0, C, dtype=jnp.int32)
        prep = jax.random.randint(ks[4], (OUT_F, n_pert), 0, 32, dtype=jnp.int32)
        rows = jnp.arange(OUT_F)[:, None]
        codes = codes.at[rows, psel].set(prep)
        bound = 1.0 / np.sqrt(IN_F)
        bias = jax.random.uniform(ks[5], (OUT_F,), dtype=jnp.float32, minval=-bound, maxval=bound)
        ln_weight = jnp.ones((NCL,), dtype=jnp.float32) * SIGMA
        return {'x': x, 'codebooks': codebooks, 'bias': bias, 'ln_weight': ln_weight, 'codes': codes.T.astype(jnp.int32), 'centroids': centroids.T.astype(jnp.int32)}
    _L1_ffn_all = _L1_ffn_setup()
    _L1_ffn_in = {k: v for k, v in _L1_ffn_all.items() if k in ('codebooks', 'bias', 'ln_weight', 'codes', 'centroids')}
    del _L1_ffn_all
    return {'x': x, 'ctx_4096': ctx_4096, 'g_xattn': g_xattn, 'g_ffn': g_ffn, 'L0_xattn_Wq': _L0_xattn_in['Wq'], 'L0_xattn_bq': _L0_xattn_in['bq'], 'L0_xattn_Wk': _L0_xattn_in['Wk'], 'L0_xattn_bk': _L0_xattn_in['bk'], 'L0_xattn_Wv': _L0_xattn_in['Wv'], 'L0_xattn_bv': _L0_xattn_in['bv'], 'L0_xattn_Wo': _L0_xattn_in['Wo'], 'L0_xattn_bo': _L0_xattn_in['bo'], 'L0_ffn_w_gate': _L0_ffn_in['w_gate'], 'L0_ffn_w_up': _L0_ffn_in['w_up'], 'L0_ffn_w_down': _L0_ffn_in['w_down'], 'L0_ffn_s_gate': _L0_ffn_in['s_gate'], 'L0_ffn_s_up': _L0_ffn_in['s_up'], 'L0_ffn_s_down': _L0_ffn_in['s_down'], 'L1_xattn_Wq': _L1_xattn_in['Wq'], 'L1_xattn_bq': _L1_xattn_in['bq'], 'L1_xattn_Wk': _L1_xattn_in['Wk'], 'L1_xattn_bk': _L1_xattn_in['bk'], 'L1_xattn_Wv': _L1_xattn_in['Wv'], 'L1_xattn_bv': _L1_xattn_in['bv'], 'L1_xattn_Wo': _L1_xattn_in['Wo'], 'L1_xattn_bo': _L1_xattn_in['bo'], 'L1_ffn_codebooks': _L1_ffn_in['codebooks'], 'L1_ffn_bias': _L1_ffn_in['bias'], 'L1_ffn_ln_weight': _L1_ffn_in['ln_weight'], 'L1_ffn_codes': _L1_ffn_in['codes'], 'L1_ffn_centroids': _L1_ffn_in['centroids']}

def reference(x, ctx_4096, g_xattn, g_ffn, L0_xattn_Wq, L0_xattn_bq, L0_xattn_Wk, L0_xattn_bk, L0_xattn_Wv, L0_xattn_bv, L0_xattn_Wo, L0_xattn_bo, L0_ffn_w_gate, L0_ffn_w_up, L0_ffn_w_down, L0_ffn_s_gate, L0_ffn_s_up, L0_ffn_s_down, L1_xattn_Wq, L1_xattn_bq, L1_xattn_Wk, L1_xattn_bk, L1_xattn_Wv, L1_xattn_bv, L1_xattn_Wo, L1_xattn_bo, L1_ffn_codebooks, L1_ffn_bias, L1_ffn_ln_weight, L1_ffn_codes, L1_ffn_centroids):
    import jax
    import jax.numpy as jnp

    def _L0_xattn_ref(x, cond, Wq, bq, Wk, bk, Wv, bv, Wo, bo):
        import jax, jax.numpy as jnp
        import numpy as np
        HEADS = 8
        WINDOW = 16

        def _pointwise(W, b, t):
            return jnp.einsum('oc,bct->bot', W, t) + b[None, :, None]
        B, C, T = x.shape
        H, W = (HEADS, WINDOW)
        hd = C // H
        scale = hd ** (-0.5)
        pad_left = W // 2
        pad_right = W - pad_left - 1
        q = _pointwise(Wq, bq, x)
        k = _pointwise(Wk, bk, cond)
        v = _pointwise(Wv, bv, cond)
        k = jnp.pad(k, ((0, 0), (0, 0), (pad_left, pad_right)))
        v = jnp.pad(v, ((0, 0), (0, 0), (pad_left, pad_right)))
        idx = jnp.arange(T)[:, None] + jnp.arange(W)[None, :]
        k_win = k[:, :, idx].reshape(B, H, hd, T, W)
        v_win = v[:, :, idx].reshape(B, H, hd, T, W)
        qh = q.reshape(B, H, hd, T)
        dots = jnp.einsum('bhdt,bhdtw->bhtw', qh, k_win) * scale
        attn = jax.nn.softmax(dots, axis=-1)
        out = jnp.einsum('bhtw,bhdtw->bhdt', attn, v_win)
        out = out.reshape(B, C, T)
        return _pointwise(Wo, bo, out)

    def _L0_ffn_ref(x, w_gate, w_up, w_down, s_gate, s_up, s_down):
        import jax, jax.numpy as jnp
        import numpy as np
        import math
        SQRT7 = math.sqrt(7.0)
        EPS = 1e-05

        def int4_quant(x):
            beta = jnp.mean(jnp.abs(x), axis=-1, keepdims=True)
            x_q = jnp.clip(jnp.round(x * SQRT7 / (beta + EPS)), -8, 7)
            return x_q * (beta * SQRT7) / SQRT7

        def int8_quant(x):
            gamma = jnp.max(jnp.abs(x), axis=-1, keepdims=True)
            x_q = jnp.clip(jnp.round(x * 127.0 / (gamma + EPS)), -128, 127)
            return x_q * gamma / 127.0

        def bitlinear(x, w, scale):
            w_mean = jnp.mean(jnp.abs(w))
            w_q = jnp.clip(jnp.round(w / (w_mean + EPS)), -1.0, 1.0)
            w_eff = w_q * w_mean * scale
            return jnp.einsum('...i,oi->...o', x, w_eff)
        xq = int4_quant(x)
        gate = bitlinear(xq, w_gate, s_gate)
        up = bitlinear(xq, w_up, s_up)
        gate = jnp.square(jax.nn.relu(gate))
        inter = int8_quant(up * gate)
        return bitlinear(inter, w_down, s_down)

    def _L1_xattn_ref(query, key, value, Wq, bq, Wk, bk, Wv, bv, Wo, bo):
        import jax, jax.numpy as jnp
        import numpy as np
        EMBED = 512
        NUM_Q = 32
        NUM_KV = 8
        GROUPS = NUM_Q // NUM_KV
        HEAD_DIM = EMBED // NUM_Q
        KV_DIM = HEAD_DIM * NUM_KV
        B, S, _ = query.shape
        Q = query @ Wq + bq
        K = key @ Wk + bk
        V = value @ Wv + bv
        Q = Q.reshape(B, S, NUM_KV, GROUPS, HEAD_DIM).transpose(0, 2, 3, 1, 4)
        K = K.reshape(B, S, NUM_KV, HEAD_DIM).transpose(0, 2, 1, 3)
        V = V.reshape(B, S, NUM_KV, HEAD_DIM).transpose(0, 2, 1, 3)
        scale = 1.0 / jnp.sqrt(jnp.asarray(HEAD_DIM, query.dtype))
        scores = jnp.einsum('bhgqd,bhkd->bhgqk', Q, K) * scale
        w = jax.nn.softmax(scores, axis=-1)
        y = jnp.einsum('bhgqk,bhkd->bhgqd', w, V)
        y = y.transpose(0, 3, 1, 2, 4).reshape(B, S, EMBED)
        return y @ Wo + bo

    def _L1_ffn_ref(x, codebooks, bias, ln_weight, codes, centroids):
        import jax, jax.numpy as jnp
        import numpy as np
        IN_F = 512
        OUT_F = 512
        C = 32
        NCL = 32
        SUB = IN_F // C
        CLS = OUT_F // NCL
        SIGMA = 10.0
        THRESH = 0.5

        def _expand(codes, codebooks):
            w = codebooks[jnp.arange(codes.shape[0])[:, None], codes]
            return jnp.transpose(w, (1, 0, 2)).reshape(codes.shape[1], -1)
        shape = x.shape
        x2 = x.reshape(-1, shape[-1])
        cw = _expand(centroids, codebooks)
        dots = x2 @ cw.T
        mu = jnp.mean(dots, axis=-1, keepdims=True)
        var = jnp.var(dots, axis=-1, keepdims=True)
        dots = (dots - mu) * jax.lax.rsqrt(var + 1e-05) * ln_weight
        soft = jax.nn.softmax(dots, axis=-1)
        m = soft > THRESH
        qmask = jnp.any(m, axis=-1)
        cmask = jnp.any(m, axis=0)
        kmask = jnp.repeat(cmask, CLS)
        W = _expand(codes, codebooks)
        y = x2 @ W.T + bias
        y = y * (qmask[:, None] & kmask[None, :]).astype(y.dtype)
        return y.reshape(*shape[:-1], OUT_F)
    x = x + jnp.tanh(g_xattn[0]) * _L0_xattn_ref(_layernorm(x, axis=-1), ctx_4096, L0_xattn_Wq, L0_xattn_bq, L0_xattn_Wk, L0_xattn_bk, L0_xattn_Wv, L0_xattn_bv, L0_xattn_Wo, L0_xattn_bo)
    x = x + jnp.tanh(g_ffn[0]) * _L0_ffn_ref(_layernorm(x, axis=-1), L0_ffn_w_gate, L0_ffn_w_up, L0_ffn_w_down, L0_ffn_s_gate, L0_ffn_s_up, L0_ffn_s_down)
    x = x + jnp.tanh(g_xattn[1]) * _L1_xattn_ref(_layernorm(x, axis=-1), ctx_4096, ctx_4096, L1_xattn_Wq, L1_xattn_bq, L1_xattn_Wk, L1_xattn_bk, L1_xattn_Wv, L1_xattn_bv, L1_xattn_Wo, L1_xattn_bo)
    x = x + jnp.tanh(g_ffn[1]) * _L1_ffn_ref(_layernorm(x, axis=-1), L1_ffn_codebooks, L1_ffn_bias, L1_ffn_ln_weight, L1_ffn_codes, L1_ffn_centroids)
    return x

_drawn_inputs = setup_inputs


def setup_inputs(seed=0):
    import zlib

    import numpy as np

    out = dict(_drawn_inputs(seed))
    spreads = {'g_ffn': (-1.0, 0.6),
     'L0_xattn_bq': (0.0, 0.8),
     'L0_xattn_bk': (0.0, 0.8),
     'L0_xattn_bv': (0.0, 0.762),
     'L0_xattn_bo': (0.0, 0.399),
     'L1_xattn_bq': (0.0, 0.8),
     'L1_xattn_bk': (0.0, 0.8),
     'L1_xattn_bv': (0.0, 0.47),
     'L1_xattn_bo': (0.0, 0.1),
     'L1_ffn_ln_weight': (10.0, 0.2)}
    factors = {'L0_xattn_Wq': 6.466,
     'L0_xattn_Wk': 5.933,
     'L1_xattn_Wq': 8.0,
     'L1_xattn_Wk': 8.0,
     'L1_ffn_bias': 8.0}
    for name, (base, spread) in spreads.items():
        noise = np.random.default_rng([zlib.crc32(name.encode()), seed]).standard_normal(out[name].shape)
        drawn = base * np.exp(spread * noise) if base else spread * noise
        out[name] = jnp.asarray(drawn.astype(out[name].dtype))
    for name, factor in factors.items():
        out[name] = (out[name] * factor).astype(out[name].dtype)
    return out
```

```python
import concourse.bass as bass
from concourse import mybir
from contextlib import ExitStack

F32 = mybir.dt.float32
F32R = mybir.dt.float32r
BF16 = mybir.dt.bfloat16
I32 = mybir.dt.int32
ALU = mybir.AluOpType
ACT = mybir.ActivationFunctionType
AX = mybir.AxisListType

P = 128
B, S, D = 32, 64, 512
N = B * S // P
BPT = P // S
KD = D // P
EPS = 1e-5
ROUND = 1.5 * 2.0 ** 23

FF = 1376
FJ = (FF + P - 1) // P
FR = FF - (FJ - 1) * P
NCH = 4
FC = FF // NCH
SQRT7 = 7.0 ** 0.5


class Steps:

    def __init__(self, eng, sem, tile, per):
        self.eng, self.sem, self.base, self.n = eng, sem, tile * per, 0

    def mark(self, ins):
        ins.then_inc(self.sem, 1)
        self.n += 1

    def done(self, ins):
        self.mark(ins)
        self.eng.wait_ge(self.sem, self.base + self.n)


def over_tiles(eng, body, ahead, behind, reach=1):
    def peeled(first, last):
        for it in range(first, last):
            body(it, it % 2, lambda k, it=it: 0 <= it + k < N, lambda k, n, it=it: it + k >= n)

    steady = lambda *_: True
    lo, hi = 4, N - 2 * reach
    peeled(-ahead, lo)
    with eng.Fori(lo, hi, 2) as it:
        body(it, 0, steady, steady)
        body(it + 1, 1, steady, steady)
    peeled(hi, N + behind)


def setup(nc, io, sh):
    with ExitStack() as c:
        sb = lambda n, s, dt=F32: c.enter_context(nc.sbuf_tensor("w0_" + n, s, dt))
        sem = lambda n: c.enter_context(nc.semaphore("w0_" + n))
        raw_gate, raw_up, raw_down = sb("raw_gate", [P, FJ, D]), sb("raw_up", [P, FJ, D]), sb("raw_down", [P, KD, FF])
        raw = [r[:, :, :].rearrange("p a b -> p (a b)") for r in (raw_gate, raw_up, raw_down)]
        low = sb("low", [P, FJ * D], BF16)
        tern = [sb(f"tern{w}", [P, FJ * D], BF16) for w in range(3)]
        sums, tot, thr = sb("sums", [P, 3, 2]), sb("tot", [P, 3]), sb("thr", [P, 3, 2])
        down = sb("down", [P, 1])
        gates_in = sb("gates_in", [P, 4])
        pT = [c.enter_context(nc.psum_tensor(f"pT{k}", [P, 4, P], BF16)) for k in range(4)]
        pS = c.enter_context(nc.psum_tensor("pS", [P, 6], F32))
        raw_loaded = [sem(f"raw_loaded{w}") for w in range(3)]
        small_loaded, zeroed, constants, identities = sem("small_loaded"), sem("zeroed"), sem("constants"), sem("identities")
        abs_summed, totals, step, ternary = sem("abs_summed"), sem("totals"), sem("vector_step"), sem("ternary")
        transposed, copied_act, copied_dve, gates = sem("transposed"), sem("copied_act"), sem("copied_dve"), sem("gates")
        block = c.enter_context(nc.Block())

        whole = [(P, 0, (FJ - 1) * D), (FR, (FJ - 1) * D, D)]
        parts = [whole, whole, [(P, 0, KD * FF)]]
        groups = []
        for j in range(FJ):
            n = P if j < FJ - 1 else FR
            groups.append((0, [j * D + k * P for k in range(KD)], n, P, sh.gateT[:, :, j * P:j * P + n]))
        for j in range(FJ):
            n = P if j < FJ - 1 else FR
            groups.append((1, [j * D + k * P for k in range(KD)], n, P, sh.upT[:, :, j * P:j * P + n]))
        for j in range(FJ):
            n = P if j < FJ - 1 else FR
            groups.append((2, [o * FF + j * P for o in range(KD)], P, n,
                           sh.downT[0:n, j, :].rearrange("p (o n) -> p o n", n=P)))

        @block.sync
        def _(sp):
            for w, (dst, name) in enumerate(((raw_gate, "L0_ffn_w_gate"), (raw_up, "L0_ffn_w_up"))):
                src = io[name]
                sp.dma_start(dst[:, 0:FJ - 1, :], src[0:(FJ - 1) * P, :].rearrange("(j p) k -> p j k", p=P)).then_inc(raw_loaded[w], 16)
                sp.dma_start(dst[0:FR, FJ - 1, :], src[(FJ - 1) * P:FF, :]).then_inc(raw_loaded[w], 16)
            sp.dma_start(raw_down[:, :, :], io["L0_ffn_w_down"].rearrange("(o p) f -> p o f", p=P)).then_inc(raw_loaded[2], 16)

        @block.gpsimd
        def _(pool):
            for n, (g, k) in enumerate((("g_xattn", 0), ("g_ffn", 0), ("g_xattn", 1), ("g_ffn", 1))):
                pool.dma_start(gates_in[:, n:n + 1], io[g][k:k + 1].rearrange("(a n) -> a n", a=1).broadcast_to([P, 1])).then_inc(small_loaded, 16)
            for n, g in enumerate(("L0_ffn_s_gate", "L0_ffn_s_up", "L0_ffn_s_down")):
                pool.dma_start(sh.scales[:, n:n + 1], io[g].rearrange("(a n) -> a n", a=1).broadcast_to([P, 1])).then_inc(small_loaded, 16)
            pool.memset(sh.ident[:, :], 0.0).then_inc(zeroed, 1)
            pool.memset(sh.identb[:, :], 0.0).then_inc(zeroed, 1)
            pool.memset(sh.ones[:, :], 1.0).then_inc(constants, 1)
            pool.memset(sums[:, :, :], 0.0).then_inc(constants, 1)
            pool.wait_ge(zeroed, 2)
            for m in (sh.ident, sh.identb):
                pool.affine_select(out=m[:, :], in_=m[:, :], compare_op=ALU.not_equal, fill=1.0, base=0,
                                   pattern=[[-1, P]], channel_multiplier=1).then_inc(identities, 1)

        @block.scalar
        def _(act):
            act.wait_ge(constants, 2)
            n = 0
            for w in range(3):
                act.wait_ge(raw_loaded[w], 16 * len(parts[w]))
                for k, (rows, at, cols) in enumerate(parts[w]):
                    if n:
                        act.wait_ge(abs_summed, n)
                    act.activation(low[0:rows, at:at + cols], raw[w][0:rows, at:at + cols], ACT.Abs,
                                   accum_out=sums[0:rows, w, k:k + 1]).then_inc(abs_summed, 1)
                    n += 1
            act.wait_ge(small_loaded, 16 * 7)
            act.activation(sh.tanh_g[:, :], gates_in[:, :], ACT.Tanh).then_inc(gates, 1)
            for g in range(0, len(groups), 2):
                w, at, rows, cols, dst = groups[g]
                act.wait_ge(transposed, g + 1)
                act.activation(dst, pT[g % 4][0:cols, :, 0:rows], ACT.Copy).then_inc(copied_act, 1)

        @block.tensor
        def _(pe):
            pe.wait_ge(constants, 2)
            pe.wait_ge(abs_summed, 5)
            pe.matmul(pS[:, :], sh.ones[:, :], sums[:, :, :].rearrange("p w n -> p (w n)"), start=True, stop=True).then_inc(totals, 1)
            pe.wait_ge(identities, 2)
            for g, (w, at, rows, cols, dst) in enumerate(groups):
                pe.wait_ge(ternary, w + 1)
                if g >= 4:
                    pe.wait_ge(copied_act if g % 2 == 0 else copied_dve, (g - 4) // 2 + 1)
                for k in range(KD):
                    mm = pe.transpose(pT[g % 4][0:cols, k, 0:rows], tern[w][0:rows, at[k]:at[k] + cols], sh.identb[0:rows, 0:rows])
                mm.then_inc(transposed, 1)

        @block.vector
        def _(dve):
            st = Steps(dve, step, 0, 0)
            dve.wait_ge(totals, 1)
            st.done(dve.tensor_reduce(tot[:, :], pS[:, :].rearrange("p (w n) -> p w n", n=2), AX.X, ALU.add))
            st.done(dve.tensor_scalar(sh.wmean[:, :], tot[:, :], 1.0 / (FF * D), None, ALU.mult))
            st.mark(dve.tensor_scalar(thr[:, :, 0], sh.wmean[:, :], EPS, 0.5, ALU.add, ALU.mult))
            st.done(dve.tensor_scalar(thr[:, :, 1], sh.wmean[:, :], EPS, -0.5, ALU.add, ALU.mult))
            for w in range(3):
                for rows, at, cols in parts[w]:
                    here = slice(at, at + cols)
                    st.done(dve.tensor_scalar(low[0:rows, here], raw[w][0:rows, here], thr[0:rows, w, 1:2], None, ALU.is_lt))
                    st.done(dve.scalar_tensor_tensor(tern[w][0:rows, here], raw[w][0:rows, here], thr[0:rows, w, 0:1],
                                                     low[0:rows, here], ALU.is_gt, ALU.subtract))
                dve.sem_inc(ternary, 1)
            dve.wait_ge(gates, 1)
            st.done(dve.tensor_tensor(sh.wscale[:, :], sh.wmean[:, :], sh.scales[:, :], ALU.mult))
            st.done(dve.tensor_tensor(down[:, :], sh.wscale[:, 2:3], sh.tanh_g[:, 1:2], ALU.mult))
            st.done(dve.tensor_scalar(sh.wscale[:, 2:3], down[:, :], 1.0 / 127.0, None, ALU.mult))
            for g in range(1, len(groups), 2):
                w, at, rows, cols, dst = groups[g]
                dve.wait_ge(transposed, g + 1)
                dve.tensor_copy(dst, pT[g % 4][0:cols, :, 0:rows]).then_inc(copied_dve, 1)


NH0, HD0, WIN = 8, 8, 16
LEFT = WIN // 2
Q4, R4 = 4, 4
TB = 32
NT = D // TB
NJ = NT + 1
W0 = TB + WIN
KPAD = NJ * TB
QPAD = D + W0
NGR = (NJ + 1) // 2
NEG = -1e30


def first_attention(nc, io, sh):
    with ExitStack() as c:
        sb = lambda n, s, dt=F32: c.enter_context(nc.sbuf_tensor("a0_" + n, s, dt))
        pb = lambda n, s, dt=F32: c.enter_context(nc.psum_tensor("a0_" + n, s, dt))
        sem = lambda n: c.enter_context(nc.semaphore("a0_" + n))
        names = ("Wq", "Wk", "Wv", "Wo")
        wnat, wsort, wT = sb("wnat", [P, 4, P]), sb("wsort", [P, P]), sb("wT", [P, 4, P])
        bias = sb("bias", [P, 4])
        gbo = sb("gbo", [P, 1])
        mask_s, mask_k = sb("mask_s", [P, 2 * R4, W0], BF16), sb("mask_k", [P, 2 * R4, W0], BF16)
        rmask, diag, quad, quadR = sb("rmask", [P, R4]), sb("diag", [P, TB]), sb("quad", [P, P]), sb("quadR", [P, P], F32R)
        ctx, xn = sb("ctx", [P, 2, D]), sb("xn", [P, 2, D])
        q, k, v = sb("q", [P, D]), sb("k", [P, KPAD]), sb("v", [P, KPAD])
        QD = sb("QD", [P, NT, Q4, TB], F32R)
        KM = sb("KM", [P, R4, KPAD], F32R)
        KD = sb("KD", [P, 2, NJ, Q4, TB])
        QM = sb("QM", [P, 2, R4, QPAD])
        nmax = sb("nmax", [P, NT, R4])
        DM = sb("DM", [P, 2, R4, QPAD], F32R)
        vT = sb("vT", [P, NJ, R4, HD0])
        VM = sb("VM", [P, NJ, R4, P])
        E = sb("E", [P, 2, 2, R4, W0])
        den, rec, yraw, yn = sb("den", [P, D]), sb("rec", [P, D]), sb("yraw", [P, D]), sb("yn", [P, D])
        o = sb("o", [P, D])
        pA, pB = pb("pA", [P, D]), pb("pB", [P, D])
        pM = [pb(f"pM{n}", [P, 2, R4, W0]) for n in range(2)]
        pE = [pb(f"pE{n}", [P, 2, R4, W0]) for n in range(2)]
        pY = [pb(f"pY{n}", [P, D]) for n in range(2)]
        loaded, const_step, cleared, quad_ready, w_sorted, w_turned, w_ready = (
            sem(n) for n in ("loaded", "const_step", "cleared", "quad_ready", "w_sorted", "w_turned", "w_ready"))
        ctx_loaded = [sem(f"ctx_loaded{n}") for n in range(2)]
        xn_ready, q_done, k_done, v_done, q_copied, k_copied, v_copied = (
            sem(n) for n in ("xn_ready", "q_done", "k_done", "v_done", "q_copied", "k_copied", "v_copied"))
        QD_ready, KM_ready, QM_ready, KD_ready, vT_ready = (sem(n) for n in ("QD_ready", "KM_ready", "QM_ready", "KD_ready", "vT_ready"))
        scored, maxed, DM_ready = sem("scored"), sem("maxed"), sem("DM_ready")
        keyed, exped, weighed, spread = sem("keyed"), sem("exped"), sem("weighed"), sem("spread")
        y_copied, inverted, normed, out_done, out_copied, added = (
            sem(n) for n in ("y_copied", "inverted", "normed", "out_done", "out_copied", "added"))
        block = c.enter_context(nc.Block())
        N_LOADS = 16 * (2 * 4 + 2 * 4)

        @block.sync
        def _(sp):
            sp.wait_ge(cleared, 1)
            for w, name in enumerate(names):
                for b in range(BPT):
                    sp.dma_start(wnat[S * b:S * b + S, w, S * b:S * b + S], io["L0_xattn_" + name]).then_inc(loaded, 16)
                    sp.dma_start(bias[S * b:S * b + S, w:w + 1], io["L0_xattn_b" + name[1]].rearrange("(p a) -> p a", a=1)).then_inc(loaded, 16)
            c_in = io["ctx_4096"].rearrange("(i b) s d -> (b s) i d", b=BPT)

            def body(it, b, live, past):
                if live(1):
                    if past(1, 2):
                        sp.wait_ge(v_done, it)
                    sp.dma_start(ctx[:, 1 - b, :], c_in[:, bass.ds(it + 1, 1), :].rearrange("p a d -> p (a d)")).then_inc(ctx_loaded[1 - b], 32)
            over_tiles(sp, body, 1, 0)

        N_CONST = 5 + 2 + 8 + 8 + 4

        @block.gpsimd
        def _(pool):
            st = Steps(pool, const_step, 0, 0)
            st.done(pool.memset(VM[:, :, :, :].rearrange("p j r n -> p (j r n)"), 0.0))
            st.done(pool.memset(mask_s[:, :, :], 0.0))
            st.done(pool.memset(mask_k[:, :, :], 0.0))
            st.done(pool.memset(rmask[:, :], 1.0))
            st.done(pool.memset(diag[:, :], 1.0))

            def keep(part, base, pattern, by, fill, op=ALU.is_ge):
                st.done(pool.affine_select(out=part, in_=part, compare_op=op, fill=fill, base=base, pattern=pattern, channel_multiplier=by))

            for n in range(Q4):
                rows = slice(TB * n, TB * n + TB)
                keep(mask_s[rows, :, :], 0, [[0, 2 * R4], [1, W0]], -1, NEG)
                keep(mask_s[rows, :, :], WIN - 1, [[0, 2 * R4], [-1, W0]], 1, NEG)
                keep(mask_k[rows, :, :], -1, [[0, 2 * R4], [1, W0]], -1, NEG)
                keep(mask_k[rows, :, :], WIN, [[0, 2 * R4], [-1, W0]], 1, NEG)
                keep(rmask[rows, :], 0, [[-HD0, R4]], 1, 0.0)
                keep(rmask[rows, :], HD0 - 1, [[HD0, R4]], -1, 0.0)
                keep(diag[rows, :], 0, [[-1, TB]], 1, 0.0, ALU.is_equal)
            sh.n = st.n

            def body(it, b, live, past):
                def values(j0, j1):
                    for n in range(Q4):
                        rows = slice(TB * n, TB * n + TB)
                        dst = VM[rows, j0:j1, :, :]
                        dst = bass.AP(dst.tensor, dst.offset + n * HD0, [dst.ap[0], [R4 * P, j1 - j0], [P + Q4 * HD0, R4], [1, HD0]])
                        one = sh.ones[rows, 0:HD0].rearrange("p (a b d) -> p a b d", a=1, b=1).broadcast_to([TB, j1 - j0, R4, HD0])
                        pool.tensor_tensor(dst, vT[rows, j0:j1, :, :], one, ALU.mult).then_inc(spread, 1)
                if live(0):
                    pool.wait_ge(vT_ready, it + 1)
                    if past(0, 1):
                        pool.wait_ge(spread, 8 * it)
                    if past(0, 1):
                        pool.wait_ge(weighed, NGR * (it - 1) + 4)
                    values(0, 8)
                if live(-2):
                    t = it - 2
                    pool.wait_ge(out_copied, t + 1)
                    pool.wait_ge(spread, 8 * it + 4 if live(0) else 8 * N)
                    xt = sh.x[:, t, :]
                    pool.tensor_tensor(xt, xt, o[:, :], ALU.add).then_inc(added, 1)
                if live(0):
                    if live(-2):
                        pool.wait_ge(added, it - 1)
                    if past(0, 1):
                        pool.wait_ge(weighed, NGR * it)
                    values(8, NJ)
            over_tiles(pool, body, 0, 2)
        n_const = sh.n

        @block.tensor
        def _(pe):
            pe.wait_ge(w_sorted, 1)
            for w in range(4):
                mm = pe.transpose(pA[:, w * P:(w + 1) * P], wsort[:, :] if w == 3 else wnat[:, w, :], sh.ident[:, :])
            mm.then_inc(w_turned, 1)
            pe.wait_ge(w_ready, 1)
            pe.wait_ge(quad_ready, 1)
            pe.wait_ge(const_step, n_const)

            def scores(t, a, g):
                n = NGR * t + g
                if g >= 2 or not (isinstance(t, int) and t == 0):
                    pe.wait_ge(exped, n - 1)
                blocks = 2 if g < NGR - 1 else 1
                cols = W0 if g < NGR - 1 else WIN
                for i in range(blocks):
                    j = 2 * g + i
                    pe.matmul(pE[g % 2][:, i, :, 0:cols], KD[:, a, j, :, :].rearrange("p n j -> p (n j)"),
                              QM[:, a, :, TB * j:TB * j + cols], start=(i == 0), stop=False, skip_group_check=True)
                    pe.matmul(pE[g % 2][:, i, :, 0:cols], quadR[:, :], DM[:, a, :, TB * j:TB * j + cols],
                              start=False, stop=False, skip_group_check=True)
                mask = mask_k[:, 0:blocks * R4, 0:cols].rearrange("p (i r) c -> p i r c", i=blocks)
                pe.matmul(pE[g % 2][:, 0:blocks, :, 0:cols], sh.identb[:, :], mask, start=False, stop=True,
                          skip_group_check=True).then_inc(keyed, 1)

            def weigh(t, g):
                n = NGR * t + g
                pe.wait_ge(exped, n + 1)
                if g == 0:
                    pe.wait_ge(spread, 8 * t + 4)
                    if not (isinstance(t, int) and t == 0):
                        pe.wait_ge(y_copied, t)
                if g == 4:
                    pe.wait_ge(spread, 8 * t + 8)
                for i in range(2 if g < NGR - 1 else 1):
                    j = 2 * g + i
                    lo, hi = max(0, TB * j - WIN), min(D, TB * j + TB)
                    at = lo - (TB * j - WIN)
                    for r in range(R4):
                        mm = pe.matmul(pY[r // 2][:, lo:hi], VM[:, j, r, :], E[:, g % 2, i, r, at:at + hi - lo],
                                       start=(j == 0 and r % 2 == 0), stop=(j == NJ - 1 and r % 2 == 1), skip_group_check=True)
                mm.then_inc(weighed, 1)

            def row_scores(it, m):
                n = NT // 2 * it + m
                if m >= 2 or not (isinstance(it, int) and it == 0):
                    pe.wait_ge(maxed, n - 1)
                for i in range(2):
                    t = 2 * m + i
                    pe.matmul(pM[m % 2][:, i, :, :], QD[:, t, :, :].rearrange("p n t -> p (n t)"),
                              KM[:, :, TB * t:TB * t + W0], start=(i == 0), stop=False, skip_group_check=True)
                pe.matmul(pM[m % 2][:, :, :, :].rearrange("p i r c -> p (i r c)"), sh.identb[:, :],
                          mask_s[:, :, :].rearrange("p a c -> p (a c)"), start=False, stop=True,
                          skip_group_check=True).then_inc(scored, 1)

            def body(it, a, live, past):
                s = 1 - a
                if live(0):
                    pe.wait_ge(xn_ready, it + 1)
                    if past(0, 1):
                        pe.wait_ge(v_copied, it)
                    pe.matmul(pA[:, :], wT[:, 0, :], xn[:, a, :], start=True, stop=True).then_inc(q_done, 1)
                    pe.wait_ge(ctx_loaded[a], 16 * (it - a) + 32)
                    if past(0, 3):
                        pe.wait_ge(out_copied, it - 2)
                    pe.matmul(pB[:, :], wT[:, 1, :], ctx[:, a, :], start=True, stop=True).then_inc(k_done, 1)
                if live(-1):
                    pe.wait_ge(DM_ready, it)
                    scores(it - 1, s, 0)
                    scores(it - 1, s, 1)
                    weigh(it - 1, 0)
                if live(0):
                    pe.wait_ge(q_copied, it + 1)
                    pe.matmul(pA[:, :], wT[:, 2, :], ctx[:, a, :], start=True, stop=True).then_inc(v_done, 1)
                for g in range(2, NGR + 1):
                    if live(-1):
                        if g < NGR:
                            scores(it - 1, s, g)
                        weigh(it - 1, g - 1)
                    if g == 4 and live(-2):
                        pe.wait_ge(normed, it - 1)
                        if live(0):
                            pe.wait_ge(k_copied, it + 1)
                        pe.matmul(pB[:, :], wT[:, 3, :], yn[:, :], start=True, stop=True).then_inc(out_done, 1)
                    if 3 <= g < 7 and live(0):
                        if g == 3:
                            pe.wait_ge(QD_ready, it + 1)
                            pe.wait_ge(KM_ready, it + 1)
                        row_scores(it, 2 * (g - 3))
                        row_scores(it, 2 * (g - 3) + 1)
            over_tiles(pe, body, 0, 2)

        @block.scalar
        def _(act):
            act.wait_ge(w_turned, 1)
            act.activation(wT[:, :, :].rearrange("p w n -> p (w n)"), pA[:, :], ACT.Copy).then_inc(w_ready, 1)
            act.wait_ge(quad_ready, 1)

            def exp(t, g):
                n = NGR * t + g
                act.wait_ge(keyed, n + 1)
                if g >= 2 or not (isinstance(t, int) and t == 0):
                    act.wait_ge(weighed, n - 1)
                blocks = 2 if g < NGR - 1 else 1
                cols = W0 if g < NGR - 1 else WIN
                act.activation(E[:, g % 2, 0:blocks, :, 0:cols], pE[g % 2][:, 0:blocks, :, 0:cols], ACT.Exp,
                               scale=HD0 ** -0.5).then_inc(exped, 1)

            def body(it, a, live, past):
                if live(0):
                    act.wait_ge(q_done, it + 1)
                    if past(0, 1):
                        act.wait_ge(QM_ready, it)
                    act.activation(q[:, :], pA[:, :], ACT.Identity, bias=bias[:, 0:1]).then_inc(q_copied, 1)
                    act.wait_ge(k_done, it + 1)
                    if past(0, 1):
                        act.wait_ge(KD_ready, it)
                    act.activation(k[:, LEFT:LEFT + D], pB[:, :], ACT.Identity, bias=bias[:, 1:2]).then_inc(k_copied, 1)
                if live(-1):
                    exp(it - 1, 0)
                if live(0):
                    if past(0, 1):
                        act.wait_ge(scored, NT // 2 * it)
                    act.wait_ge(q_copied, it + 1)
                    for n in range(Q4):
                        rows = slice(TB * n, TB * n + TB)
                        i = act.activation(QD[rows, :, n, :], q[rows, :].rearrange("p (t c) -> p t c", t=NT), ACT.Copy)
                    i.then_inc(QD_ready, 1)
                if live(-1):
                    exp(it - 1, 1)
                if live(0):
                    act.wait_ge(v_done, it + 1)
                    if past(0, 1):
                        act.wait_ge(vT_ready, it)
                    act.activation(v[:, LEFT:LEFT + D], pA[:, :], ACT.Identity, bias=bias[:, 2:3]).then_inc(v_copied, 1)
                for g in range(2, NGR):
                    if live(-1):
                        exp(it - 1, g)
                    if g == 5 and live(-2):
                        t = it - 2
                        act.wait_ge(out_done, t + 1)
                        if past(-2, 1):
                            act.wait_ge(added, t)
                        act.activation(o[:, :], pB[:, :], ACT.Identity, scale=sh.tanh_g[:, 0:1], bias=gbo[:, :]).then_inc(out_copied, 1)
                if live(-1):
                    act.wait_ge(weighed, NGR * it)
                    if past(-1, 1):
                        act.wait_ge(normed, it - 1)
                    for h in range(2):
                        mine, other = slice(64 * h, 64 * h + 64), slice(64 - 64 * h, 128 - 64 * h)
                        act.activation(den[mine, :], pY[h][other, :], ACT.Copy)
                        i = act.activation(yraw[mine, :], pY[h][mine, :], ACT.Copy)
                    i.then_inc(y_copied, 1)
            over_tiles(act, body, 0, 2)

        @block.vector
        def _(dve):
            st = Steps(dve, cleared, 0, 0)
            st.done(dve.memset(wnat[:, :, :], 0.0))
            dve.memset(wsort[:, :], 0.0)
            for tile in (k[:, :], v[:, :], QD[:, :, :, :].bitcast(F32), KD[:, :, :, :, :], QM[:, :, :, :], DM[:, :, :, :, ].bitcast(F32)):
                dve.memset(tile, 0.0)
            st.done(dve.memset(quad[:, :], 0.0))
            for n in range(Q4):
                dve.memset(quad[TB * n:TB * n + TB, TB * n:TB * n + TB], 1.0)
            dve.wait_ge(const_step, 1)
            for r in range(R4):
                for n in range(Q4):
                    at = (32 * r + 64) % P + HD0 * n
                    i = dve.memset(VM[TB * n:TB * n + TB, :, r, at:at + HD0], 1.0)
            st.done(i)
            dve.wait_ge(loaded, N_LOADS)
            for b in range(BPT):
                rows = slice(S * b, S * b + S)
                for n in range(2):
                    src = wnat[rows, 3, S * b + TB * n:S * b + TB * n + TB].rearrange("p (r d) -> p r d", r=R4)
                    dst = wsort[rows, :].rearrange("p (r n d) -> p r n d", r=R4, n=Q4)[:, :, 2 * b + n, :]
                    dve.tensor_copy(dst, src)
            dve.tensor_tensor(gbo[:, :], bias[:, 3:4], sh.tanh_g[:, 0:1], ALU.mult).then_inc(w_sorted, 1)
            dve.tensor_copy(quadR[:, :], quad[:, :]).then_inc(quad_ready, 1)
            dve.wait_ge(const_step, n_const)

            def normalize(t, u):
                if not (isinstance(t, int) and t < 2):
                    dve.wait_ge(q_done, t - 1)
                dve.tensor_scalar(xn[:, u, :], sh.x[:, t, :], sh.rstd[:, bass.ds(t, 1)], sh.nmr[:, bass.ds(t, 1)],
                                  ALU.mult, ALU.add).then_inc(xn_ready, 1)

            def body(it, a, live, past):
                if live(1):
                    normalize(it + 1, 1 - a)
                if live(0):
                    dve.wait_ge(k_copied, it + 1)
                    if past(0, 1):
                        dve.wait_ge(scored, NT // 2 * it)
                    for r in range(R4):
                        i = dve.tensor_scalar(KM[:, r, :], k[:, :], rmask[:, r:r + 1], None, ALU.mult)
                    i.then_inc(KM_ready, 1)
                if live(-2):
                    t = it - 2
                    dve.wait_ge(y_copied, t + 1)
                    dve.reciprocal(rec[:, :], den[:, :]).then_inc(inverted, 1)
                    dve.wait_ge(inverted, t + 1)
                    if past(-2, 1):
                        dve.wait_ge(out_done, t)
                    dve.tensor_tensor(yn[:, :], yraw[:, :], rec[:, :], ALU.mult).then_inc(normed, 1)
                if live(0):
                    for n in range(Q4):
                        rows = slice(TB * n, TB * n + TB)
                        i = dve.tensor_copy(KD[rows, a, :, n, :], k[rows, :].rearrange("p (j c) -> p j c", j=NJ))
                    i.then_inc(KD_ready, 1)
                    dve.wait_ge(q_copied, it + 1)
                    for r in range(R4):
                        i = dve.tensor_scalar(QM[:, a, r, WIN:WIN + D], q[:, :], rmask[:, r:r + 1], None, ALU.mult)
                    i.then_inc(QM_ready, 1)
                    dve.wait_ge(v_copied, it + 1)
                    if past(0, 1):
                        dve.wait_ge(spread, 8 * it)
                    dve.transpose(vT[:, :, :, :].rearrange("p j r d -> p (j r d)"), v[:, :]).then_inc(vT_ready, 1)
                    for m in range(NT // 2):
                        dve.wait_ge(scored, NT // 2 * it + m + 1)
                        dve.tensor_reduce(nmax[:, 2 * m:2 * m + 2, :].rearrange("p i r -> p (i r)"),
                                          pM[m % 2][:, :, :, :].rearrange("p i r c -> p (i r) c"), AX.X, ALU.max, negate=True).then_inc(maxed, 1)
                    dve.wait_ge(maxed, NT // 2 * (it + 1))
                    shape = [P, R4, NT, TB]
                    dve.tensor_tensor(DM[:, a, :, WIN:WIN + D].rearrange("p r (t c) -> p r t c", t=NT),
                                      nmax[:, :, :].rearrange("p (t a) r -> p r t a", a=1).broadcast_to(shape),
                                      diag[:, :].rearrange("p (a b c) -> p a b c", a=1, b=1).broadcast_to(shape),
                                      ALU.mult).then_inc(DM_ready, 1)
            normalize(0, 0)
            over_tiles(dve, body, 0, 2)


def first_ffn(nc, io, sh):
    with ExitStack() as c:
        sb = lambda n, s, dt=F32: c.enter_context(nc.sbuf_tensor("f0_" + n, s, dt))
        pb = lambda n, s, dt=F32: c.enter_context(nc.psum_tensor("f0_" + n, s, dt))
        sem = lambda n: c.enter_context(nc.semaphore("f0_" + n))
        qa, qb, iscale, isize = (sb(n, [P, N]) for n in ("qa", "qb", "iscale", "isize"))
        sign = sb("sign", [P, 1])
        cmax, den, inv, hf = (sb(n, [P, 2]) for n in ("cmax", "den", "inv", "hf"))
        oscale = sb("oscale", [P, 2])
        xs, xc = sb("xs", [P, 2, D]), sb("xc", [P, 2, D])
        xq, xqT = sb("xq", [P, 2, D], BF16), sb("xqT", [P, 2, KD, P], BF16)
        r, r2 = sb("r", [P, 2, FC]), sb("r2", [P, 2, FC])
        inter, amax = sb("inter", [P, 2, FF]), sb("amax", [P, 2, NCH])
        hr, hq, hqT = sb("hr", [P, 2, FF]), sb("hq", [P, 2, FF], BF16), sb("hqT", [P, 2, FJ, P], BF16)
        int4_scales(nc, sh, qa, qb, iscale, isize, sign)

        pG, pU = [pb(f"pG{k}", [P, FC]) for k in range(2)], [pb(f"pU{k}", [P, FC]) for k in range(2)]
        pXT = pb("pXT", [P, KD, P], BF16)
        pHT, pHU = pb("pHT", [P, 8, P], BF16), pb("pHU", [P, FJ - 8, P], BF16)
        pD = pb("pD", [P, D])
        x_step, xT_done, xT_copied = sem("x_step"), sem("xT_done"), sem("xT_copied")
        chunk_done, relu_done, squared, multiplied, max_done = (
            sem(n) for n in ("chunk_done", "relu_done", "squared", "multiplied", "max_done"))
        factor_step, scaled, rounded = sem("factor_step"), sem("scaled"), sem("rounded")
        hT_done, hT_copied, hU_copied, down_done, added = (
            sem(n) for n in ("hT_done", "hT_copied", "hU_copied", "down_done", "added"))
        block = c.enter_context(nc.Block())
        FACTOR = 5

        @block.tensor
        def _(pe):
            def transpose_x(t, u):
                pe.wait_ge(x_step, 3 * t + 3)
                if not (isinstance(t, int) and t == 0):
                    pe.wait_ge(xT_copied, t)
                for k in range(KD):
                    mm = pe.transpose(pXT[:, k, :], xq[:, u, k * P:(k + 1) * P], sh.identb[:, :])
                mm.then_inc(xT_done, 1)

            def body(it, b, live, past):
                o = 1 - b
                if live(0):
                    pe.wait_ge(xT_copied, it + 1)
                for ch in range(NCH):
                    if live(0):
                        u = ch % 2
                        if ch >= 2 or past(0, 1):
                            pe.wait_ge(multiplied, NCH * it + ch - 1)
                        for p, w in ((pG[u], sh.gateT), (pU[u], sh.upT)):
                            for k in range(KD):
                                mm = pe.matmul(p[:, :], xqT[:, b, k, :], w[:, k, ch * FC:(ch + 1) * FC], start=(k == 0), stop=(k == KD - 1))
                        mm.then_inc(chunk_done, 1)
                    if ch == 1 and live(1):
                        transpose_x(it + 1, o)
                    if ch == 2 and live(-1):
                        pe.wait_ge(rounded, it)
                        if past(-1, 1):
                            pe.wait_ge(hT_copied, it - 1)
                            pe.wait_ge(hU_copied, it - 1)
                        for j in range(FJ):
                            n = P if j < FJ - 1 else FR
                            dst = pHT[0:n, j, :] if j < 8 else pHU[0:n, j - 8, :]
                            mm = pe.transpose(dst, hq[:, o, j * P:j * P + n], sh.identb[:, :])
                        mm.then_inc(hT_done, 1)
                if live(-1):
                    pe.wait_ge(hT_copied, it)
                    pe.wait_ge(hU_copied, it)
                    if past(-1, 1):
                        pe.wait_ge(added, it - 1)
                    for j in range(FJ):
                        n = P if j < FJ - 1 else FR
                        mm = pe.matmul(pD[:, :], hqT[0:n, o, j, :], sh.downT[0:n, j, :], start=(j == 0), stop=(j == FJ - 1))
                    mm.then_inc(down_done, 1)
            transpose_x(0, 0)
            over_tiles(pe, body, 0, 1)

        @block.scalar
        def _(act):
            def body(it, b, live, past):
                o = 1 - b
                for ch in range(NCH):
                    if live(0):
                        u, n = ch % 2, NCH * it + ch
                        act.wait_ge(chunk_done, n + 1)
                        act.activation(r[:, u, :], pG[u][:, :], ACT.Relu, scale=sign[:, :]).then_inc(relu_done, 1)
                        if ch >= 2 or past(0, 1):
                            act.wait_ge(multiplied, n - 1)
                        act.wait_ge(relu_done, n + 1)
                        act.activation(r2[:, u, :], r[:, u, :], ACT.Square).then_inc(squared, 1)
                    if ch == 0 and live(-1):
                        act.wait_ge(factor_step, FACTOR * it)
                        if past(-1, 2):
                            act.wait_ge(rounded, it - 2)
                        act.activation(hr[:, o, :], inter[:, o, :], ACT.Identity, bias=sh.round[:, :], scale=hf[:, o:o + 1]).then_inc(scaled, 1)
                    if ch == 2 and live(-1):
                        act.wait_ge(hT_done, it)
                        act.activation(hqT[:, o, 0:8, :], pHT[:, :, :], ACT.Copy).then_inc(hT_copied, 1)
            over_tiles(act, body, 0, 1)

        @block.vector
        def _(dve):
            def scale_x(t, u):
                dve.tensor_scalar(xs[:, u, :], sh.x[:, t, :], qa[:, bass.ds(t, 1)], qb[:, bass.ds(t, 1)], ALU.mult, ALU.add).then_inc(x_step, 1)

            def clip_x(t, u):
                dve.wait_ge(x_step, 3 * t + 1)
                dve.tensor_scalar(xc[:, u, :], xs[:, u, :], 7.0, -8.0, ALU.min, ALU.max).then_inc(x_step, 1)

            def round_x(t, u):
                dve.wait_ge(x_step, 3 * t + 2)
                if not (isinstance(t, int) and t < 2):
                    dve.wait_ge(xT_done, t - 1)
                dve.tensor_scalar(xq[:, u, :], xc[:, u, :], ROUND, ROUND, ALU.add, ALU.subtract).then_inc(x_step, 1)

            def copy_xT(t, u):
                dve.wait_ge(xT_done, t + 1)
                if not (isinstance(t, int) and t < 2):
                    dve.wait_ge(chunk_done, NCH * (t - 1))
                dve.tensor_copy(xqT[:, u, :, :], pXT[:, :, :]).then_inc(xT_copied, 1)

            def body(it, b, live, past):
                o = 1 - b
                for ch in range(NCH):
                    if ch == 0 and live(-1):
                        dve.wait_ge(max_done, NCH * it)
                        if past(-1, 2):
                            dve.wait_ge(scaled, it - 2)
                            dve.wait_ge(added, it - 2)
                        st = Steps(dve, factor_step, it - 1, FACTOR)
                        size, scale = isize[:, bass.ds(it - 1, 1)], iscale[:, bass.ds(it - 1, 1)]
                        col = slice(o, o + 1)
                        st.done(dve.tensor_reduce(cmax[:, col], amax[:, o, :], AX.X, ALU.max))
                        st.mark(dve.tensor_scalar(oscale[:, col], cmax[:, col], size, sh.wscale[:, 2:3], ALU.mult, ALU.mult))
                        st.done(dve.tensor_scalar(den[:, col], cmax[:, col], size, EPS, ALU.mult, ALU.add))
                        st.done(dve.reciprocal(inv[:, col], den[:, col]))
                        st.mark(dve.tensor_scalar(hf[:, col], inv[:, col], scale, 127.0, ALU.mult, ALU.mult))
                    if live(0):
                        u, n = ch % 2, NCH * it + ch
                        dve.wait_ge(squared, n + 1)
                        if ch == 0 and past(0, 2):
                            dve.wait_ge(scaled, it - 1)
                        here = inter[:, b, ch * FC:(ch + 1) * FC]
                        dve.tensor_tensor(here, pU[u][:, :], r2[:, u, :], ALU.mult).then_inc(multiplied, 1)
                    if ch == 0 and live(2):
                        scale_x(it + 2, b)
                    if live(0):
                        dve.wait_ge(multiplied, n + 1)
                        dve.tensor_reduce(amax[:, b, ch:ch + 1], here, AX.X, ALU.max, apply_absolute_value=True).then_inc(max_done, 1)
                    if ch == 0 and live(-2):
                        dve.wait_ge(down_done, it - 1)
                        xt = sh.x[:, it - 2, :]
                        dve.scalar_tensor_tensor(xt, pD[:, :], oscale[:, b:b + 1], xt, ALU.mult, ALU.add).then_inc(added, 1)
                    if ch == 1:
                        if live(-1):
                            dve.wait_ge(scaled, it)
                            if past(-1, 2):
                                dve.wait_ge(hT_done, it - 2)
                            dve.tensor_scalar(hq[:, o, :], hr[:, o, :], ROUND, None, ALU.subtract).then_inc(rounded, 1)
                        if live(2):
                            clip_x(it + 2, b)
                        if live(1):
                            copy_xT(it + 1, o)
                    if ch == 2:
                        if live(2):
                            round_x(it + 2, b)
                        if live(-1):
                            dve.wait_ge(hT_done, it)
                            dve.tensor_copy(hqT[:, o, 8:FJ - 1, :], pHU[:, 0:FJ - 9, :])
                            dve.tensor_copy(hqT[0:FR, o, FJ - 1, :], pHU[0:FR, FJ - 9, :]).then_inc(hU_copied, 1)
            for t in range(2):
                scale_x(t, t)
                clip_x(t, t)
                round_x(t, t)
            copy_xT(0, 0)
            over_tiles(dve, body, 0, 2, reach=2)


def int4_scales(nc, sh, qa, qb, iscale, isize, sign):
    with ExitStack() as c:
        sb = lambda n, s, dt=F32: c.enter_context(nc.sbuf_tensor("q0_" + n, s, dt))
        sem = lambda n: c.enter_context(nc.semaphore("q0_" + n))
        stats, mv, nmean, asum = sb("stats", [P, N, 6]), sb("mv", [P, N, 2]), sb("nmean", [P, N]), sb("asum", [P, N])
        std, rstd, t1, t2, beta = (sb(n, [P, N]) for n in ("std", "rstd", "t1", "t2", "beta"))
        trash = sb("trash", [P, 2, D], BF16)
        stat_ready, var_ready, nmean_ready, std_ready, abs_ready, step = (
            sem(n) for n in ("stat_ready", "var_ready", "nmean_ready", "std_ready", "abs_ready", "step"))
        block = c.enter_context(nc.Block())

        @block.vector
        def _(dve):
            def aggregate(i):
                dve.wait_ge(stat_ready, i + 1)
                dve.bn_aggr(mv[:, i, :], stats[:, i, :]).then_inc(var_ready, 1)

            def negate(i):
                dve.wait_ge(var_ready, i + 1)
                dve.tensor_scalar(nmean[:, i:i + 1], mv[:, i, 0:1], -1.0, None, ALU.mult).then_inc(nmean_ready, 1)

            for i in range(N + 2):
                if i < N:
                    dve.bn_stats(stats[:, i, :], sh.x[:, i, :]).then_inc(stat_ready, 1)
                if 1 <= i < N + 1:
                    aggregate(i - 1)
                if i >= 2:
                    negate(i - 2)
            st = Steps(dve, step, 0, 0)
            st.mark(dve.tensor_scalar(sign[:, :], sh.scales[:, 0:1], 0.0, None, ALU.is_ge))
            dve.wait_ge(std_ready, 1)
            st.done(dve.reciprocal(t1[:, :], std[:, :]))
            st.done(dve.tensor_scalar(sign[:, :], sign[:, :], 2.0, 1.0, ALU.mult, ALU.subtract))
            st.done(dve.tensor_tensor(t2[:, :], t1[:, :], t1[:, :], ALU.mult))
            st.done(dve.scalar_tensor_tensor(std[:, :], mv[:, :, 1], EPS, t2[:, :], ALU.add, ALU.mult))
            st.done(dve.tensor_scalar(t2[:, :], std[:, :], -0.5, 1.5, ALU.mult, ALU.add))
            st.done(dve.tensor_tensor(rstd[:, :], t1[:, :], t2[:, :], ALU.mult))
            dve.wait_ge(abs_ready, N)
            st.done(dve.scalar_tensor_tensor(beta[:, :], asum[:, :], 1.0 / D, rstd[:, :], ALU.mult, ALU.mult))
            st.done(dve.tensor_scalar(t1[:, :], beta[:, :], EPS, 1.0 / SQRT7, ALU.add, ALU.mult))
            st.done(dve.reciprocal(t2[:, :], t1[:, :]))
            st.done(dve.tensor_tensor(qa[:, :], rstd[:, :], t2[:, :], ALU.mult))
            st.mark(dve.tensor_tensor(qb[:, :], nmean[:, :], qa[:, :], ALU.mult))
            st.done(dve.tensor_scalar(t1[:, :], beta[:, :], sh.wscale[:, 0:1], None, ALU.mult))
            st.mark(dve.tensor_scalar(t2[:, :], beta[:, :], sh.wscale[:, 1:2], None, ALU.mult))
            st.done(dve.tensor_tensor(std[:, :], t1[:, :], t1[:, :], ALU.mult))
            st.done(dve.tensor_tensor(iscale[:, :], std[:, :], t2[:, :], ALU.mult))
            st.done(dve.scalar_tensor_tensor(isize[:, :], iscale[:, :], -1.0, iscale[:, :], ALU.mult, ALU.max))

        @block.scalar
        def _(act):
            for i in range(N):
                act.wait_ge(nmean_ready, i + 1)
                if i >= 2:
                    act.wait_ge(abs_ready, i - 1)
                act.activation(trash[:, i % 2, :], sh.x[:, i, :], ACT.Abs, bias=nmean[:, i:i + 1],
                               accum_out=asum[:, i:i + 1]).then_inc(abs_ready, 1)
            act.activation(std[:, :], mv[:, :, 1], ACT.Sqrt, bias=sh.eps[:, :]).then_inc(std_ready, 1)


def layer_norms(nc, sh, tag):
    with ExitStack() as c:
        sb = lambda n, s, dt=F32: c.enter_context(nc.sbuf_tensor(tag + n, s, dt))
        sem = lambda n: c.enter_context(nc.semaphore(tag + n))
        stats, mv, std, t1, t2 = sb("stats", [P, N, 6]), sb("mv", [P, N, 2]), sb("std", [P, N]), sb("t1", [P, N]), sb("t2", [P, N])
        stat_ready, var_ready, std_ready, step = sem("stat_ready"), sem("var_ready"), sem("std_ready"), sem("norm_step")
        block = c.enter_context(nc.Block())

        @block.vector
        def _(dve):
            def stat(i):
                dve.bn_stats(stats[:, i, :], sh.x[:, i, :]).then_inc(stat_ready, 1)

            def aggregate(i):
                dve.wait_ge(stat_ready, i + 1)
                dve.bn_aggr(mv[:, i, :], stats[:, i, :]).then_inc(var_ready, 1)

            stat(0)
            for i in range(1, N):
                stat(i)
                aggregate(i - 1)
            aggregate(N - 1)
            st = Steps(dve, step, 0, 0)
            dve.wait_ge(std_ready, 1)
            st.done(dve.reciprocal(t1[:, :], std[:, :]))
            st.done(dve.tensor_tensor(t2[:, :], t1[:, :], t1[:, :], ALU.mult))
            st.done(dve.scalar_tensor_tensor(std[:, :], mv[:, :, 1], EPS, t2[:, :], ALU.add, ALU.mult))
            st.done(dve.tensor_scalar(t2[:, :], std[:, :], -0.5, 1.5, ALU.mult, ALU.add))
            st.done(dve.tensor_tensor(sh.rstd[:, :], t1[:, :], t2[:, :], ALU.mult))
            st.done(dve.scalar_tensor_tensor(sh.nmr[:, :], mv[:, :, 0], -1.0, sh.rstd[:, :], ALU.mult, ALU.mult))

        @block.scalar
        def _(act):
            act.wait_ge(var_ready, N)
            act.activation(std[:, :], mv[:, :, 1], ACT.Sqrt, bias=sh.eps[:, :]).then_inc(std_ready, 1)


NQ, NKV = 32, 8
HD = D // NQ
G = NQ // NKV
KP = NKV // 2


def second_attention(nc, io, sh):
    with ExitStack() as c:
        sb = lambda n, s, dt=F32: c.enter_context(nc.sbuf_tensor("a1_" + n, s, dt))
        pb = lambda n, s, dt=F32: c.enter_context(nc.psum_tensor("a1_" + n, s, dt))
        sem = lambda n: c.enter_context(nc.semaphore("a1_" + n))
        wq_in, wq = sb("wq_in", [P, KD, D]), sb("wq", [P, KD, G, P])
        wq_sorted = sem("wq_sorted")
        wk, wv = sb("wk", [P, KD, P]), sb("wv", [P, KD, P])
        wo = sb("wo", [P, G, D])
        bq, bk, bv, bo = sb("bq", [P, G]), sb("bk", [P, 1]), sb("bv", [P, P]), sb("bo", [P, D])
        gbo = sb("gbo", [P, D])
        ctx = sb("ctx", [P, 2, D])
        xn, xT, cT = sb("xn", [P, 2, D]), sb("xT", [P, KD, P]), sb("cT", [P, KD, P])
        QT = sb("QT", [P, 2, BPT, G, S])
        QR = sb("QR", [P, BPT, G, S], F32R)
        KT = sb("KT", [P, BPT, S])
        KB = sb("KB", [P, 2, BPT, KP, 2, S])
        KR = sb("KR", [P, BPT, KP, 2, S], F32R)
        half = sb("half", [P, BPT, 2, S])
        VB = sb("VB", [P, 2, BPT, KP, P])
        E = sb("E", [P, 2, 2, G * S])
        nmax = sb("nmax", [P, BPT, 2, NKV])
        nmaxT = sb("nmaxT", [P, P], F32R)
        sel = sb("sel", [P, BPT, 2, KP, P], F32R)
        self32 = sb("self32", [P, BPT, 2, KP, P])
        rec = sb("rec", [P, BPT, G, S])
        yT = sb("yT", [P, 2, G, BPT, S])
        pX, pC = pb("pX", [P, KD, P]), pb("pC", [P, KD, P])
        pM = [pb(f"pM{k}", [P, KP * 2, S]) for k in range(2)]
        pE = [pb(f"pE{k}", [P, 2, G * S]) for k in range(2)]
        pY = pb("pY", [P, BPT, 2, G, S])
        w_loaded, sel_set, consts, gbo_ready = sem("w_loaded"), sem("sel_set"), sem("consts"), sem("gbo_ready")
        ctx_loaded = [sem(f"ctx_loaded{k}") for k in range(2)]
        xn_ready, biased = sem("xn_ready"), sem("biased")
        turned, xT_copied, cT_copied = sem("turned"), sem("xT_copied"), sem("cT_copied")
        kv_done, q_done, k_copied, k_spread, k_rounded, v_spread, q_copied, q_rounded = (
            sem(n) for n in ("kv_done", "q_done", "k_copied", "k_spread", "k_rounded", "v_spread", "q_copied", "q_rounded"))
        scored, maxed, max_turned, max_copied = sem("scored"), sem("maxed"), sem("max_turned"), sem("max_copied")
        keyed, exped, weighed, inverted, normed = sem("keyed"), sem("exped"), sem("weighed"), sem("inverted"), sem("normed")
        out_done, added = sem("out_done"), sem("added")
        block = c.enter_context(nc.Block())
        NW = 9
        SETS = 9

        @block.sync
        def _(sp):
            c_in = io["ctx_4096"].rearrange("(i b) s d -> (b s) i d", b=BPT)
            sp.dma_start(wq_in[:, :, :], io["L1_xattn_Wq"].rearrange("(k p) n -> p k n", p=P)).then_inc(w_loaded, 16)
            sp.dma_start(wk[:, :, :], io["L1_xattn_Wk"].rearrange("(k p) n -> p k n", p=P)).then_inc(w_loaded, 16)
            sp.dma_start(wv[:, :, :], io["L1_xattn_Wv"].rearrange("(k p) n -> p k n", p=P)).then_inc(w_loaded, 16)
            wo_in = io["L1_xattn_Wo"].rearrange("(h g e) n -> h g e n", h=NKV, g=G)
            for h in range(NKV):
                sp.dma_start(wo[h * HD:(h + 1) * HD, :, :], wo_in[h].rearrange("g e n -> e g n")).then_inc(w_loaded, 16)
            bq_in = io["L1_xattn_bq"].rearrange("(h g e a) -> h g e a", h=NKV, g=G, a=1)
            for h in range(NKV):
                for g in range(G):
                    sp.dma_start(bq[h * HD:(h + 1) * HD, g:g + 1], bq_in[h, g]).then_inc(w_loaded, 16)
            sp.dma_start(bk[:, :], io["L1_xattn_bk"].rearrange("(p a) -> p a", a=1)).then_inc(w_loaded, 16)
            sp.dma_start(bv[:, :], io["L1_xattn_bv"].rearrange("(a n) -> a n", a=1).broadcast_to([P, P])).then_inc(w_loaded, 16)
            sp.dma_start(bo[:, :], io["L1_xattn_bo"].rearrange("(a n) -> a n", a=1).broadcast_to([P, D])).then_inc(w_loaded, 16)

            def body(it, b, live, past):
                if live(1):
                    if past(1, 2):
                        sp.wait_ge(turned, it)
                    sp.dma_start(ctx[:, 1 - b, :], c_in[:, bass.ds(it + 1, 1), :].rearrange("p a d -> p (a d)")).then_inc(ctx_loaded[1 - b], 32)
            over_tiles(sp, body, 1, 0)
        W_ALL = 16 * (3 + NKV + NKV * G + 3)

        @block.gpsimd
        def _(pool):
            pool.memset(KB[:, :, :, :, :, :].rearrange("p a b k e s -> p (a b k e s)"), 0.0).then_inc(consts, 1)
            pool.memset(VB[:, :, :, :, :].rearrange("p a b k n -> p (a b k n)"), 0.0).then_inc(consts, 1)
            pool.memset(half[:, :, :, :].rearrange("p b e s -> p (b e s)"), 1.0).then_inc(consts, 1)
            pool.memset(self32[:, :, :, :, :].rearrange("p b g k n -> p (b g k n)"), 1.0).then_inc(consts, 1)
            pool.wait_ge(consts, 4)
            n = 4
            for q in range(4):
                for e in range(2):
                    part = half[32 * q:32 * q + 32, :, e, :]
                    pool.affine_select(out=part, in_=part, compare_op=ALU.is_ge, fill=0.0,
                                       base=(HD - 1 if e == 0 else -HD), pattern=[[0, BPT], [0, S]],
                                       channel_multiplier=(-1 if e == 0 else 1)).then_inc(consts, 1)
                    n += 1
                    pool.wait_ge(consts, n)
            for b in range(BPT):
                for gp in range(2):
                    for kp in range(KP):
                        for e in range(2):
                            row = b * 16 + gp * 8 + kp * 2 + e
                            part = self32[:, b, gp, kp, e * S:(e + 1) * S]
                            pool.affine_select(out=part, in_=part, compare_op=ALU.is_equal, fill=0.0, base=-row,
                                               pattern=[[0, S]], channel_multiplier=1).then_inc(consts, 1)
                            n += 1
            sh.n_consts = n
            pool.wait_ge(consts, n)
            pool.wait_ge(gbo_ready, 1)

            def body(it, b, live, past):
                if live(0):
                    pool.wait_ge(xn_ready, it + 1)
                    xt = sh.x[:, it, :]
                    pool.tensor_tensor(xt, xt, gbo[:, :], ALU.add).then_inc(biased, 1)
            over_tiles(pool, body, 0, 0)
        n_consts = sh.n_consts

        @block.tensor
        def _(pe):
            pe.wait_ge(w_loaded, W_ALL)
            pe.wait_ge(sel_set, SETS)
            pe.wait_ge(wq_sorted, KD)

            def scores(t, a, b, kh):
                n = 4 * t + 2 * b + kh
                if not (isinstance(t, int) and t == 0 and b == 0):
                    pe.wait_ge(exped, n - 1)
                for j in range(2):
                    kp = 2 * kh + j
                    pe.matmul(pE[kh][:, j, :], KB[:, a, b, kp, :, :].rearrange("p e s -> p (e s)"),
                              QT[:, a, b, :, :].rearrange("p g s -> p (g s)"), start=True, stop=False,
                              skip_group_check=True)
                    for gp in range(2):
                        mm = pe.matmul(pE[kh][:, j, gp * 2 * S:(gp + 1) * 2 * S], sel[:, b, gp, kp, :], nmaxT[:, :],
                                       start=False, stop=(gp == 1), skip_group_check=True)
                mm.then_inc(keyed, 1)

            def weigh(t, a, b, kh):
                n = 4 * t + 2 * b + kh
                pe.wait_ge(exped, n + 1)
                if b == 0 and kh == 0 and not (isinstance(t, int) and t == 0):
                    pe.wait_ge(normed, t)
                for j in range(2):
                    mm = pe.matmul(pY[:, b, kh, :, :].rearrange("p g s -> p (g s)"), VB[:, a, b, 2 * kh + j, :],
                                   E[:, kh, j, :], start=(j == 0), stop=(j == 1))
                mm.then_inc(weighed, 1)

            def body(it, a, live, past):
                o = 1 - a
                if live(0):
                    pe.wait_ge(xn_ready, it + 1)
                    pe.wait_ge(ctx_loaded[a], 16 * (it - a) + 32)
                    if past(0, 1):
                        pe.wait_ge(q_copied, it)
                        pe.wait_ge(v_spread, it)
                        pe.wait_ge(k_copied, it)
                    for k in range(KD):
                        pe.transpose(pX[:, k, :], xn[:, a, k * P:(k + 1) * P], sh.ident[:, :])
                    for k in range(KD):
                        mm = pe.transpose(pC[:, k, :], ctx[:, a, k * P:(k + 1) * P], sh.ident[:, :])
                    mm.then_inc(turned, 1)
                if live(-2):
                    t = it - 2
                    pe.wait_ge(normed, t + 1)
                    if live(-1):
                        pe.wait_ge(maxed, 4 * it)
                    for g in range(G):
                        mm = pe.matmul(pM[1][:, :, :].rearrange("p a b -> p (a b)"), yT[:, a, g, :, :].rearrange("p b s -> p (b s)"),
                                       wo[:, g, :], start=(g == 0), stop=(g == G - 1))
                    mm.then_inc(out_done, 1)
                if live(-1):
                    t = it - 1
                    pe.wait_ge(maxed, 4 * it)
                    pe.transpose(pM[0][0:32, 0:2, :].rearrange("p a b -> p (a b)"), nmax[:, :, :, :].rearrange("p b g h -> p (b g h)"),
                                 sh.ident[:, :]).then_inc(max_turned, 1)
                    pe.wait_ge(max_copied, t + 1)
                    scores(t, o, 0, 0)
                    scores(t, o, 0, 1)
                if live(0):
                    pe.wait_ge(cT_copied, it + 1)
                    pC_kv = pC[:, 0:2, :]
                    for k in range(KD):
                        pe.matmul(pC[:, 0, :], wk[:, k, :], cT[:, k, :], start=(k == 0), stop=(k == KD - 1))
                    for k in range(KD):
                        mm = pe.matmul(pC[:, 1, :], cT[:, k, :], wv[:, k, :], start=(k == 0), stop=(k == KD - 1))
                    mm.then_inc(kv_done, 1)
                if live(-1):
                    weigh(it - 1, o, 0, 0)
                    scores(it - 1, o, 1, 0)
                    weigh(it - 1, o, 0, 1)
                if live(0):
                    pe.wait_ge(xT_copied, it + 1)
                    for g in range(G):
                        for k in range(KD):
                            mm = pe.matmul(pX[:, g, :], wq[:, k, g, :], xT[:, k, :], start=(k == 0), stop=(k == KD - 1))
                    mm.then_inc(q_done, 1)
                if live(-1):
                    scores(it - 1, o, 1, 1)
                    weigh(it - 1, o, 1, 0)
                    weigh(it - 1, o, 1, 1)
                if live(0):
                    pe.wait_ge(k_rounded, it + 1)
                    pe.wait_ge(q_rounded, it + 1)
                    if past(0, 2):
                        pe.wait_ge(added, it - 1)
                    if past(0, 1):
                        pe.wait_ge(max_copied, it)
                    for b in range(BPT):
                        for gp in range(2):
                            if b == 1:
                                pe.wait_ge(maxed, 4 * it + gp + 1)
                            pe.matmul(pM[gp][:, :, :].rearrange("p a b -> p (a b)"), QR[:, b, 2 * gp:2 * gp + 2, :].rearrange("p g s -> p (g s)"),
                                      KR[:, b, :, :, :].rearrange("p k e s -> p (k e s)"), start=True, stop=True).then_inc(scored, 1)
            over_tiles(pe, body, 0, 2)

        @block.scalar
        def _(act):
            act.wait_ge(w_loaded, W_ALL)
            for k in range(KD):
                act.activation(wq[:, k, :, :].rearrange("p g (h e) -> p g h e", h=NKV),
                               wq_in[:, k, :].rearrange("p (h g e) -> p g h e", h=NKV, g=G), ACT.Copy).then_inc(wq_sorted, 1)

            def exp(t, b, kh):
                n = 4 * t + 2 * b + kh
                act.wait_ge(keyed, n + 1)
                if not (isinstance(t, int) and t == 0 and b == 0):
                    act.wait_ge(weighed, n - 1)
                act.activation(E[:, kh, :, :], pE[kh][:, :, :], ACT.Exp, scale=HD ** -0.5).then_inc(exped, 1)

            def body(it, a, live, past):
                if live(0):
                    act.wait_ge(turned, it + 1)
                    act.activation(cT[:, :, :], pC[:, :, :], ACT.Copy).then_inc(cT_copied, 1)
                if live(-1):
                    exp(it - 1, 0, 0)
                    exp(it - 1, 0, 1)
                if live(0):
                    act.wait_ge(kv_done, it + 1)
                    if past(0, 1):
                        act.wait_ge(k_spread, it)
                    act.activation(KT[:, :, :].rearrange("p b s -> p (b s)"), pC[:, 0, :], ACT.Identity, bias=bk[:, :]).then_inc(k_copied, 1)
                if live(-1):
                    exp(it - 1, 1, 0)
                if live(0):
                    act.wait_ge(q_done, it + 1)
                    for g in range(G):
                        q = act.activation(QT[:, a, :, g, :], pX[:, g, :].rearrange("p (b s) -> p b s", b=BPT), ACT.Identity, bias=bq[:, g:g + 1])
                    q.then_inc(q_copied, 1)
                if live(-1):
                    exp(it - 1, 1, 1)
            over_tiles(act, body, 0, 1)

        @block.vector
        def _(dve):
            dve.wait_ge(consts, n_consts)
            dve.wait_ge(w_loaded, W_ALL)
            for a in range(2):
                for kp in range(KP):
                    for e in range(2):
                        at = (32 * kp + 64) % P + HD * e
                        dve.memset(VB[64 * e:64 * e + 64, a, :, kp, at:at + HD], 1.0)
            dve.memset(nmaxT[:, :].bitcast(F32), 0.0).then_inc(sel_set, 1)
            for b in range(BPT):
                for gp in range(2):
                    dve.tensor_copy(sel[:, b, gp, :, :], self32[:, b, gp, :, :]).then_inc(sel_set, 2)
            dve.tensor_scalar(gbo[:, :], bo[:, :], sh.tanh_g[:, 2:3], None, ALU.mult).then_inc(gbo_ready, 1)

            def normalize(t, u):
                if not (isinstance(t, int) and t < 2):
                    dve.wait_ge(turned, t - 1)
                dve.tensor_scalar(xn[:, u, :], sh.x[:, t, :], sh.rstd[:, bass.ds(t, 1)], sh.nmr[:, bass.ds(t, 1)],
                                  ALU.mult, ALU.add).then_inc(xn_ready, 1)

            def body(it, a, live, past):
                o = 1 - a
                if live(0):
                    dve.wait_ge(turned, it + 1)
                    dve.tensor_copy(xT[:, :, :], pX[:, :, :]).then_inc(xT_copied, 1)
                if live(-1):
                    dve.wait_ge(max_turned, it)
                    dve.tensor_copy(nmaxT[0:32, :], pM[0][0:32, 0:2, :].rearrange("p a b -> p (a b)")).then_inc(max_copied, 1)
                if live(1):
                    normalize(it + 1, o)
                if live(-2):
                    t = it - 2
                    dve.wait_ge(out_done, t + 1)
                    dve.wait_ge(biased, t + 1)
                    dve.scalar_tensor_tensor(sh.x[:, t, :], pM[1][:, :, :].rearrange("p a b -> p (a b)"), sh.tanh_g[:, 2:3],
                                             sh.x[:, t, :], ALU.mult, ALU.add).then_inc(added, 1)
                if live(0):
                    dve.wait_ge(k_copied, it + 1)
                    for b in range(BPT):
                        rows = slice(64 * b, 64 * b + 64)
                        for e in range(2):
                            at = HD * e
                            dst = VB[64 * e:64 * e + 64, a, b, :, :].rearrange("p k n -> p (k n)")
                            dst = bass.AP(dst.tensor, dst.offset + at, [dst.ap[0], [P + 32, KP], [1, HD]])
                            src = pC[rows, 1, :].rearrange("p (k e n) -> p k e n", k=KP, e=2)[:, :, e, :]
                            bias = bv[rows, :].rearrange("p (k e n) -> p k e n", k=KP, e=2)[:, :, e, :]
                            v = dve.tensor_tensor(dst, src, bias, ALU.add)
                    v.then_inc(v_spread, 1)
                    for q in range(KP):
                        rows = slice(32 * q, 32 * q + 32)
                        src = KT[rows, :, :].rearrange("p b (e s) -> p b e s", e=1).broadcast_to([32, BPT, 2, S])
                        k = dve.tensor_tensor(KB[rows, a, :, q, :, :], src, half[rows, :, :, :], ALU.mult)
                    k.then_inc(k_spread, 1)
                    dve.wait_ge(k_spread, it + 1)
                    dve.tensor_copy(KR[:, :, :, :, :].rearrange("p b k e s -> p (b k e s)"),
                                    KB[:, a, :, :, :, :].rearrange("p b k e s -> p (b k e s)")).then_inc(k_rounded, 1)
                    dve.wait_ge(q_copied, it + 1)
                    dve.tensor_copy(QR[:, :, :, :].rearrange("p b g s -> p (b g s)"),
                                    QT[:, a, :, :, :].rearrange("p b g s -> p (b g s)")).then_inc(q_rounded, 1)
                if live(-1):
                    t = it - 1
                    dve.wait_ge(weighed, 4 * it)
                    for kh in range(2):
                        mine, other = slice(64 * kh, 64 * kh + 64), slice(64 - 64 * kh, 128 - 64 * kh)
                        i = dve.reciprocal(rec[mine, :, :, :], pY[other, :, kh, :, :])
                    i.then_inc(inverted, 1)
                    dve.wait_ge(inverted, it)
                    for kh in range(2):
                        mine = slice(64 * kh, 64 * kh + 64)
                        i = dve.tensor_tensor(yT[mine, o, :, :, :].rearrange("p g b s -> p b g s"), pY[mine, :, kh, :, :], rec[mine, :, :, :], ALU.mult)
                    i.then_inc(normed, 1)
                if live(0):
                    for b in range(BPT):
                        for gp in range(2):
                            n = 2 * b + gp
                            dve.wait_ge(scored, 4 * it + n + 1)
                            dve.tensor_reduce(nmax[:, b, gp, :], pM[gp][:, :, :], AX.X, ALU.max, negate=True).then_inc(maxed, 1)
            normalize(0, 0)
            over_tiles(dve, body, 0, 2)


C, CODES, SUB = 32, 32, 16
NCL = 32
CLS = D // NCL
CG = P // CODES
NU = C // CG
VAR_STEPS = 5


def second_ffn(nc, io, out, sh):
    with ExitStack() as c:
        sb = lambda n, s, dt=F32: c.enter_context(nc.sbuf_tensor("f1_" + n, s, dt))
        pb = lambda n, s, dt=F32: c.enter_context(nc.psum_tensor("f1_" + n, s, dt))
        sem = lambda n: c.enter_context(nc.semaphore("f1_" + n))
        books_in, books = sb("books_in", [P, NU, SUB]), sb("books", [P, NU, CG * SUB])
        codes, cents = sb("codes", [P, NU, D], I32), sb("cents", [P, NU, NCL], I32)
        code_id, code_idf = sb("code_id", [P, 1], I32), sb("code_idf", [P, 1])
        hot = sb("hot", [P, 2, D])
        hotc = sb("hotc", [P, NU, NCL])
        WT, cT = sb("WT", [P, KD, D]), sb("cT", [P, KD, NCL])
        bias, lnw = sb("bias", [P, D]), sb("lnw", [P, NCL])
        xn, xT = sb("xn", [P, 2, D]), sb("xT", [P, 2, KD, P])
        dots, cen, z = sb("dots", [P, N, NCL]), sb("cen", [P, N, NCL]), sb("z", [P, N, NCL])
        (mean, var, std, rs, rs2, top, total, kept, keep_t) = (sb(n, [P, N]) for n in ("mean", "var", "std", "rs", "rs2", "top", "total", "kept", "keep_t"))
        used, keep_c = sb("used", [P, NCL]), sb("keep_c", [P, NCL])
        part = sb("part", [P, 2, D])
        pW = [pb(f"pW{k}", [P, D]) for k in range(2)]
        pCW = pb("pCW", [P, KD, NCL])
        pX = [pb(f"pX{k}", [P, KD, P]) for k in range(2)]
        pDot = [pb(f"pDot{k}", [P, NCL]) for k in range(2)]
        books_loaded, codes_loaded, small_loaded = sem("books_loaded"), sem("codes_loaded"), sem("small_loaded")
        zeroed, ids, ids_float, books_ready = sem("zeroed"), sem("ids"), sem("ids_float"), sem("books_ready")
        hot_ready, hotc_ready, expanded, w_copied, cents_expanded, cents_copied = (
            sem(n) for n in ("hot_ready", "hotc_ready", "expanded", "w_copied", "cents_expanded", "cents_copied"))
        xn_ready, turned, xT_copied, product, used_product = (
            [sem(f"{n}{w}") for w in range(2)] for n in ("xn_ready", "turned", "xT_copied", "product", "used_product"))
        step, std_ready, z_ready, exp_ready, used_ready, counted = (
            sem(n) for n in ("mask_step", "std_ready", "z_ready", "exp_ready", "used_ready", "counted"))
        masked, biased = sem("masked"), sem("biased")
        stored = sem("stored")
        block = c.enter_context(nc.Block())
        x_out = out.rearrange("(i b) s d -> (b s) i d", b=BPT)

        @block.sync
        def _(sp):
            sp.dma_start(books_in[:, :, :], io["L1_ffn_codebooks"].rearrange("(u c) k s -> (c k) u s", c=CG)).then_inc(books_loaded, 16)
            cents_in = io["L1_ffn_centroids"].rearrange("(u c a) n -> c a u n", c=CG, a=1)
            codes_in = io["L1_ffn_codes"].rearrange("(u c a) n -> c a u n", c=CG, a=1)
            for q in range(CG):
                rows = slice(q * CODES, (q + 1) * CODES)
                sp.dma_start(cents[rows, :, :], cents_in[q].broadcast_to([CODES, NU, NCL])).then_inc(codes_loaded, 16)
                sp.dma_start(codes[rows, :, :], codes_in[q].broadcast_to([CODES, NU, D])).then_inc(codes_loaded, 16)
            sp.dma_start(bias[:, :], io["L1_ffn_bias"].rearrange("(a n) -> a n", a=1).broadcast_to([P, D])).then_inc(small_loaded, 16)
            sp.dma_start(lnw[:, :], io["L1_ffn_ln_weight"].rearrange("(a n) -> a n", a=1).broadcast_to([P, NCL])).then_inc(small_loaded, 16)

            def body(it, b, live, past):
                if live(0):
                    sp.wait_ge(used_product[1], it + 1)
                    sp.dma_start(x_out[:, bass.ds(it, 1), :].rearrange("p a d -> p (a d)"), sh.x[:, it, :]).then_inc(stored, 16)
            over_tiles(sp, body, 0, 0)
            sp.wait_ge(stored, 16 * N)

        @block.gpsimd
        def _(pool):
            pool.memset(books[:, :, :], 0.0).then_inc(zeroed, 1)
            for q in range(CG):
                pool.iota(code_id[q * CODES:(q + 1) * CODES, :], pattern=[[0, 1]], base=0, channel_multiplier=1).then_inc(ids, 1)
                pool.wait_ge(ids, q + 1)

        @block.tensor
        def _(pe):
            pe.wait_ge(books_ready, 1)
            pe.wait_ge(hotc_ready, 1)
            for u in range(NU):
                mm = pe.matmul(pCW[64 * (u % 2):64 * (u % 2) + 64, u // 2, :], books[:, u, :], hotc[:, u, :], start=True, stop=True)
            mm.then_inc(cents_expanded, 1)
            for u in range(NU):
                pe.wait_ge(hot_ready, u + 1)
                if u >= 4 and u % 2 == 0:
                    pe.wait_ge(w_copied, u // 2 - 1)
                pe.matmul(pW[u // 2 % 2][64 * (u % 2):64 * (u % 2) + 64, :], books[:, u, :], hot[:, u % 2, :], start=True, stop=True).then_inc(expanded, 1)
            pe.wait_ge(cents_copied, 1)

            def tiles(w, dst, weights):
                def body(it, b, live, past):
                    if live(0):
                        pe.wait_ge(xn_ready[w], it + 1)
                        if past(0, 2):
                            pe.wait_ge(xT_copied[w], it - 1)
                        for k in range(KD):
                            mm = pe.transpose(pX[b][:, k, :], xn[:, b, k * P:(k + 1) * P], sh.ident[:, :])
                        mm.then_inc(turned[w], 1)
                    if live(-1):
                        o = 1 - b
                        pe.wait_ge(xT_copied[w], it)
                        if past(-1, 2):
                            pe.wait_ge(used_product[w], it - 2)
                        for k in range(KD):
                            mm = pe.matmul(dst[o][:, :], xT[:, o, k, :], weights[:, k, :], start=(k == 0), stop=(k == KD - 1))
                        mm.then_inc(product[w], 1)
                over_tiles(pe, body, 0, 1)

            tiles(0, pDot, cT)
            pe.wait_ge(used_ready, 1)
            pe.matmul(pCW[:, 0, :], sh.ones[:, :], used[:, :], start=True, stop=True).then_inc(counted, 1)
            pe.wait_ge(masked, 1)
            tiles(1, pW, WT)

        @block.scalar
        def _(act):
            def copies(w):
                def body(it, b, live, past):
                    if live(0):
                        act.wait_ge(turned[w], it + 1)
                        if past(0, 2):
                            act.wait_ge(product[w], it - 1)
                        act.activation(xT[:, b, :, :], pX[b][:, :, :], ACT.Copy).then_inc(xT_copied[w], 1)
                over_tiles(act, body, 0, 0)

            copies(0)
            act.wait_ge(step, VAR_STEPS)
            act.activation(std[:, :], var[:, :], ACT.Sqrt, bias=sh.eps[:, :], scale=1.0 / NCL).then_inc(std_ready, 1)
            act.wait_ge(z_ready, 1)
            act.activation(z[:, :, :], cen[:, :, :], ACT.Exp).then_inc(exp_ready, 1)
            copies(1)

        @block.vector
        def _(dve):
            dve.wait_ge(zeroed, 1)
            dve.wait_ge(books_loaded, 16)
            for q in range(CG):
                rows = slice(q * CODES, (q + 1) * CODES)
                i = dve.tensor_copy(books[rows, :, q * SUB:(q + 1) * SUB], books_in[rows, :, :])
            i.then_inc(books_ready, 1)
            dve.wait_ge(ids, CG)
            dve.tensor_copy(code_idf[:, :], code_id[:, :]).then_inc(ids_float, 1)
            dve.wait_ge(ids_float, 1)
            dve.wait_ge(codes_loaded, 16 * 2 * CG)
            dve.tensor_scalar(hotc[:, :, :], cents[:, :, :], code_idf[:, :], None, ALU.is_equal).then_inc(hotc_ready, 1)
            for u in range(NU):
                if u >= 2:
                    dve.wait_ge(expanded, u - 1)
                dve.tensor_scalar(hot[:, u % 2, :], codes[:, u, :], code_idf[:, :], None, ALU.is_equal).then_inc(hot_ready, 1)
                if u == 2:
                    dve.wait_ge(cents_expanded, 1)
                    dve.tensor_copy(cT[:, :, :], pCW[:, :, :]).then_inc(cents_copied, 1)
                if u % 2 == 1 and u >= 3:
                    dve.wait_ge(expanded, u - 1)
                    k = u // 2 - 1
                    dve.tensor_copy(WT[:, k, :], pW[k % 2][:, :]).then_inc(w_copied, 1)
            dve.wait_ge(expanded, NU)
            dve.tensor_copy(WT[:, KD - 1, :], pW[(KD - 1) % 2][:, :]).then_inc(w_copied, 1)

            def normalize(w, t, u):
                if not (isinstance(t, int) and t < 2):
                    dve.wait_ge(turned[w], t - 1)
                dve.tensor_scalar(xn[:, u, :], sh.x[:, t, :], sh.rstd[:, bass.ds(t, 1)], sh.nmr[:, bass.ds(t, 1)],
                                  ALU.mult, ALU.add).then_inc(xn_ready[w], 1)

            def first(it, b, live, past):
                if live(1):
                    normalize(0, it + 1, 1 - b)
                if live(-1):
                    dve.wait_ge(product[0], it)
                    dve.tensor_copy(dots[:, it - 1, :], pDot[1 - b][:, :]).then_inc(used_product[0], 1)
            over_tiles(dve, first, 1, 1)

            st = Steps(dve, step, 0, 0)
            over = lambda a: a[:, :].rearrange("p (n a) -> p n a", a=1).broadcast_to([P, N, NCL])
            dve.wait_ge(used_product[0], N)
            st.done(dve.tensor_reduce(mean[:, :], dots[:, :, :], AX.X, ALU.add))
            st.done(dve.tensor_scalar(rs[:, :], mean[:, :], 1.0 / NCL, None, ALU.mult))
            st.done(dve.tensor_tensor(cen[:, :, :], dots[:, :, :], over(rs), ALU.subtract))
            st.done(dve.tensor_tensor(z[:, :, :], cen[:, :, :], cen[:, :, :], ALU.mult))
            st.done(dve.tensor_reduce(var[:, :], z[:, :, :], AX.X, ALU.add))
            assert st.n == VAR_STEPS
            dve.wait_ge(std_ready, 1)
            st.done(dve.reciprocal(rs[:, :], std[:, :]))
            st.mark(dve.tensor_scalar(std[:, :], var[:, :], 1.0 / NCL, EPS, ALU.mult, ALU.add))
            st.done(dve.tensor_tensor(rs2[:, :], rs[:, :], rs[:, :], ALU.mult))
            st.done(dve.tensor_tensor(mean[:, :], std[:, :], rs2[:, :], ALU.mult))
            st.done(dve.tensor_scalar(rs2[:, :], mean[:, :], -0.5, 1.5, ALU.mult, ALU.add))
            st.done(dve.tensor_tensor(mean[:, :], rs[:, :], rs2[:, :], ALU.mult))
            st.done(dve.tensor_tensor(z[:, :, :], cen[:, :, :], over(mean), ALU.mult))
            dve.wait_ge(small_loaded, 32)
            st.done(dve.tensor_tensor(dots[:, :, :], z[:, :, :],
                                      lnw[:, :].rearrange("p (a c) -> p a c", a=1).broadcast_to([P, N, NCL]), ALU.mult))
            st.done(dve.tensor_reduce(top[:, :], dots[:, :, :], AX.X, ALU.max))
            dve.tensor_tensor(cen[:, :, :], dots[:, :, :], over(top), ALU.subtract).then_inc(z_ready, 1)
            dve.wait_ge(exp_ready, 1)
            st.done(dve.tensor_reduce(total[:, :], z[:, :, :], AX.X, ALU.add))
            st.done(dve.tensor_scalar(rs[:, :], total[:, :], 0.5, None, ALU.mult))
            st.done(dve.tensor_tensor(dots[:, :, :], z[:, :, :], over(rs), ALU.is_gt))
            st.done(dve.tensor_reduce(kept[:, :], dots[:, :, :], AX.X, ALU.max))
            dve.tensor_reduce(used[:, :], dots[:, :, :].rearrange("p n c -> p c n"), AX.X, ALU.max).then_inc(used_ready, 1)
            st.done(dve.tensor_scalar(keep_t[:, :], kept[:, :], sh.tanh_g[:, 3:4], None, ALU.mult))
            dve.wait_ge(counted, 1)
            st.done(dve.tensor_scalar(keep_c[:, :], pCW[:, 0, :], 0.5, None, ALU.is_gt))
            columns = keep_c[:, :].rearrange("p (c a) -> p c a", a=1).broadcast_to([P, NCL, CLS])
            dve.wait_ge(w_copied, KD)
            for k in range(KD):
                w = WT[:, k, :].rearrange("p (c a) -> p c a", c=NCL)
                dve.tensor_tensor(w, w, columns, ALU.mult)
            bm = bias[:, :].rearrange("p (c a) -> p c a", c=NCL)
            dve.tensor_tensor(bm, bm, columns, ALU.mult).then_inc(masked, 1)
            dve.wait_ge(masked, 1)

            def second(it, b, live, past):
                if live(1):
                    normalize(1, it + 1, 1 - b)
                if live(-1):
                    t, o = it - 1, 1 - b
                    keep = keep_t[:, bass.ds(t, 1)]
                    dve.scalar_tensor_tensor(part[:, o, :], bias[:, :], keep, sh.x[:, t, :], ALU.mult, ALU.add).then_inc(biased, 1)
                    dve.wait_ge(biased, it)
                    dve.wait_ge(product[1], it)
                    dve.scalar_tensor_tensor(sh.x[:, t, :], pW[o][:, :], keep, part[:, o, :], ALU.mult, ALU.add).then_inc(used_product[1], 1)
            over_tiles(dve, second, 1, 1)


class Shared:
    pass


def flamingo(nc, io, out, phases="SABCD"):
    sh = Shared()
    with ExitStack() as c:
        sb = lambda n, s, dt=F32: c.enter_context(nc.sbuf_tensor(n, s, dt))
        sh.x = sb("x", [P, N, D])
        sh.ident, sh.identb, sh.ones = sb("ident", [P, P]), sb("identb", [P, P], BF16), sb("ones", [P, P])
        sh.tanh_g, sh.scales = sb("tanh_g", [P, 4]), sb("scales", [P, 3])
        sh.wmean, sh.wscale = sb("wmean", [P, 3]), sb("wscale", [P, 3])
        sh.eps, sh.round = sb("eps", [P, 1]), sb("round", [P, 1])
        sh.rstd, sh.nmr = sb("rstd_all", [P, N]), sb("nmr_all", [P, N])
        sh.gateT, sh.upT = sb("gateT", [P, KD, FF], BF16), sb("upT", [P, KD, FF], BF16)
        sh.downT = sb("downT", [P, FJ, D], BF16)
        x_loaded = c.enter_context(nc.semaphore("x_loaded"))
        sh.x_in = io["x"].rearrange("(i b) s d -> (b s) i d", b=BPT)
        consts_set = c.enter_context(nc.semaphore("consts_set"))
        with nc.Block() as block:
            @block.sync
            def _(sp):
                x_in = io["x"].rearrange("(i b) s d -> i (b s) d", b=BPT)
                for i in range(N):
                    sp.dma_start(sh.x[:, i, :], x_in[i]).then_inc(x_loaded, 16)
                sp.wait_ge(x_loaded, 16 * N)

            @block.vector
            def _(dve):
                dve.memset(sh.eps[:, :], EPS).then_inc(consts_set, 1)
                dve.memset(sh.round[:, :], ROUND).then_inc(consts_set, 1)
                dve.wait_ge(consts_set, 2)
        if "A" in phases:
            layer_norms(nc, sh, "n0_")
        if "S" in phases:
            setup(nc, io, sh)
        if "A" in phases:
            first_attention(nc, io, sh)
        if "B" in phases:
            first_ffn(nc, io, sh)
        if "C" in phases:
            layer_norms(nc, sh, "n2_")
            second_attention(nc, io, sh)
        if "D" in phases:
            layer_norms(nc, sh, "n3_")
            second_ffn(nc, io, out, sh)
        else:
            stored = c.enter_context(nc.semaphore("stored"))
            with nc.Block() as block:
                @block.sync
                def _(sp):
                    x_out = out.rearrange("(i b) s d -> i (b s) d", b=BPT)
                    for i in range(N):
                        sp.dma_start(x_out[i], sh.x[:, i, :]).then_inc(stored, 16)
                    sp.wait_ge(stored, 16 * N)


def kernel(**inputs):
    import numpy as _np
    import concourse.bacc as _bacc
    from concourse import mybir as _mybir
    from concourse.bass_utils import run_bass_kernel_spmd as _run

    nc = _bacc.Bacc("TRN2", target_bir_lowering=False, num_devices=1)
    arrays, io = {}, {}
    for name, value in inputs.items():
        a = _np.ascontiguousarray(value)
        arrays[f"in_{name}"] = a
        io[name] = nc.dram_tensor(f"in_{name}", a.shape, _mybir.dt.from_np(a.dtype), kind="ExternalInput").ap()
    out = nc.dram_tensor("out_0", (B, S, D), F32, kind="ExternalOutput").ap()
    flamingo(nc, io, out)
    r = _run(nc, [arrays], core_ids=[0])
    return r.results[0]["out_0"]
```

```python
import concourse.bass as bass
from concourse import mybir
from contextlib import ExitStack

F32 = mybir.dt.float32
F32R = mybir.dt.float32r
BF16 = mybir.dt.bfloat16
I32 = mybir.dt.int32
ALU = mybir.AluOpType
ACT = mybir.ActivationFunctionType
AX = mybir.AxisListType

P = 128
B, S, D = 32, 64, 512
N = B * S // P
BPT = P // S
KD = D // P
EPS = 1e-5
ROUND = 1.5 * 2.0 ** 23

FF = 1376
FJ = (FF + P - 1) // P
FR = FF - (FJ - 1) * P
NCH = 4
FC = FF // NCH
SQRT7 = 7.0 ** 0.5


class Steps:

    def __init__(self, eng, sem, tile, per):
        self.eng, self.sem, self.base, self.n = eng, sem, tile * per, 0

    def mark(self, ins):
        ins.then_inc(self.sem, 1)
        self.n += 1

    def done(self, ins):
        self.mark(ins)
        self.eng.wait_ge(self.sem, self.base + self.n)


def over_tiles(eng, body, ahead, behind, reach=1):
    def peeled(first, last):
        for it in range(first, last):
            body(it, it % 2, lambda k, it=it: 0 <= it + k < N, lambda k, n, it=it: it + k >= n)

    steady = lambda *_: True
    lo, hi = 4, N - 2 * reach
    peeled(-ahead, lo)
    with eng.Fori(lo, hi, 2) as it:
        body(it, 0, steady, steady)
        body(it + 1, 1, steady, steady)
    peeled(hi, N + behind)


class FirstFfnRaw:

    def __init__(self, nc, c):
        sb = lambda n, s, dt=F32: c.enter_context(nc.sbuf_tensor("w0_" + n, s, dt))
        self.gate, self.up, self.down = sb("raw_gate", [P, FJ, D]), sb("raw_up", [P, FJ, D]), sb("raw_down", [P, KD, FF])
        self.loaded = [c.enter_context(nc.semaphore(f"w0_raw_loaded{w}")) for w in range(3)]
        self.loads = (32, 32, 16)

    def load(self, sp, io):
        for w, (dst, name) in enumerate(((self.gate, "L0_ffn_w_gate"), (self.up, "L0_ffn_w_up"))):
            src = io[name]
            sp.dma_start(dst[:, 0:FJ - 1, :], src[0:(FJ - 1) * P, :].rearrange("(j p) k -> p j k", p=P)).then_inc(self.loaded[w], 16)
            sp.dma_start(dst[0:FR, FJ - 1, :], src[(FJ - 1) * P:FF, :]).then_inc(self.loaded[w], 16)
        sp.dma_start(self.down[:, :, :], io["L0_ffn_w_down"].rearrange("(o p) f -> p o f", p=P)).then_inc(self.loaded[2], 16)


def setup(nc, io, sh, rw, a0):
    with ExitStack() as c:
        sb = lambda n, s, dt=F32: c.enter_context(nc.sbuf_tensor("w0_" + n, s, dt))
        sem = lambda n: c.enter_context(nc.semaphore("w0_" + n))
        raw = [r[:, :, :].rearrange("p a b -> p (a b)") for r in (rw.gate, rw.up, rw.down)]
        low = sb("low", [P, FJ * D], BF16)
        trash = sb("trash", [P, FJ * D], BF16)
        tern = [sb(f"tern{w}", [P, FJ * D], BF16) for w in range(3)]
        sums, tot, thr = sb("sums", [P, 3, 2]), sb("tot", [P, 3]), sb("thr", [P, 3, 2])
        down = sb("down", [P, 1])
        gates_in = sb("gates_in", [P, 4])
        pT = [c.enter_context(nc.psum_tensor(f"pT{k}", [P, 4, P], BF16)) for k in range(4)]
        pS = [c.enter_context(nc.psum_tensor(f"pS{w}", [P, 2], F32)) for w in range(3)]
        small_loaded, zeroed, constants, identities = sem("small_loaded"), sem("zeroed"), sem("constants"), sem("identities")
        abs_summed, totals, step, ternary = sem("abs_summed"), sem("totals"), sem("vector_step"), sem("ternary")
        transposed, copied_act, copied_dve, gates = sem("transposed"), sem("copied_act"), sem("copied_dve"), sem("gates")
        odd_set = sem("odd_set")
        block = c.enter_context(nc.Block())

        whole = [(P, 0, (FJ - 1) * D), (FR, (FJ - 1) * D, D)]
        parts = [whole, whole, [(P, 0, KD * FF)]]
        groups = []
        for j in range(FJ):
            n = P if j < FJ - 1 else FR
            groups.append((0, [j * D + k * P for k in range(KD)], n, P, sh.gateT[:, :, j * P:j * P + n]))
        for j in range(FJ):
            n = P if j < FJ - 1 else FR
            groups.append((1, [j * D + k * P for k in range(KD)], n, P, sh.upT[:, :, j * P:j * P + n]))
        for j in range(FJ):
            n = P if j < FJ - 1 else FR
            groups.append((2, [o * FF + j * P for o in range(KD)], P, n,
                           sh.downT[0:n, j, :].rearrange("p (o n) -> p o n", n=P)))

        @block.gpsimd
        def _(pool):
            pool.memset(sh.ident[:, :], 0.0).then_inc(zeroed, 1)
            pool.memset(sh.identb[:, :], 0.0).then_inc(zeroed, 1)
            pool.memset(sh.ones[:, :], 1.0).then_inc(constants, 1)
            pool.memset(sums[:, :, :], 0.0).then_inc(constants, 1)
            for n, (g, k) in enumerate((("g_xattn", 0), ("g_ffn", 0), ("g_xattn", 1), ("g_ffn", 1))):
                pool.dma_start(gates_in[:, n:n + 1], io[g][k:k + 1].rearrange("(a n) -> a n", a=1).broadcast_to([P, 1])).then_inc(small_loaded, 16)
            for n, g in enumerate(("L0_ffn_s_gate", "L0_ffn_s_up", "L0_ffn_s_down")):
                pool.dma_start(sh.scales[:, n:n + 1], io[g].rearrange("(a n) -> a n", a=1).broadcast_to([P, 1])).then_inc(small_loaded, 16)
            pool.wait_ge(zeroed, 2)
            pool.wait_ge(constants, 2)
            for q in range(4):
                rows = sh.odd[32 * q:32 * q + 32, :]
                pool.affine_select(out=rows[:, 0:1], in_=sh.ones[32 * q:32 * q + 32, 0:1], compare_op=ALU.is_ge, fill=0.0,
                                   base=15, pattern=[[0, 1]], channel_multiplier=-1).then_inc(odd_set, 1)
                pool.affine_select(out=rows[:, 1:2], in_=sh.ones[32 * q:32 * q + 32, 0:1], compare_op=ALU.is_ge, fill=0.0,
                                   base=-16, pattern=[[0, 1]], channel_multiplier=1).then_inc(odd_set, 1)
                pool.wait_ge(odd_set, 2 * q + 2)
            a0.build(pool)
            for m in (sh.ident, sh.identb):
                pool.affine_select(out=m[:, :], in_=m[:, :], compare_op=ALU.not_equal, fill=1.0, base=0,
                                   pattern=[[-1, P]], channel_multiplier=1).then_inc(identities, 1)

        on_vector = lambda g: g >= 2 * FJ and g % 2 == 1
        before = lambda g: sum(on_vector(h) == on_vector(g) for h in range(g + 1))

        @block.scalar
        def _(act):
            act.wait_ge(constants, 2)
            n = 0

            def abs_sums(w):
                nonlocal n
                act.wait_ge(rw.loaded[w], rw.loads[w])
                for k, (rows, at, cols) in enumerate(parts[w]):
                    if n:
                        act.wait_ge(abs_summed, n)
                    act.activation(trash[0:rows, at:at + cols], raw[w][0:rows, at:at + cols], ACT.Abs,
                                   accum_out=sums[0:rows, w, k:k + 1]).then_inc(abs_summed, 1)
                    n += 1

            def copies(w):
                for g in range(FJ * w, FJ * w + FJ):
                    if not on_vector(g):
                        _, at, rows, cols, dst = groups[g]
                        act.wait_ge(transposed, g + 1)
                        act.activation(dst, pT[g % 4][0:cols, :, 0:rows], ACT.Copy).then_inc(copied_act, 1)

            abs_sums(0)
            abs_sums(1)
            abs_sums(2)
            act.wait_ge(small_loaded, 16 * 7)
            act.activation(sh.tanh_g[:, :], gates_in[:, :], ACT.Tanh).then_inc(gates, 1)
            copies(0)
            copies(1)
            copies(2)

        @block.tensor
        def _(pe):
            pe.wait_ge(constants, 2)

            def total(w):
                pe.wait_ge(abs_summed, sum(len(p) for p in parts[:w + 1]))
                pe.matmul(pS[w][:, :], sh.ones[:, :], sums[:, w, :], start=True, stop=True).then_inc(totals, 1)

            total(0)
            total(1)
            pe.wait_ge(identities, 2)
            for g, (w, at, rows, cols, dst) in enumerate(groups):
                if g == FJ:
                    total(2)
                pe.wait_ge(ternary, w + 1)
                if g >= 4:
                    pe.wait_ge(copied_dve if on_vector(g - 4) else copied_act, before(g - 4))
                for k in range(KD):
                    mm = pe.transpose(pT[g % 4][0:cols, k, 0:rows], tern[w][0:rows, at[k]:at[k] + cols], sh.identb[0:rows, 0:rows])
                mm.then_inc(transposed, 1)

        @block.vector
        def _(dve):
            st = Steps(dve, step, 0, 0)
            for w in range(3):
                dve.wait_ge(totals, w + 1)
                mean, above, below = sh.wmean[:, w:w + 1], thr[:, w, 0:1], thr[:, w, 1:2]
                st.done(dve.tensor_reduce(tot[:, w:w + 1], pS[w][:, :], AX.X, ALU.add))
                st.done(dve.tensor_scalar(mean, tot[:, w:w + 1], 1.0 / (FF * D), None, ALU.mult))
                st.mark(dve.tensor_scalar(above, mean, EPS, 0.5, ALU.add, ALU.mult))
                st.done(dve.tensor_scalar(below, mean, EPS, -0.5, ALU.add, ALU.mult))
                for rows, at, cols in parts[w]:
                    here = slice(at, at + cols)
                    st.done(dve.tensor_scalar(low[0:rows, here], raw[w][0:rows, here], thr[0:rows, w, 1:2], None, ALU.is_lt))
                    st.done(dve.scalar_tensor_tensor(tern[w][0:rows, here], raw[w][0:rows, here], thr[0:rows, w, 0:1],
                                                     low[0:rows, here], ALU.is_gt, ALU.subtract))
                dve.sem_inc(ternary, 1)
            dve.wait_ge(gates, 1)
            st.done(dve.tensor_tensor(sh.wscale[:, :], sh.wmean[:, :], sh.scales[:, :], ALU.mult))
            st.done(dve.tensor_tensor(down[:, :], sh.wscale[:, 2:3], sh.tanh_g[:, 1:2], ALU.mult))
            st.done(dve.tensor_scalar(sh.wscale[:, 2:3], down[:, :], 1.0 / 127.0, None, ALU.mult))
            for g, (w, at, rows, cols, dst) in enumerate(groups):
                if on_vector(g):
                    dve.wait_ge(transposed, g + 1)
                    dve.tensor_copy(dst, pT[g % 4][0:cols, :, 0:rows]).then_inc(copied_dve, 1)


NH0, HD0, WIN = 8, 8, 16
LEFT = WIN // 2
Q4, R4 = 4, 4
TB = 32
NT = D // TB
NJ = NT + 1
W0 = TB + WIN
KPAD = NJ * TB
QPAD = D + W0
NGR = (NJ + 1) // 2
NEG = -1e30


class FirstAttentionConstants:
    NAMES = ("Wq", "Wk", "Wv", "Wo")

    def __init__(self, nc, c):
        sb = lambda n, s, dt=F32: c.enter_context(nc.sbuf_tensor("a0_" + n, s, dt))
        sem = lambda n: c.enter_context(nc.semaphore("a0_" + n))
        self.wnat, self.bias = sb("wnat", [P, 4, P]), sb("bias", [P, 4])
        self.win_s, self.win_k = sb("win_s", [P, W0], BF16), sb("win_k", [P, W0], BF16)
        self.rmask = sb("rmask", [P, R4])
        self.diag = sb("diag", [P, TB])
        self.zeroed, self.loaded, self.step = sem("zeroed"), sem("loaded"), sem("const_step")
        self.loads = 16 * (2 * 4 + 2 * 4)

    def load(self, eng, io):
        eng.wait_ge(self.zeroed, 1)
        for w, name in enumerate(self.NAMES):
            for b in range(BPT):
                rows = slice(S * b, S * b + S)
                eng.dma_start(self.wnat[rows, w, rows], io["L0_xattn_" + name]).then_inc(self.loaded, 16)
                eng.dma_start(self.bias[rows, w:w + 1], io["L0_xattn_b" + name[1]].rearrange("(p a) -> p a", a=1)).then_inc(self.loaded, 16)

    def build(self, pool):
        st = Steps(pool, self.step, 0, 0)
        st.mark(pool.memset(self.win_s[:, :], 0.0))
        st.mark(pool.memset(self.win_k[:, :], 0.0))
        st.mark(pool.memset(self.rmask[:, :], 1.0))
        st.done(pool.memset(self.diag[:, :], 1.0))

        def keep(part, base, pattern, by, fill, op=ALU.is_ge):
            st.done(pool.affine_select(out=part, in_=part, compare_op=op, fill=fill, base=base, pattern=pattern, channel_multiplier=by))

        for n in range(Q4):
            rows = slice(TB * n, TB * n + TB)
            keep(self.win_s[rows, :], 0, [[1, W0]], -1, NEG)
            keep(self.win_s[rows, :], WIN - 1, [[-1, W0]], 1, NEG)
            keep(self.win_k[rows, :], -1, [[1, W0]], -1, NEG)
            keep(self.win_k[rows, :], WIN, [[-1, W0]], 1, NEG)
            keep(self.rmask[rows, :], 0, [[-HD0, R4]], 1, 0.0)
            keep(self.rmask[rows, :], HD0 - 1, [[HD0, R4]], -1, 0.0)
            keep(self.diag[rows, :], 0, [[-1, TB]], 1, 0.0, ALU.is_equal)
        self.steps = st.n


def first_attention(nc, io, sh, cs):
    with ExitStack() as c:
        sb = lambda n, s, dt=F32: c.enter_context(nc.sbuf_tensor("a0_" + n, s, dt))
        pb = lambda n, s, dt=F32: c.enter_context(nc.psum_tensor("a0_" + n, s, dt))
        sem = lambda n: c.enter_context(nc.semaphore("a0_" + n))
        wnat, bias, rmask, diag = cs.wnat, cs.bias, cs.rmask, cs.diag
        wsort, wT = sb("wsort", [P, P]), sb("wT", [P, 4, P])
        gbo = sb("gbo", [P, 1])
        mask_s, mask_k = sb("mask_s", [P, 2 * R4, W0], BF16), sb("mask_k", [P, 2 * R4, W0], BF16)
        quad, quadR = sb("quad", [P, P]), sb("quadR", [P, P], F32R)
        ctx, xn = sb("ctx", [P, 2, D]), sb("xn", [P, 2, D])
        q, k, v = sb("q", [P, D]), sb("k", [P, KPAD]), sb("v", [P, KPAD])
        QD = sb("QD", [P, NT, Q4, TB], F32R)
        KM = sb("KM", [P, R4, KPAD], F32R)
        KD = sb("KD", [P, 2, NJ, Q4, TB])
        QM = sb("QM", [P, 2, R4, QPAD])
        nmax = sb("nmax", [P, NT, R4])
        DM = sb("DM", [P, 2, R4, QPAD], F32R)
        vT = sb("vT", [P, NJ, R4, HD0])
        VM = sb("VM", [P, 2, NJ, R4, 2, Q4, HD0])
        E = sb("E", [P, 2, 2, R4, W0])
        den, rec, yraw, yn = sb("den", [P, D]), sb("rec", [P, D]), sb("yraw", [P, D]), sb("yn", [P, D])
        o = sb("o", [P, D])
        pA, pB = pb("pA", [P, D]), pb("pB", [P, D])
        pM = [pb(f"pM{n}", [P, 2, R4, W0]) for n in range(2)]
        pE = [pb(f"pE{n}", [P, 2, R4, W0]) for n in range(2)]
        pY = [pb(f"pY{n}", [P, D]) for n in range(2)]
        ones_set = sem("ones_set")
        pool_zeroed, cleared, quad_ready, w_sorted, w_turned, w_ready = (
            sem(n) for n in ("pool_zeroed", "cleared", "quad_ready", "w_sorted", "w_turned", "w_ready"))
        ctx_loaded = [sem(f"ctx_loaded{n}") for n in range(2)]
        xn_ready, q_done, k_done, v_done, q_copied, k_copied, v_copied = (
            sem(n) for n in ("xn_ready", "q_done", "k_done", "v_done", "q_copied", "k_copied", "v_copied"))
        QD_ready, KM_ready, QM_ready, KD_ready, vT_ready = (sem(n) for n in ("QD_ready", "KM_ready", "QM_ready", "KD_ready", "vT_ready"))
        scored, maxed, DM_ready = sem("scored"), sem("maxed"), sem("DM_ready")
        keyed, exped, weighed, spread = sem("keyed"), sem("exped"), sem("weighed"), sem("spread")
        y_copied, den_copied, inverted, normed, out_done, out_copied, added = (
            sem(n) for n in ("y_copied", "den_copied", "inverted", "normed", "out_done", "out_copied", "added"))
        block = c.enter_context(nc.Block())

        @block.sync
        def _(sp):
            c_in = io["ctx_4096"].rearrange("(i b) s d -> (b s) i d", b=BPT)

            def body(it, b, live, past):
                if live(1):
                    if past(1, 2):
                        sp.wait_ge(v_done, it)
                    sp.dma_start(ctx[:, 1 - b, :], c_in[:, bass.ds(it + 1, 1), :].rearrange("p a d -> p (a d)")).then_inc(ctx_loaded[1 - b], 32)
            over_tiles(sp, body, 1, 0)

        @block.gpsimd
        def _(pool):
            pool.memset(KD[:, :, :, :, :], 0.0).then_inc(pool_zeroed, 1)
            pool.memset(VM[:, :, :, :, 0, :, :], 0.0).then_inc(pool_zeroed, 1)
            pool.wait_ge(pool_zeroed, 2)

            def body(it, a, live, past):
                if live(0):
                    if past(0, 3):
                        pool.wait_ge(added, it - 2)
                    pool.wait_ge(k_copied, it + 1)
                    if past(0, 2):
                        pool.wait_ge(keyed, NGR * (it - 1))
                    for n in range(Q4):
                        rows = slice(TB * n, TB * n + TB)
                        src = k[rows, :].rearrange("p (j c) -> p j c", j=NJ)
                        ones = sh.ones[rows, 0:TB].rearrange("p (b c) -> p b c", b=1).broadcast_to([TB, NJ, TB])
                        pool.tensor_tensor(KD[rows, a, :, n, :], src, ones, ALU.mult).then_inc(KD_ready, 1)
                    pool.wait_ge(KD_ready, Q4 * (it + 1))
                    pool.wait_ge(vT_ready, it + 1)
                    if past(0, 2):
                        pool.wait_ge(weighed, NGR * (it - 1))
                    for n in range(Q4):
                        rows = slice(TB * n, TB * n + TB)
                        ones = sh.ones[rows, 0:HD0].rearrange("p (a b d) -> p a b d", a=1, b=1).broadcast_to([TB, NJ, R4, HD0])
                        pool.tensor_tensor(VM[rows, a, :, :, 0, n, :], vT[rows, :, :, :], ones, ALU.mult).then_inc(spread, 1)
                if live(-2):
                    t = it - 2
                    pool.wait_ge(out_copied, t + 1)
                    pool.wait_ge(spread, Q4 * (it + 1) if live(0) else Q4 * N)
                    xt = sh.x[:, t, :]
                    pool.tensor_tensor(xt, xt, o[:, :], ALU.add).then_inc(added, 1)
            over_tiles(pool, body, 0, 2)

        @block.tensor
        def _(pe):
            pe.wait_ge(cs.loaded, cs.loads)
            pe.wait_ge(w_sorted, 1)
            for w in range(4):
                mm = pe.transpose(pA[:, w * P:(w + 1) * P], wsort[:, :] if w == 3 else wnat[:, w, :], sh.ident[:, :])
            mm.then_inc(w_turned, 1)
            pe.wait_ge(w_ready, 1)
            pe.wait_ge(quad_ready, 1)

            def scores(t, a, g):
                n = NGR * t + g
                if g >= 2 or not (isinstance(t, int) and t == 0):
                    pe.wait_ge(exped, n - 1)
                blocks = 2 if g < NGR - 1 else 1
                cols = W0 if g < NGR - 1 else WIN
                for i in range(blocks):
                    j = 2 * g + i
                    pe.matmul(pE[g % 2][:, i, :, 0:cols], KD[:, a, j, :, :].rearrange("p n j -> p (n j)"),
                              QM[:, a, :, TB * j:TB * j + cols], start=(i == 0), stop=False, skip_group_check=True)
                    pe.matmul(pE[g % 2][:, i, :, 0:cols], quadR[:, :], DM[:, a, :, TB * j:TB * j + cols],
                              start=False, stop=False, skip_group_check=True)
                mask = mask_k[:, 0:blocks * R4, 0:cols].rearrange("p (i r) c -> p i r c", i=blocks)
                pe.matmul(pE[g % 2][:, 0:blocks, :, 0:cols], sh.identb[:, :], mask, start=False, stop=True,
                          skip_group_check=True).then_inc(keyed, 1)

            def weigh(t, a, g):
                n = NGR * t + g
                pe.wait_ge(exped, n + 1)
                if g == 0:
                    pe.wait_ge(spread, Q4 * (t + 1))
                    if isinstance(t, int) and t == 0:
                        pe.wait_ge(ones_set, 1)
                    else:
                        pe.wait_ge(y_copied, t)
                        pe.wait_ge(den_copied, t)
                for i in range(2 if g < NGR - 1 else 1):
                    j = 2 * g + i
                    lo, hi = max(0, TB * j - WIN), min(D, TB * j + TB)
                    at = lo - (TB * j - WIN)
                    for r in range(R4):
                        rows = slice(64 * (r % 2), 64 * (r % 2) + 64)
                        mm = pe.matmul(pY[r // 2][rows, lo:hi], VM[:, a, j, r, :, :, :].rearrange("p e n d -> p (e n d)"),
                                       E[:, g % 2, i, r, at:at + hi - lo], start=(j == 0), stop=(j == NJ - 1), skip_group_check=True)
                mm.then_inc(weighed, 1)

            def row_scores(it, m):
                n = NT // 2 * it + m
                if m >= 2 or not (isinstance(it, int) and it == 0):
                    pe.wait_ge(maxed, n - 1)
                for i in range(2):
                    t = 2 * m + i
                    pe.matmul(pM[m % 2][:, i, :, :], QD[:, t, :, :].rearrange("p n t -> p (n t)"),
                              KM[:, :, TB * t:TB * t + W0], start=(i == 0), stop=False, skip_group_check=True)
                pe.matmul(pM[m % 2][:, :, :, :].rearrange("p i r c -> p (i r c)"), sh.identb[:, :],
                          mask_s[:, :, :].rearrange("p a c -> p (a c)"), start=False, stop=True,
                          skip_group_check=True).then_inc(scored, 1)

            def body(it, a, live, past):
                s = 1 - a
                if live(0):
                    pe.wait_ge(xn_ready, it + 1)
                    if past(0, 1):
                        pe.wait_ge(v_copied, it)
                    pe.matmul(pA[:, :], wT[:, 0, :], xn[:, a, :], start=True, stop=True).then_inc(q_done, 1)
                    pe.wait_ge(ctx_loaded[a], 16 * (it - a) + 32)
                    if past(0, 3):
                        pe.wait_ge(out_copied, it - 2)
                    pe.matmul(pB[:, :], wT[:, 1, :], ctx[:, a, :], start=True, stop=True).then_inc(k_done, 1)
                if live(-1):
                    pe.wait_ge(DM_ready, it)
                    pe.wait_ge(QM_ready, it)
                    pe.wait_ge(KD_ready, Q4 * it)
                    scores(it - 1, s, 0)
                if live(0):
                    pe.wait_ge(q_copied, it + 1)
                    pe.matmul(pA[:, :], wT[:, 2, :], ctx[:, a, :], start=True, stop=True).then_inc(v_done, 1)
                if live(-1):
                    scores(it - 1, s, 1)
                    weigh(it - 1, s, 0)
                for g in range(2, NGR + 1):
                    if live(-1):
                        if g < NGR:
                            scores(it - 1, s, g)
                        weigh(it - 1, s, g - 1)
                    if 4 <= g < 8 and live(0):
                        if g == 4:
                            pe.wait_ge(QD_ready, it + 1)
                            pe.wait_ge(KM_ready, it + 1)
                        row_scores(it, 2 * (g - 4))
                        row_scores(it, 2 * (g - 4) + 1)
                    if g == 6 and live(-2):
                        pe.wait_ge(normed, it - 1)
                        if live(0):
                            pe.wait_ge(k_copied, it + 1)
                        pe.matmul(pB[:, :], wT[:, 3, :], yn[:, :], start=True, stop=True).then_inc(out_done, 1)
            over_tiles(pe, body, 0, 2)

        @block.scalar
        def _(act):
            act.wait_ge(cs.loaded, cs.loads)
            act.wait_ge(w_turned, 1)
            act.activation(wT[:, :, :].rearrange("p w n -> p (w n)"), pA[:, :], ACT.Copy).then_inc(w_ready, 1)
            act.wait_ge(quad_ready, 1)

            def exp(t, g):
                n = NGR * t + g
                act.wait_ge(keyed, n + 1)
                if g >= 2 or not (isinstance(t, int) and t == 0):
                    act.wait_ge(weighed, n - 1)
                blocks = 2 if g < NGR - 1 else 1
                cols = W0 if g < NGR - 1 else WIN
                act.activation(E[:, g % 2, 0:blocks, :, 0:cols], pE[g % 2][:, 0:blocks, :, 0:cols], ACT.Exp,
                               scale=HD0 ** -0.5).then_inc(exped, 1)

            def body(it, a, live, past):
                if live(0):
                    act.wait_ge(q_done, it + 1)
                    if past(0, 1):
                        act.wait_ge(QM_ready, it)
                    act.activation(q[:, :], pA[:, :], ACT.Identity, bias=bias[:, 0:1]).then_inc(q_copied, 1)
                    act.wait_ge(k_done, it + 1)
                    if past(0, 1):
                        act.wait_ge(KD_ready, Q4 * it)
                        act.wait_ge(KM_ready, it)
                    act.activation(k[:, LEFT:LEFT + D], pB[:, :], ACT.Identity, bias=bias[:, 1:2]).then_inc(k_copied, 1)
                if live(-1):
                    exp(it - 1, 0)
                if live(-2):
                    t = it - 2
                    act.wait_ge(weighed, NGR * (t + 1))
                    if past(-2, 1):
                        act.wait_ge(normed, t)
                    for r in range(R4):
                        mine, at = slice(TB * r, TB * r + TB), 64 * (r % 2)
                        i = act.activation(yraw[mine, :], pY[r // 2][at:at + TB, :], ACT.Copy)
                    i.then_inc(y_copied, 1)
                if live(-1):
                    exp(it - 1, 1)
                if live(0):
                    act.wait_ge(v_done, it + 1)
                    if past(0, 1):
                        act.wait_ge(vT_ready, it)
                    act.activation(v[:, LEFT:LEFT + D], pA[:, :], ACT.Identity, bias=bias[:, 2:3]).then_inc(v_copied, 1)
                if live(-1):
                    exp(it - 1, 2)
                if live(0):
                    if past(0, 1):
                        act.wait_ge(scored, NT // 2 * it)
                    act.wait_ge(q_copied, it + 1)
                    for n in range(Q4):
                        rows = slice(TB * n, TB * n + TB)
                        i = act.activation(QD[rows, :, n, :], q[rows, :].rearrange("p (t c) -> p t c", t=NT), ACT.Copy)
                    i.then_inc(QD_ready, 1)
                for g in range(3, NGR):
                    if live(-1):
                        exp(it - 1, g)
                    if g == 7 and live(-2):
                        t = it - 2
                        act.wait_ge(out_done, t + 1)
                        if past(-2, 1):
                            act.wait_ge(added, t)
                        act.activation(o[:, :], pB[:, :], ACT.Identity, scale=sh.tanh_g[:, 0:1], bias=gbo[:, :]).then_inc(out_copied, 1)
            over_tiles(act, body, 0, 2)

        @block.vector
        def _(dve):
            st = Steps(dve, cleared, 0, 0)
            st.mark(dve.memset(wsort[:, :], 0.0))
            st.done(dve.memset(quad[:, :], 0.0))
            for n in range(Q4):
                i = dve.memset(quad[TB * n:TB * n + TB, TB * n:TB * n + TB], 1.0)
            st.mark(i)
            dve.wait_ge(cs.loaded, cs.loads)
            for b in range(BPT):
                rows = slice(S * b, S * b + S)
                for n in range(2):
                    src = wnat[rows, 3, S * b + TB * n:S * b + TB * n + TB].rearrange("p (r d) -> p r d", r=R4)
                    dst = wsort[rows, :].rearrange("p (r n d) -> p r n d", r=R4, n=Q4)[:, :, 2 * b + n, :]
                    dve.tensor_copy(dst, src)
            dve.tensor_tensor(gbo[:, :], bias[:, 3:4], sh.tanh_g[:, 0:1], ALU.mult).then_inc(w_sorted, 1)
            for tile in (k, v):
                dve.memset(tile[:, 0:LEFT], 0.0)
                dve.memset(tile[:, LEFT + D:], 0.0)
            for tile in (QM[:, :, :, :], DM[:, :, :, :].bitcast(F32)):
                dve.memset(tile[:, :, :, 0:WIN], 0.0)
                dve.memset(tile[:, :, :, WIN + D:], 0.0)
            dve.memset(QD[:, :, :, :].bitcast(F32), 0.0)
            for mask, win in ((mask_s, cs.win_s), (mask_k, cs.win_k)):
                dve.tensor_copy(mask[:, :, :], win[:, :].rearrange("p (a c) -> p a c", a=1).broadcast_to([P, 2 * R4, W0]))
            dve.wait_ge(cleared, 3)
            st.done(dve.tensor_copy(quadR[:, :], quad[:, :]))
            dve.sem_inc(quad_ready, 1)

            def normalize(t, u):
                if not (isinstance(t, int) and t < 2):
                    dve.wait_ge(q_done, t - 1)
                dve.tensor_scalar(xn[:, u, :], sh.x[:, t, :], sh.rstd[:, bass.ds(t, 1)], sh.nmr[:, bass.ds(t, 1)],
                                  ALU.mult, ALU.add).then_inc(xn_ready, 1)

            def body(it, a, live, past):
                if live(-2):
                    dve.wait_ge(weighed, NGR * (it - 1))
                    for r in range(R4):
                        at = 64 * (r % 2) + TB
                        i = dve.tensor_copy(den[TB * r:TB * r + TB, :], pY[r // 2][at:at + TB, :])
                    i.then_inc(den_copied, 1)
                if live(0):
                    dve.wait_ge(k_copied, it + 1)
                    if past(0, 1):
                        dve.wait_ge(scored, NT // 2 * it)
                    for r in range(R4):
                        i = dve.tensor_scalar(KM[:, r, :], k[:, :], rmask[:, r:r + 1], None, ALU.mult)
                    i.then_inc(KM_ready, 1)
                    dve.wait_ge(q_copied, it + 1)
                    if past(0, 2):
                        dve.wait_ge(keyed, NGR * (it - 1))
                    for r in range(R4):
                        i = dve.tensor_scalar(QM[:, a, r, WIN:WIN + D], q[:, :], rmask[:, r:r + 1], None, ALU.mult)
                    i.then_inc(QM_ready, 1)
                if live(1):
                    normalize(it + 1, 1 - a)
                if live(-2):
                    t = it - 2
                    dve.wait_ge(den_copied, t + 1)
                    dve.reciprocal(rec[:, :], den[:, :]).then_inc(inverted, 1)
                if live(0):
                    dve.wait_ge(v_copied, it + 1)
                    if past(0, 1):
                        dve.wait_ge(spread, Q4 * it)
                    dve.transpose(vT[:, :, :, :].rearrange("p j r d -> p (j r d)"), v[:, :]).then_inc(vT_ready, 1)
                if live(-2):
                    dve.wait_ge(inverted, t + 1)
                    dve.wait_ge(y_copied, t + 1)
                    if past(-2, 1):
                        dve.wait_ge(out_done, t)
                    dve.tensor_tensor(yn[:, :], yraw[:, :], rec[:, :], ALU.mult).then_inc(normed, 1)
                if live(0):
                    for m in range(NT // 2):
                        dve.wait_ge(scored, NT // 2 * it + m + 1)
                        dve.tensor_reduce(nmax[:, 2 * m:2 * m + 2, :].rearrange("p i r -> p (i r)"),
                                          pM[m % 2][:, :, :, :].rearrange("p i r c -> p (i r) c"), AX.X, ALU.max, negate=True).then_inc(maxed, 1)
                    dve.wait_ge(maxed, NT // 2 * (it + 1))
                    shape = [P, R4, NT, TB]
                    dve.tensor_tensor(DM[:, a, :, WIN:WIN + D].rearrange("p r (t c) -> p r t c", t=NT),
                                      nmax[:, :, :].rearrange("p (t a) r -> p r t a", a=1).broadcast_to(shape),
                                      diag[:, :].rearrange("p (a b c) -> p a b c", a=1, b=1).broadcast_to(shape),
                                      ALU.mult).then_inc(DM_ready, 1)
            normalize(0, 0)
            own = quad[:, :].rearrange("p (a n c) -> p a n c", a=1, n=Q4)[:, :, :, 0:HD0]
            dve.tensor_copy(VM[:, :, :, :, 1, :, :].rearrange("p a j r n d -> p (a j r) n d"),
                            own.broadcast_to([P, 2 * NJ * R4, Q4, HD0])).then_inc(ones_set, 1)
            over_tiles(dve, body, 0, 2)


def first_ffn(nc, io, sh, next_weights):
    with ExitStack() as c:
        sb = lambda n, s, dt=F32: c.enter_context(nc.sbuf_tensor("f0_" + n, s, dt))
        pb = lambda n, s, dt=F32: c.enter_context(nc.psum_tensor("f0_" + n, s, dt))
        sem = lambda n: c.enter_context(nc.semaphore("f0_" + n))
        qa, qb, iscale, isize = (sb(n, [P, N]) for n in ("qa", "qb", "iscale", "isize"))
        sign = sb("sign", [P, 1])
        cmax, den, inv, hf = (sb(n, [P, 2]) for n in ("cmax", "den", "inv", "hf"))
        oscale = sb("oscale", [P, 2])
        xs, xc = sb("xs", [P, 2, D]), sb("xc", [P, 2, D])
        xq, xqT = sb("xq", [P, 2, D], BF16), sb("xqT", [P, 2, KD, P], BF16)
        r, r2 = sb("r", [P, 2, FC]), sb("r2", [P, 2, FC])
        inter, amax = sb("inter", [P, 2, FF]), sb("amax", [P, 2, NCH])
        hr, hq, hqT = sb("hr", [P, 2, FF]), sb("hq", [P, 2, FF], BF16), sb("hqT", [P, 2, FJ, P], BF16)
        int4_scales(nc, sh, qa, qb, iscale, isize, sign)

        pG, pU = [pb(f"pG{k}", [P, FC]) for k in range(2)], [pb(f"pU{k}", [P, FC]) for k in range(2)]
        pXT = pb("pXT", [P, KD, P], BF16)
        pHT, pHU = pb("pHT", [P, 8, P], BF16), pb("pHU", [P, FJ - 8, P], BF16)
        pD = pb("pD", [P, D])
        x_step, xT_done, xT_copied = sem("x_step"), sem("xT_done"), sem("xT_copied")
        chunk_done, relu_done, squared, multiplied, max_done = (
            sem(n) for n in ("chunk_done", "relu_done", "squared", "multiplied", "max_done"))
        factor_step, scaled, rounded = sem("factor_step"), sem("scaled"), sem("rounded")
        hT_done, hT_copied, hU_copied, down_done, added = (
            sem(n) for n in ("hT_done", "hT_copied", "hU_copied", "down_done", "added"))
        block = c.enter_context(nc.Block())
        FACTOR = 5

        @block.sync
        def _(sp):
            next_weights.load(sp, io)

        @block.tensor
        def _(pe):
            def transpose_x(t, u):
                pe.wait_ge(x_step, 3 * t + 3)
                if not (isinstance(t, int) and t == 0):
                    pe.wait_ge(xT_copied, t)
                for k in range(KD):
                    mm = pe.transpose(pXT[:, k, :], xq[:, u, k * P:(k + 1) * P], sh.identb[:, :])
                mm.then_inc(xT_done, 1)

            def body(it, b, live, past):
                o = 1 - b
                if live(0):
                    pe.wait_ge(xT_copied, it + 1)
                for ch in range(NCH):
                    if live(0):
                        u = ch % 2
                        if ch >= 2 or past(0, 1):
                            pe.wait_ge(multiplied, NCH * it + ch - 1)
                        for p, w in ((pG[u], sh.gateT), (pU[u], sh.upT)):
                            for k in range(KD):
                                mm = pe.matmul(p[:, :], xqT[:, b, k, :], w[:, k, ch * FC:(ch + 1) * FC], start=(k == 0), stop=(k == KD - 1))
                        mm.then_inc(chunk_done, 1)
                    if ch == 1 and live(1):
                        transpose_x(it + 1, o)
                    if ch == 2 and live(-1):
                        pe.wait_ge(rounded, it)
                        if past(-1, 1):
                            pe.wait_ge(hT_copied, it - 1)
                            pe.wait_ge(hU_copied, it - 1)
                        for j in range(FJ):
                            n = P if j < FJ - 1 else FR
                            dst = pHT[0:n, j, :] if j < 8 else pHU[0:n, j - 8, :]
                            mm = pe.transpose(dst, hq[:, o, j * P:j * P + n], sh.identb[:, :])
                        mm.then_inc(hT_done, 1)
                if live(-1):
                    pe.wait_ge(hT_copied, it)
                    pe.wait_ge(hU_copied, it)
                    if past(-1, 1):
                        pe.wait_ge(added, it - 1)
                    for j in range(FJ):
                        n = P if j < FJ - 1 else FR
                        mm = pe.matmul(pD[:, :], hqT[0:n, o, j, :], sh.downT[0:n, j, :], start=(j == 0), stop=(j == FJ - 1))
                    mm.then_inc(down_done, 1)
            transpose_x(0, 0)
            over_tiles(pe, body, 0, 1)

        @block.scalar
        def _(act):
            def copy_xT(t, u):
                act.wait_ge(xT_done, t + 1)
                if not (isinstance(t, int) and t < 2):
                    act.wait_ge(chunk_done, NCH * (t - 1))
                act.activation(xqT[:, u, :, :], pXT[:, :, :], ACT.Copy).then_inc(xT_copied, 1)

            def body(it, b, live, past):
                o = 1 - b
                for ch in range(NCH):
                    if live(0):
                        u, n = ch % 2, NCH * it + ch
                        act.wait_ge(chunk_done, n + 1)
                        act.activation(r[:, u, :], pG[u][:, :], ACT.Relu, scale=sign[:, :]).then_inc(relu_done, 1)
                        if ch >= 2 or past(0, 1):
                            act.wait_ge(multiplied, n - 1)
                        act.wait_ge(relu_done, n + 1)
                        act.activation(r2[:, u, :], r[:, u, :], ACT.Square).then_inc(squared, 1)
                    if ch == 2 and live(-1):
                        act.wait_ge(hT_done, it)
                        act.activation(hqT[:, o, 0:8, :], pHT[:, :, :], ACT.Copy).then_inc(hT_copied, 1)
                    if ch == 0 and live(-1):
                        act.wait_ge(factor_step, FACTOR * it)
                        if past(-1, 2):
                            act.wait_ge(rounded, it - 2)
                        act.activation(hr[:, o, :], inter[:, o, :], ACT.Identity, bias=sh.round[:, :], scale=hf[:, o:o + 1]).then_inc(scaled, 1)
                    if ch == 1 and live(1):
                        copy_xT(it + 1, o)
            copy_xT(0, 0)
            over_tiles(act, body, 0, 1)

        @block.vector
        def _(dve):
            def scale_x(t, u):
                dve.tensor_scalar(xs[:, u, :], sh.x[:, t, :], qa[:, bass.ds(t, 1)], qb[:, bass.ds(t, 1)], ALU.mult, ALU.add).then_inc(x_step, 1)

            def clip_x(t, u):
                dve.wait_ge(x_step, 3 * t + 1)
                dve.tensor_scalar(xc[:, u, :], xs[:, u, :], 7.0, -8.0, ALU.min, ALU.max).then_inc(x_step, 1)

            def round_x(t, u):
                dve.wait_ge(x_step, 3 * t + 2)
                if not (isinstance(t, int) and t < 2):
                    dve.wait_ge(xT_done, t - 1)
                dve.tensor_scalar(xq[:, u, :], xc[:, u, :], ROUND, ROUND, ALU.add, ALU.subtract).then_inc(x_step, 1)

            def body(it, b, live, past):
                o = 1 - b
                if live(-1):
                    dve.wait_ge(max_done, NCH * it)
                    if past(-1, 2):
                        dve.wait_ge(scaled, it - 2)
                        dve.wait_ge(added, it - 2)
                    st = Steps(dve, factor_step, it - 1, FACTOR)
                    size, scale = isize[:, bass.ds(it - 1, 1)], iscale[:, bass.ds(it - 1, 1)]
                    col = slice(o, o + 1)
                    st.done(dve.tensor_reduce(cmax[:, col], amax[:, o, :], AX.X, ALU.max))
                    st.mark(dve.tensor_scalar(oscale[:, col], cmax[:, col], size, sh.wscale[:, 2:3], ALU.mult, ALU.mult))
                    st.done(dve.tensor_scalar(den[:, col], cmax[:, col], size, EPS, ALU.mult, ALU.add))
                    st.done(dve.reciprocal(inv[:, col], den[:, col]))
                    st.mark(dve.tensor_scalar(hf[:, col], inv[:, col], scale, 127.0, ALU.mult, ALU.mult))
                if live(2):
                    scale_x(it + 2, b)
                    clip_x(it + 2, b)
                    round_x(it + 2, b)
                for ch in range(NCH):
                    if ch == 1 and live(-1):
                        dve.wait_ge(scaled, it)
                        if past(-1, 2):
                            dve.wait_ge(hT_done, it - 2)
                        dve.tensor_scalar(hq[:, o, :], hr[:, o, :], ROUND, None, ALU.subtract).then_inc(rounded, 1)
                    if ch == 2 and live(-1):
                        dve.wait_ge(hT_done, it)
                        dve.tensor_copy(hqT[:, o, 8:FJ - 1, :], pHU[:, 0:FJ - 9, :])
                        dve.tensor_copy(hqT[0:FR, o, FJ - 1, :], pHU[0:FR, FJ - 9, :]).then_inc(hU_copied, 1)
                    if live(0):
                        u, n = ch % 2, NCH * it + ch
                        dve.wait_ge(squared, n + 1)
                        if ch == 0 and past(0, 2):
                            dve.wait_ge(scaled, it - 1)
                        here = inter[:, b, ch * FC:(ch + 1) * FC]
                        dve.tensor_tensor(here, pU[u][:, :], r2[:, u, :], ALU.mult).then_inc(multiplied, 1)
                        dve.wait_ge(multiplied, n + 1)
                        dve.tensor_reduce(amax[:, b, ch:ch + 1], here, AX.X, ALU.max, apply_absolute_value=True).then_inc(max_done, 1)
                    if ch == 1 and live(-2):
                        dve.wait_ge(down_done, it - 1)
                        xt = sh.x[:, it - 2, :]
                        dve.scalar_tensor_tensor(xt, pD[:, :], oscale[:, b:b + 1], xt, ALU.mult, ALU.add).then_inc(added, 1)
            for t in range(2):
                scale_x(t, t)
                clip_x(t, t)
                round_x(t, t)
            over_tiles(dve, body, 0, 2, reach=2)


def int4_scales(nc, sh, qa, qb, iscale, isize, sign):
    with ExitStack() as c:
        sb = lambda n, s, dt=F32: c.enter_context(nc.sbuf_tensor("q0_" + n, s, dt))
        sem = lambda n: c.enter_context(nc.semaphore("q0_" + n))
        stats, mv, nmean, asum = sb("stats", [P, N, 6]), sb("mv", [P, N, 2]), sb("nmean", [P, N]), sb("asum", [P, N])
        std, rstd, t1, t2, beta = (sb(n, [P, N]) for n in ("std", "rstd", "t1", "t2", "beta"))
        trash = sb("trash", [P, 2, D], BF16)
        stat_ready, var_ready, nmean_ready, std_ready, abs_ready, step = (
            sem(n) for n in ("stat_ready", "var_ready", "nmean_ready", "std_ready", "abs_ready", "step"))
        block = c.enter_context(nc.Block())

        @block.vector
        def _(dve):
            def aggregate(i):
                dve.wait_ge(stat_ready, i + 1)
                dve.bn_aggr(mv[:, i, :], stats[:, i, :]).then_inc(var_ready, 1)

            def negate(i):
                dve.wait_ge(var_ready, i + 1)
                dve.tensor_scalar(nmean[:, i:i + 1], mv[:, i, 0:1], -1.0, None, ALU.mult).then_inc(nmean_ready, 1)

            for i in range(N + 2):
                if i < N:
                    dve.bn_stats(stats[:, i, :], sh.x[:, i, :]).then_inc(stat_ready, 1)
                if 1 <= i < N + 1:
                    aggregate(i - 1)
                if i >= 2:
                    negate(i - 2)
            st = Steps(dve, step, 0, 0)
            st.mark(dve.tensor_scalar(sign[:, :], sh.scales[:, 0:1], 0.0, None, ALU.is_ge))
            dve.wait_ge(std_ready, 1)
            st.done(dve.reciprocal(t1[:, :], std[:, :]))
            st.done(dve.tensor_scalar(sign[:, :], sign[:, :], 2.0, 1.0, ALU.mult, ALU.subtract))
            st.done(dve.tensor_tensor(t2[:, :], t1[:, :], t1[:, :], ALU.mult))
            st.done(dve.scalar_tensor_tensor(std[:, :], mv[:, :, 1], EPS, t2[:, :], ALU.add, ALU.mult))
            st.done(dve.tensor_scalar(t2[:, :], std[:, :], -0.5, 1.5, ALU.mult, ALU.add))
            st.done(dve.tensor_tensor(rstd[:, :], t1[:, :], t2[:, :], ALU.mult))
            dve.wait_ge(abs_ready, N)
            st.done(dve.scalar_tensor_tensor(beta[:, :], asum[:, :], 1.0 / D, rstd[:, :], ALU.mult, ALU.mult))
            st.done(dve.tensor_scalar(t1[:, :], beta[:, :], EPS, 1.0 / SQRT7, ALU.add, ALU.mult))
            st.done(dve.reciprocal(t2[:, :], t1[:, :]))
            st.done(dve.tensor_tensor(qa[:, :], rstd[:, :], t2[:, :], ALU.mult))
            st.mark(dve.tensor_tensor(qb[:, :], nmean[:, :], qa[:, :], ALU.mult))
            st.done(dve.tensor_scalar(t1[:, :], beta[:, :], sh.wscale[:, 0:1], None, ALU.mult))
            st.mark(dve.tensor_scalar(t2[:, :], beta[:, :], sh.wscale[:, 1:2], None, ALU.mult))
            st.done(dve.tensor_tensor(std[:, :], t1[:, :], t1[:, :], ALU.mult))
            st.done(dve.tensor_tensor(iscale[:, :], std[:, :], t2[:, :], ALU.mult))
            st.done(dve.scalar_tensor_tensor(isize[:, :], iscale[:, :], -1.0, iscale[:, :], ALU.mult, ALU.max))

        @block.scalar
        def _(act):
            for i in range(N):
                act.wait_ge(nmean_ready, i + 1)
                if i >= 2:
                    act.wait_ge(abs_ready, i - 1)
                act.activation(trash[:, i % 2, :], sh.x[:, i, :], ACT.Abs, bias=nmean[:, i:i + 1],
                               accum_out=asum[:, i:i + 1]).then_inc(abs_ready, 1)
            act.activation(std[:, :], mv[:, :, 1], ACT.Sqrt, bias=sh.eps[:, :]).then_inc(std_ready, 1)


XT = 4


def layer_norms(nc, sh, tag, sync=None, x_loaded=None):
    with ExitStack() as c:
        sb = lambda n, s, dt=F32: c.enter_context(nc.sbuf_tensor(tag + n, s, dt))
        sem = lambda n: c.enter_context(nc.semaphore(tag + n))
        stats, mv, std, t1, t2 = sb("stats", [P, N, 6]), sb("mv", [P, N, 2]), sb("std", [P, N]), sb("t1", [P, N]), sb("t2", [P, N])
        stat_ready, var_ready, std_ready, step = sem("stat_ready"), sem("var_ready"), sem("std_ready"), sem("norm_step")
        block = c.enter_context(nc.Block())

        if sync:
            block.sync(sync)

        @block.vector
        def _(dve):
            def stat(i):
                if x_loaded and i % XT == 0:
                    dve.wait_ge(x_loaded[i // XT], 16)
                dve.bn_stats(stats[:, i, :], sh.x[:, i, :]).then_inc(stat_ready, 1)

            def aggregate(i):
                dve.wait_ge(stat_ready, i + 1)
                dve.bn_aggr(mv[:, i, :], stats[:, i, :]).then_inc(var_ready, 1)

            stat(0)
            for i in range(1, N):
                stat(i)
                aggregate(i - 1)
            aggregate(N - 1)
            st = Steps(dve, step, 0, 0)
            dve.wait_ge(std_ready, 1)
            st.done(dve.reciprocal(t1[:, :], std[:, :]))
            st.done(dve.tensor_tensor(t2[:, :], t1[:, :], t1[:, :], ALU.mult))
            st.done(dve.scalar_tensor_tensor(std[:, :], mv[:, :, 1], EPS, t2[:, :], ALU.add, ALU.mult))
            st.done(dve.tensor_scalar(t2[:, :], std[:, :], -0.5, 1.5, ALU.mult, ALU.add))
            st.done(dve.tensor_tensor(sh.rstd[:, :], t1[:, :], t2[:, :], ALU.mult))
            st.done(dve.scalar_tensor_tensor(sh.nmr[:, :], mv[:, :, 0], -1.0, sh.rstd[:, :], ALU.mult, ALU.mult))

        @block.scalar
        def _(act):
            act.wait_ge(var_ready, N)
            act.activation(std[:, :], mv[:, :, 1], ACT.Sqrt, bias=sh.eps[:, :]).then_inc(std_ready, 1)


NQ, NKV = 32, 8
HD = D // NQ
G = NQ // NKV
KP = NKV // 2


class SecondAttentionWeights:

    def __init__(self, nc, c):
        sb = lambda n, s, dt=F32: c.enter_context(nc.sbuf_tensor("a1_" + n, s, dt))
        self.wq, self.wk, self.wv = sb("wq_in", [P, KD, D]), sb("wk", [P, KD, P]), sb("wv", [P, KD, P])
        self.wo = sb("wo", [P, G, D])
        self.bq, self.bk, self.bv, self.bo = sb("bq", [P, G]), sb("bk", [P, 1]), sb("bv", [P, P]), sb("bo", [P, D])
        self.loaded = c.enter_context(nc.semaphore("a1_w_loaded"))
        self.loads = 16 * (3 + NKV + NKV * G + 3)

    def load(self, sp, io):
        for dst, name in ((self.wq, "Wq"), (self.wk, "Wk"), (self.wv, "Wv")):
            sp.dma_start(dst[:, :, :], io["L1_xattn_" + name].rearrange("(k p) n -> p k n", p=P)).then_inc(self.loaded, 16)
        wo_in = io["L1_xattn_Wo"].rearrange("(h g e) n -> h g e n", h=NKV, g=G)
        for h in range(NKV):
            sp.dma_start(self.wo[h * HD:(h + 1) * HD, :, :], wo_in[h].rearrange("g e n -> e g n")).then_inc(self.loaded, 16)
        bq_in = io["L1_xattn_bq"].rearrange("(h g e a) -> h g e a", h=NKV, g=G, a=1)
        for h in range(NKV):
            for g in range(G):
                sp.dma_start(self.bq[h * HD:(h + 1) * HD, g:g + 1], bq_in[h, g]).then_inc(self.loaded, 16)
        sp.dma_start(self.bk[:, :], io["L1_xattn_bk"].rearrange("(p a) -> p a", a=1)).then_inc(self.loaded, 16)
        sp.dma_start(self.bv[:, :], io["L1_xattn_bv"].rearrange("(a n) -> a n", a=1).broadcast_to([P, P])).then_inc(self.loaded, 16)
        sp.dma_start(self.bo[:, :], io["L1_xattn_bo"].rearrange("(a n) -> a n", a=1).broadcast_to([P, D])).then_inc(self.loaded, 16)


def second_attention(nc, io, sh, w_in, next_weights):
    with ExitStack() as c:
        sb = lambda n, s, dt=F32: c.enter_context(nc.sbuf_tensor("a1_" + n, s, dt))
        pb = lambda n, s, dt=F32: c.enter_context(nc.psum_tensor("a1_" + n, s, dt))
        sem = lambda n: c.enter_context(nc.semaphore("a1_" + n))
        wk, wv, wo, bq, bk, bv = w_in.wk, w_in.wv, w_in.wo, w_in.bq, w_in.bk, w_in.bv
        wq = sb("wq", [P, KD, G, P])
        wq_sorted = sem("wq_sorted")
        gbo = sb("gbo", [P, D])
        ctx = sb("ctx", [P, 2, D])
        xn, xT, cT = sb("xn", [P, 2, D]), sb("xT", [P, KD, P]), sb("cT", [P, KD, P])
        QT = sb("QT", [P, 2, BPT, G, S])
        QR = sb("QR", [P, BPT, G, S], F32R)
        KT = sb("KT", [P, BPT, S])
        KB = sb("KB", [P, 2, BPT, KP, 2, S])
        KR = sb("KR", [P, BPT, KP, 2, S], F32R)
        VB = sb("VB", [P, 2, BPT, KP, 2, 2, HD])
        E = sb("E", [P, 2, 2, G * S])
        nmax = sb("nmax", [P, BPT, 2, NKV])
        nmaxT = sb("nmaxT", [P, P], F32R)
        sel = sb("sel", [P, BPT, 2, KP, P], F32R)
        den, rec, yraw = (sb(n, [P, BPT, G, S]) for n in ("den", "rec", "yraw"))
        yT = sb("yT", [P, G, BPT, S])
        pX, pC = pb("pX", [P, KD, P]), pb("pC", [P, KD, P])
        pM = [pb(f"pM{k}", [P, KP * 2, S]) for k in range(2)]
        pE = [pb(f"pE{k}", [P, 2, G * S]) for k in range(2)]
        pY = pb("pY", [P, BPT, 2, G, S])
        vector_set, zeroed, gbo_ready = sem("vector_set"), sem("zeroed"), sem("gbo_ready")
        ctx_loaded = [sem(f"ctx_loaded{k}") for k in range(2)]
        xn_ready, biased = sem("xn_ready"), sem("biased")
        x_turned, turned, xT_copied, cT_copied = sem("x_turned"), sem("turned"), sem("xT_copied"), sem("cT_copied")
        kv_done, q_done, k_copied, k_spread, k_rounded, v_spread, q_copied, q_rounded = (
            sem(n) for n in ("kv_done", "q_done", "k_copied", "k_spread", "k_rounded", "v_spread", "q_copied", "q_rounded"))
        scored, maxed, max_turned, max_copied = sem("scored"), sem("maxed"), sem("max_turned"), sem("max_copied")
        keyed, exped, weighed, inverted, normed = (sem(n) for n in ("keyed", "exped", "weighed", "inverted", "normed"))
        y_copied = [sem(f"y_copied{b}") for b in range(BPT)]
        out_done, added = sem("out_done"), sem("added")
        block = c.enter_context(nc.Block())

        @block.sync
        def _(sp):
            c_in = io["ctx_4096"].rearrange("(i b) s d -> (b s) i d", b=BPT)
            def body(it, b, live, past):
                if live(1):
                    if past(1, 2):
                        sp.wait_ge(turned, it)
                    sp.dma_start(ctx[:, 1 - b, :], c_in[:, bass.ds(it + 1, 1), :].rearrange("p a d -> p (a d)")).then_inc(ctx_loaded[1 - b], 32)
            over_tiles(sp, body, 1, 0)
            next_weights.load(sp, io)

        @block.gpsimd
        def _(pool):
            pool.memset(VB[:, :, :, :, :, :, :].rearrange("p a b k o e n -> p (a b k o e n)"), 0.0).then_inc(zeroed, 1)
            pool.memset(KB[:, :, :, :, :, :].rearrange("p a b k e s -> p (a b k e s)"), 0.0).then_inc(zeroed, 1)
            pool.wait_ge(gbo_ready, 1)

            def body(it, b, live, past):
                if live(0):
                    pool.wait_ge(xn_ready, it + 1)
                    xt = sh.x[:, it, :]
                    pool.tensor_tensor(xt, xt, gbo[:, :], ALU.add).then_inc(biased, 1)
            over_tiles(pool, body, 0, 0)

        @block.tensor
        def _(pe):
            pe.wait_ge(w_in.loaded, w_in.loads)
            pe.wait_ge(vector_set, 2)
            pe.wait_ge(wq_sorted, KD)

            def scores(t, a, b, kh):
                n = 4 * t + 2 * b + kh
                if not (isinstance(t, int) and t == 0 and b == 0):
                    pe.wait_ge(exped, n - 1)
                for j in range(2):
                    kp = 2 * kh + j
                    pe.matmul(pE[kh][:, j, :], KB[:, a, b, kp, :, :].rearrange("p e s -> p (e s)"),
                              QT[:, a, b, :, :].rearrange("p g s -> p (g s)"), start=True, stop=False,
                              skip_group_check=True)
                    for gp in range(2):
                        mm = pe.matmul(pE[kh][:, j, gp * 2 * S:(gp + 1) * 2 * S], sel[:, b, gp, kp, :], nmaxT[:, :],
                                       start=False, stop=(gp == 1), skip_group_check=True)
                mm.then_inc(keyed, 1)

            def weigh(t, a, b, kh):
                n = 4 * t + 2 * b + kh
                pe.wait_ge(exped, n + 1)
                if kh == 0 and not (isinstance(t, int) and t == 0):
                    pe.wait_ge(y_copied[b], t)
                for j in range(2):
                    mm = pe.matmul(pY[64 * j:64 * j + 64, b, kh, :, :].rearrange("p g s -> p (g s)"),
                                   VB[:, a, b, 2 * kh + j, :, :, :].rearrange("p o e n -> p (o e n)"),
                                   E[:, kh, j, :], start=True, stop=True, skip_group_check=True)
                mm.then_inc(weighed, 1)

            def row_scores(it, b, gp):
                pe.matmul(pM[gp][:, :, :].rearrange("p a b -> p (a b)"), QR[:, b, 2 * gp:2 * gp + 2, :].rearrange("p g s -> p (g s)"),
                          KR[:, b, :, :, :].rearrange("p k e s -> p (k e s)"), start=True, stop=True).then_inc(scored, 1)

            def body(it, a, live, past):
                o = 1 - a
                if live(0):
                    pe.wait_ge(xn_ready, it + 1)
                    pe.wait_ge(ctx_loaded[a], 16 * (it - a) + 32)
                    if past(0, 1):
                        pe.wait_ge(q_copied, it)
                    for k in range(KD):
                        mm = pe.transpose(pX[:, k, :], xn[:, a, k * P:(k + 1) * P], sh.ident[:, :])
                    mm.then_inc(x_turned, 1)
                    if past(0, 1):
                        pe.wait_ge(v_spread, it)
                        pe.wait_ge(k_copied, it)
                    if past(0, 3):
                        pe.wait_ge(added, it - 2)
                    for k in range(KD):
                        mm = pe.transpose(pC[:, k, :], ctx[:, a, k * P:(k + 1) * P], sh.ident[:, :])
                    mm.then_inc(turned, 1)
                if live(-1):
                    t = it - 1
                    pe.wait_ge(maxed, 4 * it)
                    pe.transpose(pM[0][0:32, 0:2, :].rearrange("p a b -> p (a b)"), nmax[:, :, :, :].rearrange("p b g h -> p (b g h)"),
                                 sh.ident[:, :]).then_inc(max_turned, 1)
                if live(0):
                    pe.wait_ge(cT_copied, it + 1)
                    for k in range(KD):
                        pe.matmul(pC[:, 0, :], wk[:, k, :], cT[:, k, :], start=(k == 0), stop=(k == KD - 1))
                    for k in range(KD):
                        mm = pe.matmul(pC[:, 1, :], cT[:, k, :], wv[:, k, :], start=(k == 0), stop=(k == KD - 1))
                    mm.then_inc(kv_done, 1)
                if live(-1):
                    pe.wait_ge(max_copied, it)
                    scores(it - 1, o, 0, 0)
                    scores(it - 1, o, 0, 1)
                    weigh(it - 1, o, 0, 0)
                    scores(it - 1, o, 1, 0)
                    weigh(it - 1, o, 0, 1)
                if live(0):
                    pe.wait_ge(xT_copied, it + 1)
                    for g in range(G):
                        for k in range(KD):
                            mm = pe.matmul(pX[:, g, :], wq[:, k, g, :], xT[:, k, :], start=(k == 0), stop=(k == KD - 1))
                    mm.then_inc(q_done, 1)
                if live(-1):
                    scores(it - 1, o, 1, 1)
                    weigh(it - 1, o, 1, 0)
                if live(-2):
                    pe.wait_ge(normed, it - 1)
                    if live(0):
                        pe.wait_ge(v_spread, it + 1)
                        pe.wait_ge(k_copied, it + 1)
                for half in range(2):
                    if live(-2):
                        for g in (2 * half, 2 * half + 1):
                            mm = pe.matmul(pC[:, :, :].rearrange("p a b -> p (a b)"), yT[:, g, :, :].rearrange("p b s -> p (b s)"),
                                           wo[:, g, :], start=(g == 0), stop=(g == G - 1))
                        if half == 1:
                            mm.then_inc(out_done, 1)
                    if half == 0 and live(0):
                        pe.wait_ge(k_rounded, it + 1)
                        pe.wait_ge(q_rounded, it + 1)
                        if past(0, 1):
                            pe.wait_ge(max_copied, it)
                        row_scores(it, 0, 0)
                        row_scores(it, 0, 1)
                if live(-1):
                    weigh(it - 1, o, 1, 1)
                if live(0):
                    for gp in range(2):
                        pe.wait_ge(maxed, 4 * it + gp + 1)
                        row_scores(it, 1, gp)
            over_tiles(pe, body, 0, 2)

        @block.scalar
        def _(act):
            act.wait_ge(w_in.loaded, w_in.loads)
            for k in range(KD):
                act.activation(wq[:, k, :, :].rearrange("p g (h e) -> p g h e", h=NKV),
                               w_in.wq[:, k, :].rearrange("p (h g e) -> p g h e", h=NKV, g=G), ACT.Copy).then_inc(wq_sorted, 1)

            def exp(t, b, kh):
                n = 4 * t + 2 * b + kh
                act.wait_ge(keyed, n + 1)
                if not (isinstance(t, int) and t == 0 and b == 0):
                    act.wait_ge(weighed, n - 1)
                act.activation(E[:, kh, :, :], pE[kh][:, :, :], ACT.Exp, scale=HD ** -0.5).then_inc(exped, 1)

            def copy_y(t, b):
                act.wait_ge(weighed, 4 * t + 2 * b + 2)
                for kp in range(KP):
                    mine, at = slice(32 * kp, 32 * kp + 32), 64 * (kp % 2)
                    act.activation(yraw[mine, b, :, :], pY[at:at + 32, b, kp // 2, :, :], ACT.Copy)
                    i = act.activation(den[mine, b, :, :], pY[at + 32:at + 64, b, kp // 2, :, :], ACT.Copy)
                i.then_inc(y_copied[b], 1)

            def body(it, a, live, past):
                if live(0):
                    act.wait_ge(turned, it + 1)
                    act.activation(cT[:, :, :], pC[:, :, :], ACT.Copy).then_inc(cT_copied, 1)
                if live(-2):
                    copy_y(it - 2, 1)
                if live(-1):
                    exp(it - 1, 0, 0)
                    exp(it - 1, 0, 1)
                if live(0):
                    act.wait_ge(kv_done, it + 1)
                    if past(0, 1):
                        act.wait_ge(k_spread, it)
                    act.activation(KT[:, :, :].rearrange("p b s -> p (b s)"), pC[:, 0, :], ACT.Identity, bias=bk[:, :]).then_inc(k_copied, 1)
                if live(-1):
                    exp(it - 1, 1, 0)
                if live(0):
                    act.wait_ge(q_done, it + 1)
                    for g in range(G):
                        q = act.activation(QT[:, a, :, g, :], pX[:, g, :].rearrange("p (b s) -> p b s", b=BPT), ACT.Identity, bias=bq[:, g:g + 1])
                    q.then_inc(q_copied, 1)
                if live(-1):
                    exp(it - 1, 1, 1)
                    if past(-1, 1):
                        act.wait_ge(normed, it - 1)
                    copy_y(it - 1, 0)
            over_tiles(act, body, 0, 2)

        @block.vector
        def _(dve):
            rows = BPT * 2 * NKV
            dve.tensor_copy(sel[:, :, :, :, :].rearrange("p b g k (e s) -> p (b g k e) s", e=2),
                            sh.ident[:, 0:rows].rearrange("p (n a) -> p n a", a=1).broadcast_to([P, rows, S])).then_inc(vector_set, 1)
            dve.memset(nmaxT[:, :].bitcast(F32), 0.0).then_inc(vector_set, 1)
            dve.wait_ge(vector_set, 2)
            dve.wait_ge(zeroed, 2)
            for e in range(2):
                dve.memset(VB[64 * e:64 * e + 64, :, :, :, 1, e, :].rearrange("p a b k n -> p (a b k) n"), 1.0)
            dve.wait_ge(w_in.loaded, w_in.loads)
            dve.tensor_scalar(gbo[:, :], w_in.bo[:, :], sh.tanh_g[:, 2:3], None, ALU.mult).then_inc(gbo_ready, 1)

            def normalize(t, u):
                if not (isinstance(t, int) and t < 2):
                    dve.wait_ge(turned, t - 1)
                dve.tensor_scalar(xn[:, u, :], sh.x[:, t, :], sh.rstd[:, bass.ds(t, 1)], sh.nmr[:, bass.ds(t, 1)],
                                  ALU.mult, ALU.add).then_inc(xn_ready, 1)

            def body(it, a, live, past):
                o = 1 - a
                if live(0):
                    dve.wait_ge(x_turned, it + 1)
                    dve.tensor_copy(xT[:, :, :], pX[:, :, :]).then_inc(xT_copied, 1)
                if live(-1):
                    dve.wait_ge(max_turned, it)
                    dve.tensor_copy(nmaxT[0:32, :], pM[0][0:32, 0:2, :].rearrange("p a b -> p (a b)")).then_inc(max_copied, 1)
                if live(-2):
                    for b in range(BPT):
                        dve.wait_ge(y_copied[b], it - 1)
                    dve.reciprocal(rec[:, :, :, :], den[:, :, :, :]).then_inc(inverted, 1)
                if live(0):
                    dve.wait_ge(k_copied, it + 1)
                    for b in range(BPT):
                        rows = slice(64 * b, 64 * b + 64)
                        for e in range(2):
                            dst = VB[64 * e:64 * e + 64, a, b, :, 0, e, :]
                            src = pC[rows, 1, :].rearrange("p (k e n) -> p k e n", k=KP, e=2)[:, :, e, :]
                            bias = bv[rows, :].rearrange("p (k e n) -> p k e n", k=KP, e=2)[:, :, e, :]
                            v = dve.tensor_tensor(dst, src, bias, ALU.add)
                    v.then_inc(v_spread, 1)
                if live(0):
                    for q in range(KP):
                        rows = slice(32 * q, 32 * q + 32)
                        src = KT[rows, :, :].rearrange("p b (e s) -> p b e s", e=1).broadcast_to([32, BPT, 2, S])
                        keep = sh.odd[rows, :].rearrange("p (b e s) -> p b e s", b=1, s=1).broadcast_to([32, BPT, 2, S])
                        k = dve.tensor_tensor(KB[rows, a, :, q, :, :], src, keep, ALU.mult)
                    k.then_inc(k_spread, 1)
                if live(-2):
                    dve.wait_ge(inverted, it - 1)
                    if past(-2, 1):
                        dve.wait_ge(out_done, it - 2)
                    dve.tensor_tensor(yT[:, :, :, :].rearrange("p g b s -> p b g s"), yraw[:, :, :, :], rec[:, :, :, :], ALU.mult).then_inc(normed, 1)
                if live(1):
                    normalize(it + 1, o)
                if live(0):
                    dve.wait_ge(k_spread, it + 1)
                    dve.tensor_copy(KR[:, :, :, :, :].rearrange("p b k e s -> p (b k e s)"),
                                    KB[:, a, :, :, :, :].rearrange("p b k e s -> p (b k e s)")).then_inc(k_rounded, 1)
                    dve.wait_ge(q_copied, it + 1)
                    dve.tensor_copy(QR[:, :, :, :].rearrange("p b g s -> p (b g s)"),
                                    QT[:, a, :, :, :].rearrange("p b g s -> p (b g s)")).then_inc(q_rounded, 1)
                for b in range(BPT):
                    if live(0):
                        for gp in range(2):
                            dve.wait_ge(scored, 4 * it + 2 * b + gp + 1)
                            dve.tensor_reduce(nmax[:, b, gp, :], pM[gp][:, :, :], AX.X, ALU.max, negate=True).then_inc(maxed, 1)
                    if b == 0 and live(-2):
                        t = it - 2
                        dve.wait_ge(out_done, t + 1)
                        dve.wait_ge(biased, t + 1)
                        dve.scalar_tensor_tensor(sh.x[:, t, :], pC[:, :, :].rearrange("p a b -> p (a b)"), sh.tanh_g[:, 2:3],
                                                 sh.x[:, t, :], ALU.mult, ALU.add).then_inc(added, 1)
            normalize(0, 0)
            over_tiles(dve, body, 0, 2)


C, CODES, SUB = 32, 32, 16
NCL = 32
CLS = D // NCL
CG = P // CODES
NU = C // CG
VAR_STEPS = 5


class SecondFfnWeights:

    def __init__(self, nc, c):
        sb = lambda n, s, dt=F32: c.enter_context(nc.sbuf_tensor("f1_" + n, s, dt))
        self.books = sb("books_in", [P, NU, SUB])
        self.codes, self.cents = sb("codes", [P, NU, D], I32), sb("cents", [P, NU, NCL], I32)
        self.bias, self.lnw = sb("bias", [P, D]), sb("lnw", [P, NCL])
        self.loaded = c.enter_context(nc.semaphore("f1_w_loaded"))
        self.loads = 16 * (1 + 2 * CG + 2)

    def load(self, sp, io):
        sp.dma_start(self.books[:, :, :], io["L1_ffn_codebooks"].rearrange("(u c) k s -> (c k) u s", c=CG)).then_inc(self.loaded, 16)
        cents_in = io["L1_ffn_centroids"].rearrange("(u c a) n -> c a u n", c=CG, a=1)
        codes_in = io["L1_ffn_codes"].rearrange("(u c a) n -> c a u n", c=CG, a=1)
        for q in range(CG):
            rows = slice(q * CODES, (q + 1) * CODES)
            sp.dma_start(self.cents[rows, :, :], cents_in[q].broadcast_to([CODES, NU, NCL])).then_inc(self.loaded, 16)
            sp.dma_start(self.codes[rows, :, :], codes_in[q].broadcast_to([CODES, NU, D])).then_inc(self.loaded, 16)
        sp.dma_start(self.bias[:, :], io["L1_ffn_bias"].rearrange("(a n) -> a n", a=1).broadcast_to([P, D])).then_inc(self.loaded, 16)
        sp.dma_start(self.lnw[:, :], io["L1_ffn_ln_weight"].rearrange("(a n) -> a n", a=1).broadcast_to([P, NCL])).then_inc(self.loaded, 16)


def second_ffn(nc, io, out, sh, w_in):
    with ExitStack() as c:
        sb = lambda n, s, dt=F32: c.enter_context(nc.sbuf_tensor("f1_" + n, s, dt))
        pb = lambda n, s, dt=F32: c.enter_context(nc.psum_tensor("f1_" + n, s, dt))
        sem = lambda n: c.enter_context(nc.semaphore("f1_" + n))
        books_in, codes, cents, bias, lnw = w_in.books, w_in.codes, w_in.cents, w_in.bias, w_in.lnw
        books = sb("books", [P, NU, CG * SUB])
        code_id, code_idf = sb("code_id", [P, 1], I32), sb("code_idf", [P, 1])
        hot = sb("hot", [P, 2, D])
        hotc = sb("hotc", [P, NU, NCL])
        WT, cT = sb("WT", [P, KD, D]), sb("cT", [P, KD, NCL])
        xn, xT = sb("xn", [P, 2, D]), sb("xT", [P, 2, KD, P])
        dots, cen, z = sb("dots", [P, N, NCL]), sb("cen", [P, N, NCL]), sb("z", [P, N, NCL])
        (mean, var, std, rs, rs2, top, total, kept, keep_t) = (sb(n, [P, N]) for n in ("mean", "var", "std", "rs", "rs2", "top", "total", "kept", "keep_t"))
        used, keep_c = sb("used", [P, NCL]), sb("keep_c", [P, NCL])
        part = sb("part", [P, 2, D])
        pW = [pb(f"pW{k}", [P, D]) for k in range(2)]
        pCW = pb("pCW", [P, KD, NCL])
        pX = [pb(f"pX{k}", [P, KD, P]) for k in range(2)]
        pDot = [pb(f"pDot{k}", [P, NCL]) for k in range(2)]
        zeroed, ids, ids_float, books_ready = sem("zeroed"), sem("ids"), sem("ids_float"), sem("books_ready")
        hot_ready, hotc_ready, expanded, w_copied, cents_expanded, cents_copied = (
            sem(n) for n in ("hot_ready", "hotc_ready", "expanded", "w_copied", "cents_expanded", "cents_copied"))
        xn_ready, turned, xT_copied, product, used_product = (
            [sem(f"{n}{w}") for w in range(2)] for n in ("xn_ready", "turned", "xT_copied", "product", "used_product"))
        step, std_ready, z_ready, exp_ready, used_ready, counted = (
            sem(n) for n in ("mask_step", "std_ready", "z_ready", "exp_ready", "used_ready", "counted"))
        masked, biased = sem("masked"), sem("biased")
        stored = sem("stored")
        block = c.enter_context(nc.Block())
        x_out = out.rearrange("(i b) s d -> (b s) i d", b=BPT)

        @block.sync
        def _(sp):
            def body(it, b, live, past):
                if live(0):
                    sp.wait_ge(used_product[1], it + 1)
                    sp.dma_start(x_out[:, bass.ds(it, 1), :].rearrange("p a d -> p (a d)"), sh.x[:, it, :]).then_inc(stored, 16)
            over_tiles(sp, body, 0, 0)
            sp.wait_ge(stored, 16 * N)

        @block.gpsimd
        def _(pool):
            pool.memset(books[:, :, :], 0.0).then_inc(zeroed, 1)
            for q in range(CG):
                pool.iota(code_id[q * CODES:(q + 1) * CODES, :], pattern=[[0, 1]], base=0, channel_multiplier=1).then_inc(ids, 1)
                pool.wait_ge(ids, q + 1)

        @block.tensor
        def _(pe):
            pe.wait_ge(books_ready, 1)
            pe.wait_ge(hotc_ready, 1)
            for u in range(NU):
                mm = pe.matmul(pCW[64 * (u % 2):64 * (u % 2) + 64, u // 2, :], books[:, u, :], hotc[:, u, :], start=True, stop=True)
            mm.then_inc(cents_expanded, 1)
            for u in range(NU):
                pe.wait_ge(hot_ready, u + 1)
                if u >= 4 and u % 2 == 0:
                    pe.wait_ge(w_copied, u // 2 - 1)
                pe.matmul(pW[u // 2 % 2][64 * (u % 2):64 * (u % 2) + 64, :], books[:, u, :], hot[:, u % 2, :], start=True, stop=True).then_inc(expanded, 1)
            pe.wait_ge(cents_copied, 1)

            def tiles(w, dst, weights):
                def body(it, b, live, past):
                    if live(0):
                        pe.wait_ge(xn_ready[w], it + 1)
                        if past(0, 2):
                            pe.wait_ge(xT_copied[w], it - 1)
                        for k in range(KD):
                            mm = pe.transpose(pX[b][:, k, :], xn[:, b, k * P:(k + 1) * P], sh.ident[:, :])
                        mm.then_inc(turned[w], 1)
                    if live(-1):
                        o = 1 - b
                        pe.wait_ge(xT_copied[w], it)
                        if past(-1, 2):
                            pe.wait_ge(used_product[w], it - 2)
                        for k in range(KD):
                            mm = pe.matmul(dst[o][:, :], xT[:, o, k, :], weights[:, k, :], start=(k == 0), stop=(k == KD - 1))
                        mm.then_inc(product[w], 1)
                over_tiles(pe, body, 0, 1)

            tiles(0, pDot, cT)
            pe.wait_ge(used_ready, 1)
            pe.matmul(pCW[:, 0, :], sh.ones[:, :], used[:, :], start=True, stop=True).then_inc(counted, 1)
            pe.wait_ge(masked, 1)
            tiles(1, pW, WT)

        @block.scalar
        def _(act):
            def copies(w):
                def body(it, b, live, past):
                    if live(0):
                        act.wait_ge(turned[w], it + 1)
                        if past(0, 2):
                            act.wait_ge(product[w], it - 1)
                        act.activation(xT[:, b, :, :], pX[b][:, :, :], ACT.Copy).then_inc(xT_copied[w], 1)
                over_tiles(act, body, 0, 0)

            copies(0)
            act.wait_ge(step, VAR_STEPS)
            act.activation(std[:, :], var[:, :], ACT.Sqrt, bias=sh.eps[:, :], scale=1.0 / NCL).then_inc(std_ready, 1)
            act.wait_ge(z_ready, 1)
            act.activation(z[:, :, :], cen[:, :, :], ACT.Exp).then_inc(exp_ready, 1)
            copies(1)

        @block.vector
        def _(dve):
            dve.wait_ge(zeroed, 1)
            dve.wait_ge(w_in.loaded, w_in.loads)
            for q in range(CG):
                rows = slice(q * CODES, (q + 1) * CODES)
                i = dve.tensor_copy(books[rows, :, q * SUB:(q + 1) * SUB], books_in[rows, :, :])
            i.then_inc(books_ready, 1)
            dve.wait_ge(ids, CG)
            dve.tensor_copy(code_idf[:, :], code_id[:, :]).then_inc(ids_float, 1)
            dve.wait_ge(ids_float, 1)
            dve.tensor_scalar(hotc[:, :, :], cents[:, :, :], code_idf[:, :], None, ALU.is_equal).then_inc(hotc_ready, 1)
            for u in range(NU):
                if u >= 2:
                    dve.wait_ge(expanded, u - 1)
                dve.tensor_scalar(hot[:, u % 2, :], codes[:, u, :], code_idf[:, :], None, ALU.is_equal).then_inc(hot_ready, 1)
                if u == 2:
                    dve.wait_ge(cents_expanded, 1)
                    dve.tensor_copy(cT[:, :, :], pCW[:, :, :]).then_inc(cents_copied, 1)
                if u % 2 == 1 and u >= 3:
                    dve.wait_ge(expanded, u - 1)
                    k = u // 2 - 1
                    dve.tensor_copy(WT[:, k, :], pW[k % 2][:, :]).then_inc(w_copied, 1)
            dve.wait_ge(expanded, NU)
            dve.tensor_copy(WT[:, KD - 1, :], pW[(KD - 1) % 2][:, :]).then_inc(w_copied, 1)

            def normalize(w, t, u):
                if not (isinstance(t, int) and t < 2):
                    dve.wait_ge(turned[w], t - 1)
                dve.tensor_scalar(xn[:, u, :], sh.x[:, t, :], sh.rstd[:, bass.ds(t, 1)], sh.nmr[:, bass.ds(t, 1)],
                                  ALU.mult, ALU.add).then_inc(xn_ready[w], 1)

            def first(it, b, live, past):
                if live(1):
                    normalize(0, it + 1, 1 - b)
                if live(-1):
                    dve.wait_ge(product[0], it)
                    dve.tensor_copy(dots[:, it - 1, :], pDot[1 - b][:, :]).then_inc(used_product[0], 1)
            over_tiles(dve, first, 1, 1)

            st = Steps(dve, step, 0, 0)
            over = lambda a: a[:, :].rearrange("p (n a) -> p n a", a=1).broadcast_to([P, N, NCL])
            dve.wait_ge(used_product[0], N)
            st.done(dve.tensor_reduce(mean[:, :], dots[:, :, :], AX.X, ALU.add))
            st.done(dve.tensor_scalar(rs[:, :], mean[:, :], 1.0 / NCL, None, ALU.mult))
            st.done(dve.tensor_tensor(cen[:, :, :], dots[:, :, :], over(rs), ALU.subtract))
            st.done(dve.tensor_tensor(z[:, :, :], cen[:, :, :], cen[:, :, :], ALU.mult))
            st.done(dve.tensor_reduce(var[:, :], z[:, :, :], AX.X, ALU.add))
            assert st.n == VAR_STEPS
            dve.wait_ge(std_ready, 1)
            st.done(dve.reciprocal(rs[:, :], std[:, :]))
            st.mark(dve.tensor_scalar(std[:, :], var[:, :], 1.0 / NCL, EPS, ALU.mult, ALU.add))
            st.done(dve.tensor_tensor(rs2[:, :], rs[:, :], rs[:, :], ALU.mult))
            st.done(dve.tensor_tensor(mean[:, :], std[:, :], rs2[:, :], ALU.mult))
            st.done(dve.tensor_scalar(rs2[:, :], mean[:, :], -0.5, 1.5, ALU.mult, ALU.add))
            st.done(dve.tensor_tensor(mean[:, :], rs[:, :], rs2[:, :], ALU.mult))
            st.done(dve.tensor_tensor(z[:, :, :], cen[:, :, :], over(mean), ALU.mult))
            st.done(dve.tensor_tensor(dots[:, :, :], z[:, :, :],
                                      lnw[:, :].rearrange("p (a c) -> p a c", a=1).broadcast_to([P, N, NCL]), ALU.mult))
            st.done(dve.tensor_reduce(top[:, :], dots[:, :, :], AX.X, ALU.max))
            dve.tensor_tensor(cen[:, :, :], dots[:, :, :], over(top), ALU.subtract).then_inc(z_ready, 1)
            dve.wait_ge(exp_ready, 1)
            st.done(dve.tensor_reduce(total[:, :], z[:, :, :], AX.X, ALU.add))
            st.done(dve.tensor_scalar(rs[:, :], total[:, :], 0.5, None, ALU.mult))
            st.done(dve.tensor_tensor(dots[:, :, :], z[:, :, :], over(rs), ALU.is_gt))
            st.done(dve.tensor_reduce(kept[:, :], dots[:, :, :], AX.X, ALU.max))
            dve.tensor_reduce(used[:, :], dots[:, :, :].rearrange("p n c -> p c n"), AX.X, ALU.max).then_inc(used_ready, 1)
            st.done(dve.tensor_scalar(keep_t[:, :], kept[:, :], sh.tanh_g[:, 3:4], None, ALU.mult))
            dve.wait_ge(counted, 1)
            st.done(dve.tensor_scalar(keep_c[:, :], pCW[:, 0, :], 0.5, None, ALU.is_gt))
            columns = keep_c[:, :].rearrange("p (c a) -> p c a", a=1).broadcast_to([P, NCL, CLS])
            dve.wait_ge(w_copied, KD)
            for k in range(KD):
                w = WT[:, k, :].rearrange("p (c a) -> p c a", c=NCL)
                dve.tensor_tensor(w, w, columns, ALU.mult)
            bm = bias[:, :].rearrange("p (c a) -> p c a", c=NCL)
            dve.tensor_tensor(bm, bm, columns, ALU.mult).then_inc(masked, 1)
            dve.wait_ge(masked, 1)

            def second(it, b, live, past):
                if live(1):
                    normalize(1, it + 1, 1 - b)
                if live(-1):
                    t, o = it - 1, 1 - b
                    keep = keep_t[:, bass.ds(t, 1)]
                    dve.scalar_tensor_tensor(part[:, o, :], bias[:, :], keep, sh.x[:, t, :], ALU.mult, ALU.add).then_inc(biased, 1)
                    dve.wait_ge(biased, it)
                    dve.wait_ge(product[1], it)
                    dve.scalar_tensor_tensor(sh.x[:, t, :], pW[o][:, :], keep, part[:, o, :], ALU.mult, ALU.add).then_inc(used_product[1], 1)
            over_tiles(dve, second, 1, 1)


class Shared:
    pass


def load_now(nc, io, w):
    with nc.Block() as block:
        @block.sync
        def _(sp):
            w.load(sp, io)


def flamingo(nc, io, out, phases="SABCD"):
    sh = Shared()
    with ExitStack() as c:
        sb = lambda n, s, dt=F32: c.enter_context(nc.sbuf_tensor(n, s, dt))
        sh.x = sb("x", [P, N, D])
        sh.ident, sh.identb, sh.ones = sb("ident", [P, P]), sb("identb", [P, P], BF16), sb("ones", [P, P])
        sh.odd = sb("odd", [P, 2])
        sh.tanh_g, sh.scales = sb("tanh_g", [P, 4]), sb("scales", [P, 3])
        sh.wmean, sh.wscale = sb("wmean", [P, 3]), sb("wscale", [P, 3])
        sh.eps, sh.round = sb("eps", [P, 1]), sb("round", [P, 1])
        sh.rstd, sh.nmr = sb("rstd_all", [P, N]), sb("nmr_all", [P, N])
        sh.gateT, sh.upT = sb("gateT", [P, KD, FF], BF16), sb("upT", [P, KD, FF], BF16)
        sh.downT = sb("downT", [P, FJ, D], BF16)
        x_loaded = [c.enter_context(nc.semaphore(f"x_loaded{k}")) for k in range(N // XT)]
        consts_set = c.enter_context(nc.semaphore("consts_set"))
        a0 = FirstAttentionConstants(nc, c)
        with ExitStack() as raw_stack:
            raw = FirstFfnRaw(nc, raw_stack)
            with nc.Block() as block:
                @block.vector
                def _(dve):
                    dve.memset(a0.wnat[:, :, :], 0.0).then_inc(a0.zeroed, 1)
                    dve.memset(sh.eps[:, :], EPS).then_inc(consts_set, 1)
                    dve.memset(sh.round[:, :], ROUND).then_inc(consts_set, 1)
                    dve.wait_ge(consts_set, 2)

            def loads(sp):
                x_in = io["x"].rearrange("(n i b) s d -> n (b s) i d", b=BPT, i=XT)
                for n in range(N // XT):
                    sp.dma_start(sh.x[:, n * XT:(n + 1) * XT, :], x_in[n]).then_inc(x_loaded[n], 16)
                raw.load(sp, io)
                a0.load(sp, io)

            layer_norms(nc, sh, "n0_", loads, x_loaded)
            setup(nc, io, sh, raw, a0)
        if "A" in phases:
            first_attention(nc, io, sh, a0)
        w1, w2 = SecondAttentionWeights(nc, c), SecondFfnWeights(nc, c)
        if "B" in phases:
            first_ffn(nc, io, sh, w1)
        elif "C" in phases:
            load_now(nc, io, w1)
        if "C" in phases:
            layer_norms(nc, sh, "n2_")
            second_attention(nc, io, sh, w1, w2)
        elif "D" in phases:
            load_now(nc, io, w2)
        if "D" in phases:
            layer_norms(nc, sh, "n3_")
            second_ffn(nc, io, out, sh, w2)
        else:
            stored = c.enter_context(nc.semaphore("stored"))
            with nc.Block() as block:
                @block.sync
                def _(sp):
                    x_out = out.rearrange("(i b) s d -> i (b s) d", b=BPT)
                    for i in range(N):
                        sp.dma_start(x_out[i], sh.x[:, i, :]).then_inc(stored, 16)
                    sp.wait_ge(stored, 16 * N)


def kernel(**inputs):
    import numpy as _np
    import concourse.bacc as _bacc
    from concourse import mybir as _mybir
    from concourse.bass_utils import run_bass_kernel_spmd as _run

    nc = _bacc.Bacc("TRN2", target_bir_lowering=False, num_devices=1)
    arrays, io = {}, {}
    for name, value in inputs.items():
        a = _np.ascontiguousarray(value)
        arrays[f"in_{name}"] = a
        io[name] = nc.dram_tensor(f"in_{name}", a.shape, _mybir.dt.from_np(a.dtype), kind="ExternalInput").ap()
    out = nc.dram_tensor("out_0", (B, S, D), F32, kind="ExternalOutput").ap()
    flamingo(nc, io, out)
    r = _run(nc, [arrays], core_ids=[0])
    return r.results[0]["out_0"]
```

```python
import concourse.bass as bass
from concourse import mybir
from contextlib import ExitStack

F32 = mybir.dt.float32
F32R = mybir.dt.float32r
BF16 = mybir.dt.bfloat16
I32 = mybir.dt.int32
ALU = mybir.AluOpType
ACT = mybir.ActivationFunctionType
AX = mybir.AxisListType

P = 128
B, S, D = 32, 64, 512
N = B * S // P
BPT = P // S
KD = D // P
EPS = 1e-5
ROUND = 1.5 * 2.0 ** 23

FF = 1376
FJ = (FF + P - 1) // P
FR = FF - (FJ - 1) * P
NCH = 4
FC = FF // NCH
SQRT7 = 7.0 ** 0.5


class Steps:

    def __init__(self, eng, sem, tile, per):
        self.eng, self.sem, self.base, self.n = eng, sem, tile * per, 0

    def mark(self, ins):
        ins.then_inc(self.sem, 1)
        self.n += 1

    def done(self, ins):
        self.mark(ins)
        self.eng.wait_ge(self.sem, self.base + self.n)


def over_tiles(eng, body, ahead, behind, reach=1):
    def peeled(first, last):
        for it in range(first, last):
            body(it, it % 2, lambda k, it=it: 0 <= it + k < N, lambda k, n, it=it: it + k >= n)

    steady = lambda *_: True
    lo, hi = 4, N - 2 * reach
    peeled(-ahead, lo)
    with eng.Fori(lo, hi, 2) as it:
        body(it, 0, steady, steady)
        body(it + 1, 1, steady, steady)
    peeled(hi, N + behind)


class FirstFfnRaw:

    def __init__(self, nc, c):
        sb = lambda n, s, dt=F32: c.enter_context(nc.sbuf_tensor("w0_" + n, s, dt))
        self.gate, self.up, self.down = sb("raw_gate", [P, FJ, D]), sb("raw_up", [P, FJ, D]), sb("raw_down", [P, KD, FF])
        self.loaded = [c.enter_context(nc.semaphore(f"w0_raw_loaded{w}")) for w in range(3)]
        self.loads = (32, 32, 16)

    def load(self, sp, io):
        for w, (dst, name) in enumerate(((self.gate, "L0_ffn_w_gate"), (self.up, "L0_ffn_w_up"))):
            src = io[name]
            sp.dma_start(dst[:, 0:FJ - 1, :], src[0:(FJ - 1) * P, :].rearrange("(j p) k -> p j k", p=P)).then_inc(self.loaded[w], 16)
            sp.dma_start(dst[0:FR, FJ - 1, :], src[(FJ - 1) * P:FF, :]).then_inc(self.loaded[w], 16)
        sp.dma_start(self.down[:, :, :], io["L0_ffn_w_down"].rearrange("(o p) f -> p o f", p=P)).then_inc(self.loaded[2], 16)


def setup(nc, io, sh, rw, a0):
    with ExitStack() as c:
        sb = lambda n, s, dt=F32: c.enter_context(nc.sbuf_tensor("w0_" + n, s, dt))
        sem = lambda n: c.enter_context(nc.semaphore("w0_" + n))
        raw = [r[:, :, :].rearrange("p a b -> p (a b)") for r in (rw.gate, rw.up, rw.down)]
        low = sb("low", [P, FJ * D], BF16)
        trash = sb("trash", [P, FJ * D], BF16)
        tern = [sb(f"tern{w}", [P, FJ * D], BF16) for w in range(3)]
        sums, tot, thr = sb("sums", [P, 3, 2]), sb("tot", [P, 3]), sb("thr", [P, 3, 2])
        down = sb("down", [P, 1])
        gates_in = sb("gates_in", [P, 4])
        pT = [c.enter_context(nc.psum_tensor(f"pT{k}", [P, 4, P], BF16)) for k in range(4)]
        pS = [c.enter_context(nc.psum_tensor(f"pS{w}", [P, 2], F32)) for w in range(3)]
        small_loaded, zeroed, constants, identities = sem("small_loaded"), sem("zeroed"), sem("constants"), sem("identities")
        abs_summed, totals, step, ternary = sem("abs_summed"), sem("totals"), sem("vector_step"), sem("ternary")
        transposed, copied_act, copied_dve, gates = sem("transposed"), sem("copied_act"), sem("copied_dve"), sem("gates")
        odd_set = sem("odd_set")
        block = c.enter_context(nc.Block())

        whole = [(P, 0, (FJ - 1) * D), (FR, (FJ - 1) * D, D)]
        parts = [whole, whole, [(P, 0, KD * FF)]]
        groups = []
        for j in range(FJ):
            n = P if j < FJ - 1 else FR
            groups.append((0, [j * D + k * P for k in range(KD)], n, P, sh.gateT[:, :, j * P:j * P + n]))
        for j in range(FJ):
            n = P if j < FJ - 1 else FR
            groups.append((1, [j * D + k * P for k in range(KD)], n, P, sh.upT[:, :, j * P:j * P + n]))
        for j in range(FJ):
            n = P if j < FJ - 1 else FR
            groups.append((2, [o * FF + j * P for o in range(KD)], P, n,
                           sh.downT[0:n, j, :].rearrange("p (o n) -> p o n", n=P)))

        @block.gpsimd
        def _(pool):
            pool.memset(sh.ident[:, :], 0.0).then_inc(zeroed, 1)
            pool.memset(sh.identb[:, :], 0.0).then_inc(zeroed, 1)
            pool.memset(sh.ones[:, :], 1.0).then_inc(constants, 1)
            pool.memset(sums[:, :, :], 0.0).then_inc(constants, 1)
            for n, (g, k) in enumerate((("g_xattn", 0), ("g_ffn", 0), ("g_xattn", 1), ("g_ffn", 1))):
                pool.dma_start(gates_in[:, n:n + 1], io[g][k:k + 1].rearrange("(a n) -> a n", a=1).broadcast_to([P, 1])).then_inc(small_loaded, 16)
            for n, g in enumerate(("L0_ffn_s_gate", "L0_ffn_s_up", "L0_ffn_s_down")):
                pool.dma_start(sh.scales[:, n:n + 1], io[g].rearrange("(a n) -> a n", a=1).broadcast_to([P, 1])).then_inc(small_loaded, 16)
            pool.wait_ge(zeroed, 2)
            pool.wait_ge(constants, 2)
            for q in range(4):
                rows = sh.odd[32 * q:32 * q + 32, :]
                pool.affine_select(out=rows[:, 0:1], in_=sh.ones[32 * q:32 * q + 32, 0:1], compare_op=ALU.is_ge, fill=0.0,
                                   base=15, pattern=[[0, 1]], channel_multiplier=-1).then_inc(odd_set, 1)
                pool.affine_select(out=rows[:, 1:2], in_=sh.ones[32 * q:32 * q + 32, 0:1], compare_op=ALU.is_ge, fill=0.0,
                                   base=-16, pattern=[[0, 1]], channel_multiplier=1).then_inc(odd_set, 1)
                pool.wait_ge(odd_set, 2 * q + 2)
            a0.build(pool)
            for m in (sh.ident, sh.identb):
                pool.affine_select(out=m[:, :], in_=m[:, :], compare_op=ALU.not_equal, fill=1.0, base=0,
                                   pattern=[[-1, P]], channel_multiplier=1).then_inc(identities, 1)

        on_vector = lambda g: g >= 2 * FJ and g % 2 == 1
        before = lambda g: sum(on_vector(h) == on_vector(g) for h in range(g + 1))

        @block.scalar
        def _(act):
            act.wait_ge(constants, 2)
            n = 0

            def abs_sums(w):
                nonlocal n
                act.wait_ge(rw.loaded[w], rw.loads[w])
                for k, (rows, at, cols) in enumerate(parts[w]):
                    if n:
                        act.wait_ge(abs_summed, n)
                    act.activation(trash[0:rows, at:at + cols], raw[w][0:rows, at:at + cols], ACT.Abs,
                                   accum_out=sums[0:rows, w, k:k + 1]).then_inc(abs_summed, 1)
                    n += 1

            def copies(w):
                for g in range(FJ * w, FJ * w + FJ):
                    if not on_vector(g):
                        _, at, rows, cols, dst = groups[g]
                        act.wait_ge(transposed, g + 1)
                        act.activation(dst, pT[g % 4][0:cols, :, 0:rows], ACT.Copy).then_inc(copied_act, 1)

            abs_sums(0)
            abs_sums(1)
            abs_sums(2)
            act.wait_ge(small_loaded, 16 * 7)
            act.activation(sh.tanh_g[:, :], gates_in[:, :], ACT.Tanh).then_inc(gates, 1)
            copies(0)
            copies(1)
            copies(2)

        @block.tensor
        def _(pe):
            pe.wait_ge(constants, 2)

            def total(w):
                pe.wait_ge(abs_summed, sum(len(p) for p in parts[:w + 1]))
                pe.matmul(pS[w][:, :], sh.ones[:, :], sums[:, w, :], start=True, stop=True).then_inc(totals, 1)

            total(0)
            total(1)
            pe.wait_ge(identities, 2)
            for g, (w, at, rows, cols, dst) in enumerate(groups):
                if g == FJ:
                    total(2)
                pe.wait_ge(ternary, w + 1)
                if g >= 4:
                    pe.wait_ge(copied_dve if on_vector(g - 4) else copied_act, before(g - 4))
                for k in range(KD):
                    mm = pe.transpose(pT[g % 4][0:cols, k, 0:rows], tern[w][0:rows, at[k]:at[k] + cols], sh.identb[0:rows, 0:rows])
                mm.then_inc(transposed, 1)

        @block.vector
        def _(dve):
            st = Steps(dve, step, 0, 0)
            for w in range(3):
                dve.wait_ge(totals, w + 1)
                mean, above, below = sh.wmean[:, w:w + 1], thr[:, w, 0:1], thr[:, w, 1:2]
                st.done(dve.tensor_reduce(tot[:, w:w + 1], pS[w][:, :], AX.X, ALU.add))
                st.done(dve.tensor_scalar(mean, tot[:, w:w + 1], 1.0 / (FF * D), None, ALU.mult))
                st.mark(dve.tensor_scalar(above, mean, EPS, 0.5, ALU.add, ALU.mult))
                st.done(dve.tensor_scalar(below, mean, EPS, -0.5, ALU.add, ALU.mult))
                for rows, at, cols in parts[w]:
                    here = slice(at, at + cols)
                    st.done(dve.tensor_scalar(low[0:rows, here], raw[w][0:rows, here], thr[0:rows, w, 1:2], None, ALU.is_lt))
                    st.done(dve.scalar_tensor_tensor(tern[w][0:rows, here], raw[w][0:rows, here], thr[0:rows, w, 0:1],
                                                     low[0:rows, here], ALU.is_gt, ALU.subtract))
                dve.sem_inc(ternary, 1)
            dve.wait_ge(gates, 1)
            st.done(dve.tensor_tensor(sh.wscale[:, :], sh.wmean[:, :], sh.scales[:, :], ALU.mult))
            st.done(dve.tensor_tensor(down[:, :], sh.wscale[:, 2:3], sh.tanh_g[:, 1:2], ALU.mult))
            st.done(dve.tensor_scalar(sh.wscale[:, 2:3], down[:, :], 1.0 / 127.0, None, ALU.mult))
            for g, (w, at, rows, cols, dst) in enumerate(groups):
                if on_vector(g):
                    dve.wait_ge(transposed, g + 1)
                    dve.tensor_copy(dst, pT[g % 4][0:cols, :, 0:rows]).then_inc(copied_dve, 1)


NH0, HD0, WIN = 8, 8, 16
LEFT = WIN // 2
Q4, R4 = 4, 4
TB = 32
NT = D // TB
NJ = NT + 1
W0 = TB + WIN
KPAD = NJ * TB
QPAD = D + W0
NGR = (NJ + 1) // 2
NEG = -1e30


class FirstAttentionConstants:
    NAMES = ("Wq", "Wk", "Wv", "Wo")

    def __init__(self, nc, c):
        sb = lambda n, s, dt=F32: c.enter_context(nc.sbuf_tensor("a0_" + n, s, dt))
        sem = lambda n: c.enter_context(nc.semaphore("a0_" + n))
        self.wnat, self.bias = sb("wnat", [P, 4, P]), sb("bias", [P, 4])
        self.win_s, self.win_k = sb("win_s", [P, W0], BF16), sb("win_k", [P, W0], BF16)
        self.rmask = sb("rmask", [P, R4])
        self.diag = sb("diag", [P, TB])
        self.zeroed, self.loaded, self.step = sem("zeroed"), sem("loaded"), sem("const_step")
        self.loads = 16 * (2 * 4 + 2 * 4)

    def load(self, eng, io):
        eng.wait_ge(self.zeroed, 1)
        for w, name in enumerate(self.NAMES):
            for b in range(BPT):
                rows = slice(S * b, S * b + S)
                eng.dma_start(self.wnat[rows, w, rows], io["L0_xattn_" + name]).then_inc(self.loaded, 16)
                eng.dma_start(self.bias[rows, w:w + 1], io["L0_xattn_b" + name[1]].rearrange("(p a) -> p a", a=1)).then_inc(self.loaded, 16)

    def build(self, pool):
        st = Steps(pool, self.step, 0, 0)
        st.mark(pool.memset(self.win_s[:, :], 0.0))
        st.mark(pool.memset(self.win_k[:, :], 0.0))
        st.mark(pool.memset(self.rmask[:, :], 1.0))
        st.done(pool.memset(self.diag[:, :], 1.0))

        def keep(part, base, pattern, by, fill, op=ALU.is_ge):
            st.done(pool.affine_select(out=part, in_=part, compare_op=op, fill=fill, base=base, pattern=pattern, channel_multiplier=by))

        for n in range(Q4):
            rows = slice(TB * n, TB * n + TB)
            keep(self.win_s[rows, :], 0, [[1, W0]], -1, NEG)
            keep(self.win_s[rows, :], WIN - 1, [[-1, W0]], 1, NEG)
            keep(self.win_k[rows, :], -1, [[1, W0]], -1, NEG)
            keep(self.win_k[rows, :], WIN, [[-1, W0]], 1, NEG)
            keep(self.rmask[rows, :], 0, [[-HD0, R4]], 1, 0.0)
            keep(self.rmask[rows, :], HD0 - 1, [[HD0, R4]], -1, 0.0)
            keep(self.diag[rows, :], 0, [[-1, TB]], 1, 0.0, ALU.is_equal)


def first_attention(nc, io, sh, cs):
    with ExitStack() as c:
        sb = lambda n, s, dt=F32: c.enter_context(nc.sbuf_tensor("a0_" + n, s, dt))
        pb = lambda n, s, dt=F32: c.enter_context(nc.psum_tensor("a0_" + n, s, dt))
        sem = lambda n: c.enter_context(nc.semaphore("a0_" + n))
        wnat, bias, rmask, diag = cs.wnat, cs.bias, cs.rmask, cs.diag
        wsort, wT = sb("wsort", [P, P]), sb("wT", [P, 4, P])
        gbo = sb("gbo", [P, 1])
        mask_s, mask_k = sb("mask_s", [P, 2 * R4, W0], BF16), sb("mask_k", [P, 2 * R4, W0], BF16)
        quad, quadR = sb("quad", [P, P]), sb("quadR", [P, P], F32R)
        ctx, xn = sb("ctx", [P, 2, D]), sb("xn", [P, 2, D])
        q, k, v = sb("q", [P, D]), sb("k", [P, KPAD]), sb("v", [P, KPAD])
        QD = sb("QD", [P, NT, Q4, TB], F32R)
        KM = sb("KM", [P, R4, KPAD], F32R)
        KD = sb("KD", [P, 2, NJ, Q4, TB])
        QM = sb("QM", [P, 2, R4, QPAD])
        nmax = sb("nmax", [P, NT, R4])
        DM = sb("DM", [P, 2, R4, QPAD], F32R)
        vT = sb("vT", [P, NJ, R4, HD0])
        VM = sb("VM", [P, 2, NJ, R4, 2, Q4, HD0])
        E = sb("E", [P, 2, 2, R4, W0])
        den, rec, yraw, yn = sb("den", [P, D]), sb("rec", [P, D]), sb("yraw", [P, D]), sb("yn", [P, D])
        o = sb("o", [P, D])
        pA, pB = pb("pA", [P, D]), pb("pB", [P, D])
        pM = [pb(f"pM{n}", [P, 2, R4, W0]) for n in range(2)]
        pE = [pb(f"pE{n}", [P, 2, R4, W0]) for n in range(2)]
        pY = [pb(f"pY{n}", [P, D]) for n in range(2)]
        ones_set = sem("ones_set")
        pool_zeroed, cleared, quad_ready, w_sorted, w_turned, w_ready = (
            sem(n) for n in ("pool_zeroed", "cleared", "quad_ready", "w_sorted", "w_turned", "w_ready"))
        ctx_loaded = [sem(f"ctx_loaded{n}") for n in range(2)]
        xn_ready, q_done, k_done, v_done, q_copied, k_copied, v_copied = (
            sem(n) for n in ("xn_ready", "q_done", "k_done", "v_done", "q_copied", "k_copied", "v_copied"))
        QD_ready, KM_ready, QM_ready, KD_ready, vT_ready = (sem(n) for n in ("QD_ready", "KM_ready", "QM_ready", "KD_ready", "vT_ready"))
        scored, maxed, DM_ready = sem("scored"), sem("maxed"), sem("DM_ready")
        keyed, exped, weighed, spread = sem("keyed"), sem("exped"), sem("weighed"), sem("spread")
        y_copied, den_copied, inverted, normed, out_done, out_copied, added = (
            sem(n) for n in ("y_copied", "den_copied", "inverted", "normed", "out_done", "out_copied", "added"))
        block = c.enter_context(nc.Block())

        @block.sync
        def _(sp):
            c_in = io["ctx_4096"].rearrange("(i b) s d -> (b s) i d", b=BPT)

            def body(it, b, live, past):
                if live(1):
                    if past(1, 2):
                        sp.wait_ge(v_done, it)
                    sp.dma_start(ctx[:, 1 - b, :], c_in[:, bass.ds(it + 1, 1), :].rearrange("p a d -> p (a d)")).then_inc(ctx_loaded[1 - b], 32)
            over_tiles(sp, body, 1, 0)

        @block.gpsimd
        def _(pool):
            pool.memset(KD[:, :, :, :, :], 0.0).then_inc(pool_zeroed, 1)
            pool.memset(VM[:, :, :, :, 0, :, :], 0.0).then_inc(pool_zeroed, 1)
            pool.wait_ge(pool_zeroed, 2)

            def body(it, a, live, past):
                if live(0):
                    if past(0, 3):
                        pool.wait_ge(added, it - 2)
                    pool.wait_ge(k_copied, it + 1)
                    if past(0, 2):
                        pool.wait_ge(keyed, NGR * (it - 1))
                    for n in range(Q4):
                        rows = slice(TB * n, TB * n + TB)
                        src = k[rows, :].rearrange("p (j c) -> p j c", j=NJ)
                        ones = sh.ones[rows, 0:TB].rearrange("p (b c) -> p b c", b=1).broadcast_to([TB, NJ, TB])
                        pool.tensor_tensor(KD[rows, a, :, n, :], src, ones, ALU.mult).then_inc(KD_ready, 1)
                    pool.wait_ge(KD_ready, Q4 * (it + 1))
                    pool.wait_ge(vT_ready, it + 1)
                    if past(0, 2):
                        pool.wait_ge(weighed, NGR * (it - 1))
                    for n in range(Q4):
                        rows = slice(TB * n, TB * n + TB)
                        ones = sh.ones[rows, 0:HD0].rearrange("p (a b d) -> p a b d", a=1, b=1).broadcast_to([TB, NJ, R4, HD0])
                        pool.tensor_tensor(VM[rows, a, :, :, 0, n, :], vT[rows, :, :, :], ones, ALU.mult).then_inc(spread, 1)
                if live(-2):
                    t = it - 2
                    pool.wait_ge(out_copied, t + 1)
                    pool.wait_ge(spread, Q4 * (it + 1) if live(0) else Q4 * N)
                    xt = sh.x[:, t, :]
                    pool.tensor_tensor(xt, xt, o[:, :], ALU.add).then_inc(added, 1)
            over_tiles(pool, body, 0, 2)

        @block.tensor
        def _(pe):
            pe.wait_ge(cs.loaded, cs.loads)
            pe.wait_ge(w_sorted, 1)
            for w in range(4):
                mm = pe.transpose(pA[:, w * P:(w + 1) * P], wsort[:, :] if w == 3 else wnat[:, w, :], sh.ident[:, :])
            mm.then_inc(w_turned, 1)
            pe.wait_ge(w_ready, 1)

            def scores(t, a, g):
                n = NGR * t + g
                if g >= 2 or not (isinstance(t, int) and t == 0):
                    pe.wait_ge(exped, n - 1)
                blocks = 2 if g < NGR - 1 else 1
                cols = W0 if g < NGR - 1 else WIN
                for i in range(blocks):
                    j = 2 * g + i
                    pe.matmul(pE[g % 2][:, i, :, 0:cols], KD[:, a, j, :, :].rearrange("p n j -> p (n j)"),
                              QM[:, a, :, TB * j:TB * j + cols], start=(i == 0), stop=False, skip_group_check=True)
                    pe.matmul(pE[g % 2][:, i, :, 0:cols], quadR[:, :], DM[:, a, :, TB * j:TB * j + cols],
                              start=False, stop=False, skip_group_check=True)
                mask = mask_k[:, 0:blocks * R4, 0:cols].rearrange("p (i r) c -> p i r c", i=blocks)
                pe.matmul(pE[g % 2][:, 0:blocks, :, 0:cols], sh.identb[:, :], mask, start=False, stop=True,
                          skip_group_check=True).then_inc(keyed, 1)

            def weigh(t, a, g):
                n = NGR * t + g
                pe.wait_ge(exped, n + 1)
                if g == 0:
                    pe.wait_ge(spread, Q4 * (t + 1))
                    if isinstance(t, int) and t == 0:
                        pe.wait_ge(ones_set, 1)
                    else:
                        pe.wait_ge(y_copied, t)
                        pe.wait_ge(den_copied, t)
                for i in range(2 if g < NGR - 1 else 1):
                    j = 2 * g + i
                    lo, hi = max(0, TB * j - WIN), min(D, TB * j + TB)
                    at = lo - (TB * j - WIN)
                    for r in range(R4):
                        rows = slice(64 * (r % 2), 64 * (r % 2) + 64)
                        mm = pe.matmul(pY[r // 2][rows, lo:hi], VM[:, a, j, r, :, :, :].rearrange("p e n d -> p (e n d)"),
                                       E[:, g % 2, i, r, at:at + hi - lo], start=(j == 0), stop=(j == NJ - 1), skip_group_check=True)
                mm.then_inc(weighed, 1)

            def row_scores(it, m):
                n = NT // 2 * it + m
                if m >= 2 or not (isinstance(it, int) and it == 0):
                    pe.wait_ge(maxed, n - 1)
                for i in range(2):
                    t = 2 * m + i
                    pe.matmul(pM[m % 2][:, i, :, :], QD[:, t, :, :].rearrange("p n t -> p (n t)"),
                              KM[:, :, TB * t:TB * t + W0], start=(i == 0), stop=False, skip_group_check=True)
                pe.matmul(pM[m % 2][:, :, :, :].rearrange("p i r c -> p (i r c)"), sh.identb[:, :],
                          mask_s[:, :, :].rearrange("p a c -> p (a c)"), start=False, stop=True,
                          skip_group_check=True).then_inc(scored, 1)

            def body(it, a, live, past):
                s = 1 - a
                if live(0):
                    pe.wait_ge(xn_ready, it + 1)
                    if past(0, 1):
                        pe.wait_ge(v_copied, it)
                    pe.matmul(pA[:, :], wT[:, 0, :], xn[:, a, :], start=True, stop=True).then_inc(q_done, 1)
                    pe.wait_ge(ctx_loaded[a], 16 * (it - a) + 32)
                    if past(0, 3):
                        pe.wait_ge(out_copied, it - 2)
                    pe.matmul(pB[:, :], wT[:, 1, :], ctx[:, a, :], start=True, stop=True).then_inc(k_done, 1)
                if live(-1):
                    pe.wait_ge(DM_ready, 2 * it - 1)
                    pe.wait_ge(QM_ready, it)
                    pe.wait_ge(KD_ready, Q4 * it)
                    scores(it - 1, s, 0)
                if live(0):
                    pe.wait_ge(q_copied, it + 1)
                    pe.matmul(pA[:, :], wT[:, 2, :], ctx[:, a, :], start=True, stop=True).then_inc(v_done, 1)
                if live(-1):
                    scores(it - 1, s, 1)
                    weigh(it - 1, s, 0)
                for g in range(2, NGR + 1):
                    if live(-1):
                        if g == 4:
                            pe.wait_ge(DM_ready, 2 * it)
                        if g < NGR:
                            scores(it - 1, s, g)
                        weigh(it - 1, s, g - 1)
                    if 5 <= g < 9 and live(0):
                        if g == 5:
                            if not past(0, 1):
                                pe.wait_ge(quad_ready, 1)
                            pe.wait_ge(QD_ready, it + 1)
                            pe.wait_ge(KM_ready, it + 1)
                        row_scores(it, 2 * (g - 5))
                        row_scores(it, 2 * (g - 5) + 1)
                    if g == 6 and live(-2):
                        pe.wait_ge(normed, it - 1)
                        if live(0):
                            pe.wait_ge(k_copied, it + 1)
                        pe.matmul(pB[:, :], wT[:, 3, :], yn[:, :], start=True, stop=True).then_inc(out_done, 1)
            over_tiles(pe, body, 0, 2)

        @block.scalar
        def _(act):
            act.wait_ge(cs.loaded, cs.loads)
            act.wait_ge(w_turned, 1)
            act.activation(wT[:, :, :].rearrange("p w n -> p (w n)"), pA[:, :], ACT.Copy).then_inc(w_ready, 1)

            def exp(t, g):
                n = NGR * t + g
                act.wait_ge(keyed, n + 1)
                if g >= 2 or not (isinstance(t, int) and t == 0):
                    act.wait_ge(weighed, n - 1)
                blocks = 2 if g < NGR - 1 else 1
                cols = W0 if g < NGR - 1 else WIN
                act.activation(E[:, g % 2, 0:blocks, :, 0:cols], pE[g % 2][:, 0:blocks, :, 0:cols], ACT.Exp,
                               scale=HD0 ** -0.5).then_inc(exped, 1)

            def body(it, a, live, past):
                if live(-2):
                    t = it - 2
                    act.wait_ge(weighed, NGR * (t + 1))
                    if past(-2, 1):
                        act.wait_ge(normed, t)
                    for r in range(R4):
                        mine, at = slice(TB * r, TB * r + TB), 64 * (r % 2)
                        i = act.activation(yraw[mine, :], pY[r // 2][at:at + TB, :], ACT.Copy)
                    i.then_inc(y_copied, 1)
                if live(0):
                    act.wait_ge(q_done, it + 1)
                    if past(0, 1):
                        act.wait_ge(QM_ready, it)
                    act.activation(q[:, :], pA[:, :], ACT.Identity, bias=bias[:, 0:1]).then_inc(q_copied, 1)
                    act.wait_ge(k_done, it + 1)
                    if past(0, 1):
                        act.wait_ge(KD_ready, Q4 * it)
                        act.wait_ge(KM_ready, it)
                    act.activation(k[:, LEFT:LEFT + D], pB[:, :], ACT.Identity, bias=bias[:, 1:2]).then_inc(k_copied, 1)
                if live(-1):
                    exp(it - 1, 0)
                    exp(it - 1, 1)
                if live(0):
                    act.wait_ge(v_done, it + 1)
                    if past(0, 1):
                        act.wait_ge(vT_ready, it)
                    act.activation(v[:, LEFT:LEFT + D], pA[:, :], ACT.Identity, bias=bias[:, 2:3]).then_inc(v_copied, 1)
                if live(-1):
                    exp(it - 1, 2)
                if live(0):
                    if past(0, 1):
                        act.wait_ge(scored, NT // 2 * it)
                    if not past(0, 1):
                        act.wait_ge(quad_ready, 1)
                    act.wait_ge(q_copied, it + 1)
                    for n in range(Q4):
                        rows = slice(TB * n, TB * n + TB)
                        i = act.activation(QD[rows, :, n, :], q[rows, :].rearrange("p (t c) -> p t c", t=NT), ACT.Copy)
                    i.then_inc(QD_ready, 1)
                for g in range(3, NGR):
                    if live(-1):
                        exp(it - 1, g)
                    if g == 7 and live(-2):
                        t = it - 2
                        act.wait_ge(out_done, t + 1)
                        if past(-2, 1):
                            act.wait_ge(added, t)
                        act.activation(o[:, :], pB[:, :], ACT.Identity, scale=sh.tanh_g[:, 0:1], bias=gbo[:, :]).then_inc(out_copied, 1)
            over_tiles(act, body, 0, 2)

        @block.vector
        def _(dve):
            def normalize(t, u):
                if not (isinstance(t, int) and t < 2):
                    dve.wait_ge(q_done, t - 1)
                dve.tensor_scalar(xn[:, u, :], sh.x[:, t, :], sh.rstd[:, bass.ds(t, 1)], sh.nmr[:, bass.ds(t, 1)],
                                  ALU.mult, ALU.add).then_inc(xn_ready, 1)

            st = Steps(dve, cleared, 0, 0)
            st.mark(dve.memset(wsort[:, :], 0.0))
            st.done(dve.memset(quad[:, :], 0.0))
            for n in range(Q4):
                i = dve.memset(quad[TB * n:TB * n + TB, TB * n:TB * n + TB], 1.0)
            st.mark(i)
            dve.wait_ge(cs.loaded, cs.loads)
            for b in range(BPT):
                rows = slice(S * b, S * b + S)
                for n in range(2):
                    src = wnat[rows, 3, S * b + TB * n:S * b + TB * n + TB].rearrange("p (r d) -> p r d", r=R4)
                    dst = wsort[rows, :].rearrange("p (r n d) -> p r n d", r=R4, n=Q4)[:, :, 2 * b + n, :]
                    dve.tensor_copy(dst, src)
            for tile in (k, v):
                dve.memset(tile[:, 0:LEFT], 0.0)
                dve.memset(tile[:, LEFT + D:], 0.0)
            dve.tensor_tensor(gbo[:, :], bias[:, 3:4], sh.tanh_g[:, 0:1], ALU.mult).then_inc(w_sorted, 1)
            normalize(0, 0)
            for tile in (QM[:, :, :, :], DM[:, :, :, :].bitcast(F32)):
                dve.memset(tile[:, :, :, 0:WIN], 0.0)
                dve.memset(tile[:, :, :, WIN + D:], 0.0)
            dve.memset(QD[:, :, :, :].bitcast(F32), 0.0)
            for mask, win in ((mask_s, cs.win_s), (mask_k, cs.win_k)):
                dve.tensor_copy(mask[:, :, :], win[:, :].rearrange("p (a c) -> p a c", a=1).broadcast_to([P, 2 * R4, W0]))
            dve.wait_ge(cleared, 3)
            st.done(dve.tensor_copy(quadR[:, :], quad[:, :]))
            dve.sem_inc(quad_ready, 1)

            def body(it, a, live, past):
                if live(-3):
                    dve.wait_ge(added, it - 2)
                if live(-2):
                    dve.wait_ge(weighed, NGR * (it - 1))
                    for r in range(R4):
                        at = 64 * (r % 2) + TB
                        i = dve.tensor_copy(den[TB * r:TB * r + TB, :], pY[r // 2][at:at + TB, :])
                    i.then_inc(den_copied, 1)
                if live(0):
                    dve.wait_ge(k_copied, it + 1)
                    if past(0, 1):
                        dve.wait_ge(scored, NT // 2 * it)
                    for r in range(R4):
                        i = dve.tensor_scalar(KM[:, r, :], k[:, :], rmask[:, r:r + 1], None, ALU.mult)
                    i.then_inc(KM_ready, 1)
                    dve.wait_ge(q_copied, it + 1)
                    if past(0, 2):
                        dve.wait_ge(keyed, NGR * (it - 1))
                    for r in range(R4):
                        i = dve.tensor_scalar(QM[:, a, r, WIN:WIN + D], q[:, :], rmask[:, r:r + 1], None, ALU.mult)
                    i.then_inc(QM_ready, 1)
                if live(1):
                    normalize(it + 1, 1 - a)
                if live(-3):
                    dve.bn_stats(sh.stats[:, it - 3, :], sh.x[:, it - 3, :])
                if live(-2):
                    t = it - 2
                    dve.wait_ge(den_copied, t + 1)
                    dve.reciprocal(rec[:, :], den[:, :]).then_inc(inverted, 1)
                if live(0):
                    dve.wait_ge(v_copied, it + 1)
                    if past(0, 1):
                        dve.wait_ge(spread, Q4 * it)
                    dve.transpose(vT[:, :, :, :].rearrange("p j r d -> p (j r d)"), v[:, :]).then_inc(vT_ready, 1)
                if live(-2):
                    dve.wait_ge(inverted, t + 1)
                    dve.wait_ge(y_copied, t + 1)
                    if past(-2, 1):
                        dve.wait_ge(out_done, t)
                    dve.tensor_tensor(yn[:, :], yraw[:, :], rec[:, :], ALU.mult).then_inc(normed, 1)
                if live(0):
                    for m in range(NT // 2):
                        dve.wait_ge(scored, NT // 2 * it + m + 1)
                        dve.tensor_reduce(nmax[:, 2 * m:2 * m + 2, :].rearrange("p i r -> p (i r)"),
                                          pM[m % 2][:, :, :, :].rearrange("p i r c -> p (i r) c"), AX.X, ALU.max, negate=True).then_inc(maxed, 1)
                        if m % (NT // 4) == NT // 4 - 1:
                            dve.wait_ge(maxed, NT // 2 * it + m + 1)
                            h = NT // 2
                            t0 = h * (m // (NT // 4))
                            shape = [P, R4, h, TB]
                            dve.tensor_tensor(DM[:, a, :, WIN + TB * t0:WIN + TB * (t0 + h)].rearrange("p r (t c) -> p r t c", t=h),
                                              nmax[:, t0:t0 + h, :].rearrange("p (t a) r -> p r t a", a=1).broadcast_to(shape),
                                              diag[:, :].rearrange("p (a b c) -> p a b c", a=1, b=1).broadcast_to(shape),
                                              ALU.mult).then_inc(DM_ready, 1)
                if live(0) and not past(0, 1):
                    own = quad[:, :].rearrange("p (a n c) -> p a n c", a=1, n=Q4)[:, :, :, 0:HD0]
                    dve.tensor_copy(VM[:, :, :, :, 1, :, :].rearrange("p a j r n d -> p (a j r) n d"),
                                    own.broadcast_to([P, 2 * NJ * R4, Q4, HD0])).then_inc(ones_set, 1)
            over_tiles(dve, body, 0, 3)


def first_ffn(nc, io, sh, next_weights):
    with ExitStack() as c:
        sb = lambda n, s, dt=F32: c.enter_context(nc.sbuf_tensor("f0_" + n, s, dt))
        pb = lambda n, s, dt=F32: c.enter_context(nc.psum_tensor("f0_" + n, s, dt))
        sem = lambda n: c.enter_context(nc.semaphore("f0_" + n))
        qa, qb, iscale, isize = (sb(n, [P, N]) for n in ("qa", "qb", "iscale", "isize"))
        sign = sb("sign", [P, 1])
        cmax, den, inv, hf = (sb(n, [P, 2]) for n in ("cmax", "den", "inv", "hf"))
        oscale = sb("oscale", [P, 2])
        xs, xc = sb("xs", [P, 2, D]), sb("xc", [P, 2, D])
        xq, xqT = sb("xq", [P, 2, D], BF16), sb("xqT", [P, 2, KD, P], BF16)
        r, r2 = sb("r", [P, 2, FC]), sb("r2", [P, 2, FC])
        inter, amax = sb("inter", [P, 2, FF]), sb("amax", [P, 2, NCH])
        hr, hq, hqT = sb("hr", [P, 2, FF]), sb("hq", [P, 2, FF], BF16), sb("hqT", [P, 2, FJ, P], BF16)
        int4_scales(nc, sh, qa, qb, iscale, isize, sign)

        pG, pU = [pb(f"pG{k}", [P, FC]) for k in range(2)], [pb(f"pU{k}", [P, FC]) for k in range(2)]
        pXT = pb("pXT", [P, KD, P], BF16)
        pHT, pHU = pb("pHT", [P, 8, P], BF16), pb("pHU", [P, FJ - 8, P], BF16)
        pD = pb("pD", [P, D])
        x_step, xT_done, xT_copied = sem("x_step"), sem("xT_done"), sem("xT_copied")
        chunk_done, relu_done, squared, multiplied, max_done = (
            sem(n) for n in ("chunk_done", "relu_done", "squared", "multiplied", "max_done"))
        factor_step, scaled, rounded = sem("factor_step"), sem("scaled"), sem("rounded")
        hT_done, hT_copied, hU_copied, down_done, added = (
            sem(n) for n in ("hT_done", "hT_copied", "hU_copied", "down_done", "added"))
        block = c.enter_context(nc.Block())
        FACTOR = 5

        @block.sync
        def _(sp):
            next_weights.load(sp, io)

        @block.tensor
        def _(pe):
            def transpose_x(t, u):
                pe.wait_ge(x_step, 3 * t + 3)
                if not (isinstance(t, int) and t == 0):
                    pe.wait_ge(xT_copied, t)
                for k in range(KD):
                    mm = pe.transpose(pXT[:, k, :], xq[:, u, k * P:(k + 1) * P], sh.identb[:, :])
                mm.then_inc(xT_done, 1)

            def body(it, b, live, past):
                o = 1 - b
                if live(0):
                    pe.wait_ge(xT_copied, it + 1)
                for ch in range(NCH):
                    if live(0):
                        u = ch % 2
                        if ch >= 2 or past(0, 1):
                            pe.wait_ge(multiplied, NCH * it + ch - 1)
                        for p, w in ((pG[u], sh.gateT), (pU[u], sh.upT)):
                            for k in range(KD):
                                mm = pe.matmul(p[:, :], xqT[:, b, k, :], w[:, k, ch * FC:(ch + 1) * FC], start=(k == 0), stop=(k == KD - 1))
                        mm.then_inc(chunk_done, 1)
                    if ch == 1 and live(-2):
                        pe.wait_ge(hT_copied, it - 1)
                        pe.wait_ge(hU_copied, it - 1)
                        if past(-2, 1):
                            pe.wait_ge(added, it - 2)
                        for j in range(FJ):
                            n = P if j < FJ - 1 else FR
                            mm = pe.matmul(pD[:, :], hqT[0:n, b, j, :], sh.downT[0:n, j, :], start=(j == 0), stop=(j == FJ - 1))
                        mm.then_inc(down_done, 1)
                    if ch == 1 and live(1):
                        transpose_x(it + 1, o)
                if live(-1):
                    pe.wait_ge(rounded, it)
                    for j in range(FJ):
                        n = P if j < FJ - 1 else FR
                        dst = pHT[0:n, j, :] if j < 8 else pHU[0:n, j - 8, :]
                        mm = pe.transpose(dst, hq[:, o, j * P:j * P + n], sh.identb[:, :])
                    mm.then_inc(hT_done, 1)
            transpose_x(0, 0)
            over_tiles(pe, body, 0, 2)

        @block.scalar
        def _(act):
            def copy_xT(t, u):
                act.wait_ge(xT_done, t + 1)
                if not (isinstance(t, int) and t < 2):
                    act.wait_ge(chunk_done, NCH * (t - 1))
                act.activation(xqT[:, u, :, :], pXT[:, :, :], ACT.Copy).then_inc(xT_copied, 1)

            def body(it, b, live, past):
                o = 1 - b
                for ch in range(NCH):
                    if live(0):
                        u, n = ch % 2, NCH * it + ch
                        act.wait_ge(chunk_done, n + 1)
                        act.activation(r[:, u, :], pG[u][:, :], ACT.Relu, scale=sign[:, :]).then_inc(relu_done, 1)
                        if ch >= 2 or past(0, 1):
                            act.wait_ge(multiplied, n - 1)
                        act.wait_ge(relu_done, n + 1)
                        act.activation(r2[:, u, :], r[:, u, :], ACT.Square).then_inc(squared, 1)
                    if ch == 1 and live(-1):
                        act.wait_ge(factor_step, FACTOR * it)
                        if past(-1, 2):
                            act.wait_ge(rounded, it - 2)
                        act.activation(hr[:, o, :], inter[:, o, :], ACT.Identity, bias=sh.round[:, :], scale=hf[:, o:o + 1]).then_inc(scaled, 1)
                    if ch == 2 and live(1):
                        copy_xT(it + 1, o)
                    if ch == 3 and live(-1):
                        act.wait_ge(hT_done, it)
                        if past(-1, 2):
                            act.wait_ge(down_done, it - 2)
                        act.activation(hqT[:, o, 0:8, :], pHT[:, :, :], ACT.Copy).then_inc(hT_copied, 1)
            copy_xT(0, 0)
            over_tiles(act, body, 0, 1)

        @block.vector
        def _(dve):
            def scale_x(t, u):
                dve.tensor_scalar(xs[:, u, :], sh.x[:, t, :], qa[:, bass.ds(t, 1)], qb[:, bass.ds(t, 1)], ALU.mult, ALU.add).then_inc(x_step, 1)

            def clip_x(t, u):
                dve.wait_ge(x_step, 3 * t + 1)
                dve.tensor_scalar(xc[:, u, :], xs[:, u, :], 7.0, -8.0, ALU.min, ALU.max).then_inc(x_step, 1)

            def round_x(t, u):
                dve.wait_ge(x_step, 3 * t + 2)
                if not (isinstance(t, int) and t < 2):
                    dve.wait_ge(xT_done, t - 1)
                dve.tensor_scalar(xq[:, u, :], xc[:, u, :], ROUND, ROUND, ALU.add, ALU.subtract).then_inc(x_step, 1)

            def body(it, b, live, past):
                o = 1 - b
                col = slice(o, o + 1)

                def multiply(ch):
                    if live(0):
                        dve.wait_ge(squared, NCH * it + ch + 1)
                        if ch == 0 and past(0, 2):
                            dve.wait_ge(scaled, it - 1)
                        dve.tensor_tensor(inter[:, b, ch * FC:(ch + 1) * FC], pU[ch % 2][:, :], r2[:, ch % 2, :],
                                          ALU.mult).then_inc(multiplied, 1)

                def largest(ch):
                    if live(0):
                        dve.wait_ge(multiplied, NCH * it + ch + 1)
                        dve.tensor_reduce(amax[:, b, ch:ch + 1], inter[:, b, ch * FC:(ch + 1) * FC], AX.X, ALU.max,
                                          apply_absolute_value=True).then_inc(max_done, 1)

                if live(-1):
                    size, scale = isize[:, bass.ds(it - 1, 1)], iscale[:, bass.ds(it - 1, 1)]
                    dve.wait_ge(max_done, NCH * it)
                    dve.tensor_reduce(cmax[:, col], amax[:, o, :], AX.X, ALU.max).then_inc(factor_step, 1)
                if live(2):
                    scale_x(it + 2, b)
                if live(-1):
                    if past(-1, 2):
                        dve.wait_ge(scaled, it - 2)
                        dve.wait_ge(added, it - 2)
                    dve.wait_ge(factor_step, FACTOR * (it - 1) + 1)
                    dve.tensor_scalar(den[:, col], cmax[:, col], size, EPS, ALU.mult, ALU.add).then_inc(factor_step, 1)
                    dve.tensor_scalar(oscale[:, col], cmax[:, col], size, sh.wscale[:, 2:3], ALU.mult, ALU.mult).then_inc(factor_step, 1)
                if live(2):
                    clip_x(it + 2, b)
                if live(-1):
                    dve.wait_ge(factor_step, FACTOR * (it - 1) + 3)
                    dve.reciprocal(inv[:, col], den[:, col]).then_inc(factor_step, 1)
                multiply(0)
                if live(-1):
                    dve.wait_ge(factor_step, FACTOR * (it - 1) + 4)
                    dve.tensor_scalar(hf[:, col], inv[:, col], scale, 127.0, ALU.mult, ALU.mult).then_inc(factor_step, 1)
                if live(2):
                    round_x(it + 2, b)
                if live(-3):
                    dve.wait_ge(added, it - 2)
                multiply(1)
                largest(0)
                if live(-3):
                    dve.bn_stats(sh.stats[:, it - 3, :], sh.x[:, it - 3, :])
                if live(-1):
                    dve.wait_ge(scaled, it)
                    if past(-1, 2):
                        dve.wait_ge(hT_done, it - 2)
                    dve.tensor_scalar(hq[:, o, :], hr[:, o, :], ROUND, None, ALU.subtract).then_inc(rounded, 1)
                multiply(2)
                largest(1)
                if live(-2):
                    dve.wait_ge(down_done, it - 1)
                    xt = sh.x[:, it - 2, :]
                    dve.scalar_tensor_tensor(xt, pD[:, :], oscale[:, b:b + 1], xt, ALU.mult, ALU.add).then_inc(added, 1)
                multiply(3)
                largest(2)
                if live(-1):
                    dve.wait_ge(hT_done, it)
                    dve.tensor_copy(hqT[:, o, 8:FJ - 1, :], pHU[:, 0:FJ - 9, :])
                    dve.tensor_copy(hqT[0:FR, o, FJ - 1, :], pHU[0:FR, FJ - 9, :]).then_inc(hU_copied, 1)
                largest(3)
            for t in range(2):
                scale_x(t, t)
                clip_x(t, t)
                round_x(t, t)
            over_tiles(dve, body, 0, 3, reach=2)


def int4_scales(nc, sh, qa, qb, iscale, isize, sign):
    with ExitStack() as c:
        sb = lambda n, s, dt=F32: c.enter_context(nc.sbuf_tensor("q0_" + n, s, dt))
        sem = lambda n: c.enter_context(nc.semaphore("q0_" + n))
        mv, nmean, asum = sb("mv", [P, N, 2]), sb("nmean", [P, N]), sb("asum", [P, N])
        centred = sb("centred", [P, 2, D])
        std, rstd, t1, t2, beta = (sb(n, [P, N]) for n in ("std", "rstd", "t1", "t2", "beta"))
        trash = sb("trash", [P, 2, D], BF16)
        ON_ACT = 5 * N // 8
        std_ready, abs_ready, centred_ready, summed, step = (
            sem(n) for n in ("std_ready", "abs_ready", "centred_ready", "summed", "step"))
        block = c.enter_context(nc.Block())

        @block.vector
        def _(dve):
            st = Steps(dve, step, 0, 0)
            for i in range(N):
                st.mark(dve.bn_aggr(mv[:, i, :], sh.stats[:, i, :]))
            dve.wait_ge(step, N)
            st.done(dve.tensor_scalar(nmean[:, :], mv[:, :, 0], -1.0, None, ALU.mult))
            for i in range(ON_ACT, N):
                n = i - ON_ACT
                if n >= 2:
                    dve.wait_ge(summed, n - 1)
                dve.tensor_scalar(centred[:, n % 2, :], sh.x[:, i, :], nmean[:, i:i + 1], None, ALU.add).then_inc(centred_ready, 1)
                if n >= 1:
                    dve.wait_ge(centred_ready, n)
                    dve.tensor_reduce(asum[:, i - 1:i], centred[:, (n - 1) % 2, :], AX.X, ALU.add, apply_absolute_value=True).then_inc(summed, 1)
            n = N - ON_ACT
            dve.wait_ge(centred_ready, n)
            dve.tensor_reduce(asum[:, N - 1:N], centred[:, (n - 1) % 2, :], AX.X, ALU.add, apply_absolute_value=True).then_inc(summed, 1)
            st.mark(dve.tensor_scalar(sign[:, :], sh.scales[:, 0:1], 0.0, None, ALU.is_ge))
            dve.wait_ge(std_ready, 1)
            st.done(dve.reciprocal(t1[:, :], std[:, :]))
            st.done(dve.tensor_scalar(sign[:, :], sign[:, :], 2.0, 1.0, ALU.mult, ALU.subtract))
            st.done(dve.tensor_tensor(t2[:, :], t1[:, :], t1[:, :], ALU.mult))
            st.done(dve.scalar_tensor_tensor(std[:, :], mv[:, :, 1], EPS, t2[:, :], ALU.add, ALU.mult))
            st.done(dve.tensor_scalar(t2[:, :], std[:, :], -0.5, 1.5, ALU.mult, ALU.add))
            st.done(dve.tensor_tensor(rstd[:, :], t1[:, :], t2[:, :], ALU.mult))
            dve.wait_ge(abs_ready, ON_ACT)
            dve.wait_ge(summed, N - ON_ACT)
            st.done(dve.scalar_tensor_tensor(beta[:, :], asum[:, :], 1.0 / D, rstd[:, :], ALU.mult, ALU.mult))
            st.done(dve.tensor_scalar(t1[:, :], beta[:, :], EPS, 1.0 / SQRT7, ALU.add, ALU.mult))
            st.done(dve.reciprocal(t2[:, :], t1[:, :]))
            st.done(dve.tensor_tensor(qa[:, :], rstd[:, :], t2[:, :], ALU.mult))
            st.mark(dve.tensor_tensor(qb[:, :], nmean[:, :], qa[:, :], ALU.mult))
            st.done(dve.tensor_scalar(t1[:, :], beta[:, :], sh.wscale[:, 0:1], None, ALU.mult))
            st.mark(dve.tensor_scalar(t2[:, :], beta[:, :], sh.wscale[:, 1:2], None, ALU.mult))
            st.done(dve.tensor_tensor(std[:, :], t1[:, :], t1[:, :], ALU.mult))
            st.done(dve.tensor_tensor(iscale[:, :], std[:, :], t2[:, :], ALU.mult))
            st.done(dve.scalar_tensor_tensor(isize[:, :], iscale[:, :], -1.0, iscale[:, :], ALU.mult, ALU.max))

        @block.scalar
        def _(act):
            act.wait_ge(step, N + 1)
            act.activation(std[:, :], mv[:, :, 1], ACT.Sqrt, bias=sh.eps[:, :]).then_inc(std_ready, 1)
            for i in range(ON_ACT):
                if i >= 2:
                    act.wait_ge(abs_ready, i - 1)
                act.activation(trash[:, i % 2, :], sh.x[:, i, :], ACT.Abs, bias=nmean[:, i:i + 1],
                               accum_out=asum[:, i:i + 1]).then_inc(abs_ready, 1)


XT = 4


def layer_norms(nc, sh, tag, sync=None, x_loaded=None):
    with ExitStack() as c:
        sb = lambda n, s, dt=F32: c.enter_context(nc.sbuf_tensor(tag + n, s, dt))
        sem = lambda n: c.enter_context(nc.semaphore(tag + n))
        mv, std, t1, t2 = sb("mv", [P, N, 2]), sb("std", [P, N]), sb("t1", [P, N]), sb("t2", [P, N])
        stat_ready = sem("stat_ready") if x_loaded else None
        std_ready, step = sem("std_ready"), sem("norm_step")
        block = c.enter_context(nc.Block())

        if sync:
            block.sync(sync)

        @block.vector
        def _(dve):
            def stat(i):
                if i % XT == 0:
                    dve.wait_ge(x_loaded[i // XT], 16)
                dve.bn_stats(sh.stats[:, i, :], sh.x[:, i, :]).then_inc(stat_ready, 1)

            def aggregate(i):
                if x_loaded:
                    dve.wait_ge(stat_ready, i + 1)
                dve.bn_aggr(mv[:, i, :], sh.stats[:, i, :]).then_inc(step, 1)

            if x_loaded:
                stat(0)
            for i in range(1, N):
                if x_loaded:
                    stat(i)
                aggregate(i - 1)
            aggregate(N - 1)
            st = Steps(dve, step, 0, 0)
            st.n = N
            dve.wait_ge(std_ready, 1)
            st.done(dve.reciprocal(t1[:, :], std[:, :]))
            st.done(dve.tensor_tensor(t2[:, :], t1[:, :], t1[:, :], ALU.mult))
            st.done(dve.scalar_tensor_tensor(std[:, :], mv[:, :, 1], EPS, t2[:, :], ALU.add, ALU.mult))
            st.done(dve.tensor_scalar(t2[:, :], std[:, :], -0.5, 1.5, ALU.mult, ALU.add))
            st.done(dve.tensor_tensor(sh.rstd[:, :], t1[:, :], t2[:, :], ALU.mult))
            st.done(dve.scalar_tensor_tensor(sh.nmr[:, :], mv[:, :, 0], -1.0, sh.rstd[:, :], ALU.mult, ALU.mult))

        @block.scalar
        def _(act):
            act.wait_ge(step, N)
            act.activation(std[:, :], mv[:, :, 1], ACT.Sqrt, bias=sh.eps[:, :]).then_inc(std_ready, 1)


NQ, NKV = 32, 8
HD = D // NQ
G = NQ // NKV
KP = NKV // 2


class SecondAttentionWeights:

    def __init__(self, nc, c):
        sb = lambda n, s, dt=F32: c.enter_context(nc.sbuf_tensor("a1_" + n, s, dt))
        self.wq, self.wk, self.wv = sb("wq_in", [P, KD, D]), sb("wk", [P, KD, P]), sb("wv", [P, KD, P])
        self.wo = sb("wo", [P, G, D])
        self.bq, self.bk, self.bv, self.bo = sb("bq", [P, G]), sb("bk", [P, 1]), sb("bv", [P, P]), sb("bo", [P, D])
        self.loaded = c.enter_context(nc.semaphore("a1_w_loaded"))
        self.loads = 16 * (3 + NKV + NKV * G + 3)
        self.ctx = sb("ctx", [P, 2, D])
        self.ctx_loaded = [c.enter_context(nc.semaphore(f"a1_ctx_loaded{k}")) for k in range(2)]

    def load(self, sp, io):
        sp.dma_start(self.ctx[:, 0, :], io["ctx_4096"][0:BPT].rearrange("b s d -> (b s) d")).then_inc(self.ctx_loaded[0], 32)
        for dst, name in ((self.wq, "Wq"), (self.wk, "Wk"), (self.wv, "Wv")):
            sp.dma_start(dst[:, :, :], io["L1_xattn_" + name].rearrange("(k p) n -> p k n", p=P)).then_inc(self.loaded, 16)
        wo_in = io["L1_xattn_Wo"].rearrange("(h g e) n -> h g e n", h=NKV, g=G)
        for h in range(NKV):
            sp.dma_start(self.wo[h * HD:(h + 1) * HD, :, :], wo_in[h].rearrange("g e n -> e g n")).then_inc(self.loaded, 16)
        bq_in = io["L1_xattn_bq"].rearrange("(h g e a) -> h g e a", h=NKV, g=G, a=1)
        for h in range(NKV):
            for g in range(G):
                sp.dma_start(self.bq[h * HD:(h + 1) * HD, g:g + 1], bq_in[h, g]).then_inc(self.loaded, 16)
        sp.dma_start(self.bk[:, :], io["L1_xattn_bk"].rearrange("(p a) -> p a", a=1)).then_inc(self.loaded, 16)
        sp.dma_start(self.bv[:, :], io["L1_xattn_bv"].rearrange("(a n) -> a n", a=1).broadcast_to([P, P])).then_inc(self.loaded, 16)
        sp.dma_start(self.bo[:, :], io["L1_xattn_bo"].rearrange("(a n) -> a n", a=1).broadcast_to([P, D])).then_inc(self.loaded, 16)


def second_attention(nc, io, sh, w_in, next_weights):
    with ExitStack() as c:
        sb = lambda n, s, dt=F32: c.enter_context(nc.sbuf_tensor("a1_" + n, s, dt))
        pb = lambda n, s, dt=F32: c.enter_context(nc.psum_tensor("a1_" + n, s, dt))
        sem = lambda n: c.enter_context(nc.semaphore("a1_" + n))
        wk, wv, wo, bq, bk, bv = w_in.wk, w_in.wv, w_in.wo, w_in.bq, w_in.bk, w_in.bv
        ctx, ctx_loaded = w_in.ctx, w_in.ctx_loaded
        wq = sb("wq", [P, KD, G, P])
        wq_sorted = sem("wq_sorted")
        gbo = sb("gbo", [P, D])
        xn, xT, cT = sb("xn", [P, 2, D]), sb("xT", [P, KD, P]), sb("cT", [P, KD, P])
        QT = sb("QT", [P, 2, BPT, G, S])
        QR = sb("QR", [P, BPT, G, S], F32R)
        KT = sb("KT", [P, BPT, S])
        KB = sb("KB", [P, 2, BPT, KP, 2, S])
        KR = sb("KR", [P, BPT, KP, 2, S], F32R)
        VB = sb("VB", [P, 2, BPT, KP, 2, 2, HD])
        E = sb("E", [P, 2, 2, G * S])
        nmax = sb("nmax", [P, BPT, 2, NKV])
        nmaxT = sb("nmaxT", [P, P], F32R)
        sel = sb("sel", [P, BPT, 2, KP, P], F32R)
        den, rec, yraw = (sb(n, [P, BPT, G, S]) for n in ("den", "rec", "yraw"))
        yT, yh, yl = sb("yT", [P, G, BPT, S]), sb("yh", [P, G, BPT, S], F32R), sb("yl", [P, G, BPT, S], F32R)
        woh, wol = sb("woh", [P, G, D], F32R), sb("wol", [P, G, D], F32R)
        wo_high, wo_split, y_high, y_low = (sem(n) for n in ("wo_high", "wo_split", "y_high", "y_low"))
        pX, pC = pb("pX", [P, KD, P]), pb("pC", [P, KD, P])
        pM = [pb(f"pM{k}", [P, KP * 2, S]) for k in range(2)]
        pE = [pb(f"pE{k}", [P, 2, G * S]) for k in range(2)]
        pY = pb("pY", [P, BPT, 2, G, S])
        vector_set, zeroed, gbo_ready = sem("vector_set"), sem("zeroed"), sem("gbo_ready")
        xn_ready, biased = sem("xn_ready"), sem("biased")
        x_turned, turned, xT_copied, cT_copied = sem("x_turned"), sem("turned"), sem("xT_copied"), sem("cT_copied")
        kv_done, q_done, k_copied, k_spread, k_rounded, v_spread, q_copied, q_rounded = (
            sem(n) for n in ("kv_done", "q_done", "k_copied", "k_spread", "k_rounded", "v_spread", "q_copied", "q_rounded"))
        scored, maxed, max_turned, max_copied = sem("scored"), sem("maxed"), sem("max_turned"), sem("max_copied")
        keyed, exped, weighed, inverted, normed = (sem(n) for n in ("keyed", "exped", "weighed", "inverted", "normed"))
        y_copied = [sem(f"y_copied{b}") for b in range(BPT)]
        out_done, added = sem("out_done"), sem("added")
        block = c.enter_context(nc.Block())

        @block.sync
        def _(sp):
            c_in = io["ctx_4096"].rearrange("(i b) s d -> (b s) i d", b=BPT)
            def body(it, b, live, past):
                if live(1):
                    if past(1, 2):
                        sp.wait_ge(turned, it)
                    sp.dma_start(ctx[:, 1 - b, :], c_in[:, bass.ds(it + 1, 1), :].rearrange("p a d -> p (a d)")).then_inc(ctx_loaded[1 - b], 32)
            over_tiles(sp, body, 0, 0)
            next_weights.load(sp, io)

        @block.gpsimd
        def _(pool):
            pool.memset(VB[:, :, :, :, :, :, :].rearrange("p a b k o e n -> p (a b k o e n)"), 0.0).then_inc(zeroed, 1)
            pool.memset(KB[:, :, :, :, :, :].rearrange("p a b k e s -> p (a b k e s)"), 0.0).then_inc(zeroed, 1)
            pool.wait_ge(gbo_ready, 1)

            def body(it, b, live, past):
                if live(0):
                    pool.wait_ge(xn_ready, it + 1)
                    xt = sh.x[:, it, :]
                    pool.tensor_tensor(xt, xt, gbo[:, :], ALU.add).then_inc(biased, 1)
            over_tiles(pool, body, 0, 0)

        @block.tensor
        def _(pe):
            pe.wait_ge(w_in.loaded, w_in.loads)

            def scores(t, a, b, kh):
                n = 4 * t + 2 * b + kh
                if not (isinstance(t, int) and t == 0 and b == 0):
                    pe.wait_ge(exped, n - 1)
                for j in range(2):
                    kp = 2 * kh + j
                    pe.matmul(pE[kh][:, j, :], KB[:, a, b, kp, :, :].rearrange("p e s -> p (e s)"),
                              QT[:, a, b, :, :].rearrange("p g s -> p (g s)"), start=True, stop=False,
                              skip_group_check=True)
                    for gp in range(2):
                        mm = pe.matmul(pE[kh][:, j, gp * 2 * S:(gp + 1) * 2 * S], sel[:, b, gp, kp, :], nmaxT[:, :],
                                       start=False, stop=(gp == 1), skip_group_check=True)
                mm.then_inc(keyed, 1)

            def weigh(t, a, b, kh):
                n = 4 * t + 2 * b + kh
                pe.wait_ge(exped, n + 1)
                if kh == 0 and not (isinstance(t, int) and t == 0):
                    pe.wait_ge(y_copied[b], t)
                for j in range(2):
                    mm = pe.matmul(pY[64 * j:64 * j + 64, b, kh, :, :].rearrange("p g s -> p (g s)"),
                                   VB[:, a, b, 2 * kh + j, :, :, :].rearrange("p o e n -> p (o e n)"),
                                   E[:, kh, j, :], start=True, stop=True, skip_group_check=True)
                mm.then_inc(weighed, 1)

            def row_scores(it, b, gp):
                pe.matmul(pM[gp][:, :, :].rearrange("p a b -> p (a b)"), QR[:, b, 2 * gp:2 * gp + 2, :].rearrange("p g s -> p (g s)"),
                          KR[:, b, :, :, :].rearrange("p k e s -> p (k e s)"), start=True, stop=True).then_inc(scored, 1)

            def body(it, a, live, past):
                o = 1 - a
                if live(0):
                    pe.wait_ge(xn_ready, it + 1)
                    if past(0, 1):
                        pe.wait_ge(q_copied, it)
                    for k in range(KD):
                        mm = pe.transpose(pX[:, k, :], xn[:, a, k * P:(k + 1) * P], sh.ident[:, :])
                    mm.then_inc(x_turned, 1)
                    pe.wait_ge(ctx_loaded[a], 16 * (it - a) + 32)
                    if past(0, 1):
                        pe.wait_ge(v_spread, it)
                        pe.wait_ge(k_copied, it)
                    if past(0, 3):
                        pe.wait_ge(added, it - 2)
                    for k in range(KD):
                        mm = pe.transpose(pC[:, k, :], ctx[:, a, k * P:(k + 1) * P], sh.ident[:, :])
                    mm.then_inc(turned, 1)
                if live(-1):
                    if not past(-1, 1):
                        pe.wait_ge(vector_set, 2)
                    pe.wait_ge(maxed, 4 * it)
                    pe.transpose(pM[0][0:32, 0:2, :].rearrange("p a b -> p (a b)"), nmax[:, :, :, :].rearrange("p b g h -> p (b g h)"),
                                 sh.ident[:, :]).then_inc(max_turned, 1)
                if live(0):
                    pe.wait_ge(cT_copied, it + 1)
                    for k in range(KD):
                        pe.matmul(pC[:, 0, :], wk[:, k, :], cT[:, k, :], start=(k == 0), stop=(k == KD - 1))
                    for k in range(KD):
                        mm = pe.matmul(pC[:, 1, :], cT[:, k, :], wv[:, k, :], start=(k == 0), stop=(k == KD - 1))
                    mm.then_inc(kv_done, 1)
                if live(-1):
                    pe.wait_ge(max_copied, it)
                    scores(it - 1, o, 0, 0)
                    scores(it - 1, o, 0, 1)
                    weigh(it - 1, o, 0, 0)
                    scores(it - 1, o, 1, 0)
                    weigh(it - 1, o, 0, 1)
                if live(0):
                    pe.wait_ge(xT_copied, it + 1)
                    if not past(0, 1):
                        pe.wait_ge(wq_sorted, KD)
                    for g in range(G):
                        for k in range(KD):
                            mm = pe.matmul(pX[:, g, :], wq[:, k, g, :], xT[:, k, :], start=(k == 0), stop=(k == KD - 1))
                    mm.then_inc(q_done, 1)
                if live(-1):
                    scores(it - 1, o, 1, 1)
                    weigh(it - 1, o, 1, 0)
                if live(-2):
                    if not past(-2, 1):
                        pe.wait_ge(wo_split, 1)
                    pe.wait_ge(y_low, it - 1)
                    if live(0):
                        pe.wait_ge(v_spread, it + 1)
                        pe.wait_ge(k_copied, it + 1)
                for half in range(2):
                    if live(-2):
                        for g in (2 * half, 2 * half + 1):
                            for y, w in ((yh, woh), (yh, wol), (yl, woh)):
                                mm = pe.matmul(pC[:, :, :].rearrange("p a b -> p (a b)"), y[:, g, :, :].rearrange("p b s -> p (b s)"),
                                               w[:, g, :], start=(g == 0 and w is woh and y is yh), stop=(g == G - 1 and y is yl))
                        if half == 1:
                            mm.then_inc(out_done, 1)
                    if half == 0 and live(0):
                        pe.wait_ge(k_rounded, it + 1)
                        pe.wait_ge(q_rounded, it + 1)
                        if past(0, 1):
                            pe.wait_ge(max_copied, it)
                        row_scores(it, 0, 0)
                        row_scores(it, 0, 1)
                if live(-1):
                    weigh(it - 1, o, 1, 1)
                if live(0):
                    for gp in range(2):
                        pe.wait_ge(maxed, 4 * it + gp + 1)
                        row_scores(it, 1, gp)
            over_tiles(pe, body, 0, 2)

        @block.scalar
        def _(act):
            act.wait_ge(w_in.loaded, w_in.loads)
            for k in range(KD):
                act.activation(wq[:, k, :, :].rearrange("p g (h e) -> p g h e", h=NKV),
                               w_in.wq[:, k, :].rearrange("p (h g e) -> p g h e", h=NKV, g=G), ACT.Copy).then_inc(wq_sorted, 1)

            def exp(t, b, kh):
                n = 4 * t + 2 * b + kh
                act.wait_ge(keyed, n + 1)
                if not (isinstance(t, int) and t == 0 and b == 0):
                    act.wait_ge(weighed, n - 1)
                act.activation(E[:, kh, :, :], pE[kh][:, :, :], ACT.Exp, scale=HD ** -0.5).then_inc(exped, 1)

            def copy_y(t, b):
                act.wait_ge(weighed, 4 * t + 2 * b + 2)
                for kp in range(KP):
                    mine, at = slice(32 * kp, 32 * kp + 32), 64 * (kp % 2)
                    act.activation(yraw[mine, b, :, :], pY[at:at + 32, b, kp // 2, :, :], ACT.Copy)
                    i = act.activation(den[mine, b, :, :], pY[at + 32:at + 64, b, kp // 2, :, :], ACT.Copy)
                i.then_inc(y_copied[b], 1)

            def body(it, a, live, past):
                if live(0):
                    act.wait_ge(turned, it + 1)
                    act.activation(cT[:, :, :], pC[:, :, :], ACT.Copy).then_inc(cT_copied, 1)
                if live(-2):
                    copy_y(it - 2, 1)
                if live(-1):
                    exp(it - 1, 0, 0)
                    exp(it - 1, 0, 1)
                if live(0):
                    act.wait_ge(kv_done, it + 1)
                    if past(0, 1):
                        act.wait_ge(k_spread, it)
                    act.activation(KT[:, :, :].rearrange("p b s -> p (b s)"), pC[:, 0, :], ACT.Identity, bias=bk[:, :]).then_inc(k_copied, 1)
                if live(-2):
                    act.wait_ge(normed, it - 1)
                    if past(-2, 1):
                        act.wait_ge(out_done, it - 2)
                    act.activation(yh[:, :, :, :], yT[:, :, :, :], ACT.Copy).then_inc(y_high, 1)
                if live(-1):
                    exp(it - 1, 1, 0)
                if live(0):
                    act.wait_ge(q_done, it + 1)
                    for g in range(G):
                        q = act.activation(QT[:, a, :, g, :], pX[:, g, :].rearrange("p (b s) -> p b s", b=BPT), ACT.Identity, bias=bq[:, g:g + 1])
                    q.then_inc(q_copied, 1)
                    if not past(0, 1):
                        act.activation(woh[:, :, :], wo[:, :, :], ACT.Copy).then_inc(wo_high, 1)
                if live(-1):
                    exp(it - 1, 1, 1)
                    if past(-1, 1):
                        act.wait_ge(normed, it - 1)
                    copy_y(it - 1, 0)
            over_tiles(act, body, 0, 2)

        @block.vector
        def _(dve):
            def normalize(t, u):
                if not (isinstance(t, int) and t < 2):
                    dve.wait_ge(turned, t - 1)
                dve.tensor_scalar(xn[:, u, :], sh.x[:, t, :], sh.rstd[:, bass.ds(t, 1)], sh.nmr[:, bass.ds(t, 1)],
                                  ALU.mult, ALU.add).then_inc(xn_ready, 1)

            normalize(0, 0)
            rows = BPT * 2 * NKV
            dve.tensor_copy(sel[:, :, :, :, :].rearrange("p b g k (e s) -> p (b g k e) s", e=2),
                            sh.ident[:, 0:rows].rearrange("p (n a) -> p n a", a=1).broadcast_to([P, rows, S])).then_inc(vector_set, 1)
            dve.memset(nmaxT[:, :].bitcast(F32), 0.0).then_inc(vector_set, 1)
            dve.wait_ge(vector_set, 2)
            dve.wait_ge(zeroed, 2)
            for e in range(2):
                dve.memset(VB[64 * e:64 * e + 64, :, :, :, 1, e, :].rearrange("p a b k n -> p (a b k) n"), 1.0)
            dve.wait_ge(w_in.loaded, w_in.loads)
            dve.tensor_scalar(gbo[:, :], w_in.bo[:, :], sh.tanh_g[:, 2:3], None, ALU.mult).then_inc(gbo_ready, 1)

            def body(it, a, live, past):
                o = 1 - a
                if live(0):
                    dve.wait_ge(x_turned, it + 1)
                    dve.tensor_copy(xT[:, :, :], pX[:, :, :]).then_inc(xT_copied, 1)
                if live(-1):
                    dve.wait_ge(max_turned, it)
                    dve.tensor_copy(nmaxT[0:32, :], pM[0][0:32, 0:2, :].rearrange("p a b -> p (a b)")).then_inc(max_copied, 1)
                if live(-2):
                    for b in range(BPT):
                        dve.wait_ge(y_copied[b], it - 1)
                    dve.reciprocal(rec[:, :, :, :], den[:, :, :, :]).then_inc(inverted, 1)
                if live(0):
                    dve.wait_ge(k_copied, it + 1)
                    for b in range(BPT):
                        rows = slice(64 * b, 64 * b + 64)
                        for e in range(2):
                            dst = VB[64 * e:64 * e + 64, a, b, :, 0, e, :]
                            src = pC[rows, 1, :].rearrange("p (k e n) -> p k e n", k=KP, e=2)[:, :, e, :]
                            bias = bv[rows, :].rearrange("p (k e n) -> p k e n", k=KP, e=2)[:, :, e, :]
                            v = dve.tensor_tensor(dst, src, bias, ALU.add)
                    v.then_inc(v_spread, 1)
                if live(0):
                    for q in range(KP):
                        rows = slice(32 * q, 32 * q + 32)
                        src = KT[rows, :, :].rearrange("p b (e s) -> p b e s", e=1).broadcast_to([32, BPT, 2, S])
                        keep = sh.odd[rows, :].rearrange("p (b e s) -> p b e s", b=1, s=1).broadcast_to([32, BPT, 2, S])
                        k = dve.tensor_tensor(KB[rows, a, :, q, :, :], src, keep, ALU.mult)
                    k.then_inc(k_spread, 1)
                if live(-1) and not past(-1, 1):
                    dve.wait_ge(wo_high, 1)
                    dve.tensor_tensor(wol[:, :, :], wo[:, :, :], woh[:, :, :], ALU.subtract).then_inc(wo_split, 1)
                if live(-2):
                    dve.wait_ge(inverted, it - 1)
                    if past(-2, 1):
                        dve.wait_ge(y_low, it - 2)
                    dve.tensor_tensor(yT[:, :, :, :].rearrange("p g b s -> p b g s"), yraw[:, :, :, :], rec[:, :, :, :], ALU.mult).then_inc(normed, 1)
                if live(1):
                    normalize(it + 1, o)
                if live(0):
                    dve.wait_ge(k_spread, it + 1)
                    dve.tensor_copy(KR[:, :, :, :, :].rearrange("p b k e s -> p (b k e s)"),
                                    KB[:, a, :, :, :, :].rearrange("p b k e s -> p (b k e s)")).then_inc(k_rounded, 1)
                if live(-2):
                    dve.wait_ge(y_high, it - 1)
                    if past(-2, 1):
                        dve.wait_ge(out_done, it - 2)
                    dve.tensor_tensor(yl[:, :, :, :], yT[:, :, :, :], yh[:, :, :, :], ALU.subtract).then_inc(y_low, 1)
                if live(0):
                    dve.wait_ge(q_copied, it + 1)
                    dve.tensor_copy(QR[:, :, :, :].rearrange("p b g s -> p (b g s)"),
                                    QT[:, a, :, :, :].rearrange("p b g s -> p (b g s)")).then_inc(q_rounded, 1)
                for b in range(BPT):
                    if b == 1 and live(-2):
                        dve.wait_ge(added, it - 1)
                    if live(0):
                        for gp in range(2):
                            dve.wait_ge(scored, 4 * it + 2 * b + gp + 1)
                            dve.tensor_reduce(nmax[:, b, gp, :], pM[gp][:, :, :], AX.X, ALU.max, negate=True).then_inc(maxed, 1)
                    if b == 0 and live(-2):
                        t = it - 2
                        dve.wait_ge(out_done, t + 1)
                        dve.wait_ge(biased, t + 1)
                        dve.scalar_tensor_tensor(sh.x[:, t, :], pC[:, :, :].rearrange("p a b -> p (a b)"), sh.tanh_g[:, 2:3],
                                                 sh.x[:, t, :], ALU.mult, ALU.add).then_inc(added, 1)
                if live(-2):
                    dve.bn_stats(sh.stats[:, it - 2, :], sh.x[:, it - 2, :])
            over_tiles(dve, body, 0, 2)


C, CODES, SUB = 32, 32, 16
NCL = 32
CLS = D // NCL
CG = P // CODES
NU = C // CG
VAR_STEPS = 5


class SecondFfnWeights:

    def __init__(self, nc, c):
        sb = lambda n, s, dt=F32: c.enter_context(nc.sbuf_tensor("f1_" + n, s, dt))
        self.books = sb("books_in", [P, NU, SUB])
        self.codes, self.cents = sb("codes", [P, NU, D], I32), sb("cents", [P, NU, NCL], I32)
        self.bias, self.lnw = sb("bias", [P, D]), sb("lnw", [P, NCL])
        self.loaded = c.enter_context(nc.semaphore("f1_w_loaded"))
        self.loads = 16 * (1 + 2 * CG + 2)

    def load(self, sp, io):
        sp.dma_start(self.books[:, :, :], io["L1_ffn_codebooks"].rearrange("(u c) k s -> (c k) u s", c=CG)).then_inc(self.loaded, 16)
        cents_in = io["L1_ffn_centroids"].rearrange("(u c a) n -> c a u n", c=CG, a=1)
        codes_in = io["L1_ffn_codes"].rearrange("(u c a) n -> c a u n", c=CG, a=1)
        for q in range(CG):
            rows = slice(q * CODES, (q + 1) * CODES)
            sp.dma_start(self.cents[rows, :, :], cents_in[q].broadcast_to([CODES, NU, NCL])).then_inc(self.loaded, 16)
            sp.dma_start(self.codes[rows, :, :], codes_in[q].broadcast_to([CODES, NU, D])).then_inc(self.loaded, 16)
        sp.dma_start(self.bias[:, :], io["L1_ffn_bias"].rearrange("(a n) -> a n", a=1).broadcast_to([P, D])).then_inc(self.loaded, 16)
        sp.dma_start(self.lnw[:, :], io["L1_ffn_ln_weight"].rearrange("(a n) -> a n", a=1).broadcast_to([P, NCL])).then_inc(self.loaded, 16)


def second_ffn(nc, io, out, sh, w_in):
    with ExitStack() as c:
        sb = lambda n, s, dt=F32: c.enter_context(nc.sbuf_tensor("f1_" + n, s, dt))
        pb = lambda n, s, dt=F32: c.enter_context(nc.psum_tensor("f1_" + n, s, dt))
        sem = lambda n: c.enter_context(nc.semaphore("f1_" + n))
        books_in, codes, cents, bias, lnw = w_in.books, w_in.codes, w_in.cents, w_in.bias, w_in.lnw
        books = sb("books", [P, NU, P])
        code_id, code_idf = sb("code_id", [P, 1], I32), sb("code_idf", [P, 1])
        bh, bl = sb("bh", [P, NU, P], F32R), sb("bl", [P, NU, P], F32R)
        hot = sb("hot", [P, 2, D], F32R)
        hotc = sb("hotc", [P, NU, NCL])
        Wh, Wl, cT = sb("Wh", [P, KD, D], F32R), sb("Wl", [P, KD, D], F32R), sb("cT", [P, KD, NCL])
        y = sb("y", [P, N, D])
        xn, xT = sb("xn", [P, 2, D]), sb("xT", [P, 2, KD, P])
        xh, xl = sb("xh", [P, 2, KD, P], F32R), sb("xl", [P, 2, KD, P], F32R)
        dots, cen, z = sb("dots", [P, N, NCL]), sb("cen", [P, N, NCL]), sb("z", [P, N, NCL])
        (mean, var, std, rs, rs2, top, total, kept, keep_t) = (sb(n, [P, N]) for n in ("mean", "var", "std", "rs", "rs2", "top", "total", "kept", "keep_t"))
        used, keep_c = sb("used", [P, NCL]), sb("keep_c", [P, NCL])
        pW = [pb(f"pW{k}", [P, D]) for k in range(2)]
        pCW = pb("pCW", [P, KD, NCL])
        pX = [pb(f"pX{k}", [P, KD, P]) for k in range(2)]
        pDot = [pb(f"pDot{k}", [P, NCL]) for k in range(2)]
        zeroed, ids, ids_float, books_ready = sem("zeroed"), sem("ids"), sem("ids_float"), sem("books_ready")
        hot_ready, hotc_ready, expanded, w_high, w_copied, cents_expanded, cents_copied = (
            sem(n) for n in ("hot_ready", "hotc_ready", "expanded", "w_high", "w_copied", "cents_expanded", "cents_copied"))
        xn_ready, turned, x_high, x_low, dots_done, product, dots_used, product_used = (
            sem(n) for n in ("xn_ready", "turned", "x_high", "x_low", "dots_done", "product", "dots_used", "product_used"))
        step, std_ready, z_ready, exp_ready, used_ready, counted = (
            sem(n) for n in ("mask_step", "std_ready", "z_ready", "exp_ready", "used_ready", "counted"))
        cols_ready, masked, masked_pool, finished = (sem(n) for n in ("cols_ready", "masked", "masked_pool", "finished"))
        stored, books_split = sem("stored"), sem("books_split")
        block = c.enter_context(nc.Block())
        ON_V = N // 4
        x_out = out.rearrange("(i b) s d -> (b s) i d", b=BPT)

        by_cluster = lambda t: y[:, bass.ds(t, 1), :].rearrange("p a (c n) -> p (a c) n", c=NCL)
        columns = lambda: keep_c[:, :].rearrange("p (c a) -> p c a", a=1).broadcast_to([P, NCL, CLS])

        @block.sync
        def _(sp):
            def body(it, b, live, past):
                if live(0):
                    sp.wait_ge(finished, it + 1)
                    sp.dma_start(x_out[:, bass.ds(it, 1), :].rearrange("p a d -> p (a d)"), sh.x[:, it, :]).then_inc(stored, 16)
            over_tiles(sp, body, 0, 0)
            sp.wait_ge(stored, 16 * N)

        @block.gpsimd
        def _(pool):
            pool.memset(books[:, :, :], 0.0).then_inc(zeroed, 1)
            for q in range(CG):
                pool.iota(code_id[q * CODES:(q + 1) * CODES, :], pattern=[[0, 1]], base=0, channel_multiplier=1).then_inc(ids, 1)
                pool.wait_ge(ids, q + 1)
            pool.wait_ge(cols_ready, 1)
            pool.wait_ge(product_used, N)
            with pool.Fori(ON_V, N, 1) as t:
                yt = by_cluster(t)
                pool.tensor_tensor(yt, yt, columns(), ALU.mult).then_inc(masked_pool, 1)

        @block.tensor
        def _(pe):
            pe.wait_ge(books_ready, 1)
            pe.wait_ge(hotc_ready, 1)
            for u in range(NU):
                mm = pe.matmul(pCW[64 * (u % 2):64 * (u % 2) + 64, u // 2, :], books[:, u, 64 * (u % 2):64 * (u % 2) + 64], hotc[:, u, :], start=True, stop=True)
            mm.then_inc(cents_expanded, 1)
            for u in range(NU):
                pe.wait_ge(hot_ready, u + 1)
                if u >= 4 and u % 2 == 0:
                    pe.wait_ge(w_copied, u // 2 - 1)
                pe.matmul(pW[u // 2 % 2][:, :], bh[:, u, :], hot[:, u % 2, :], start=(u % 2 == 0), stop=False)
                pe.matmul(pW[u // 2 % 2][:, :], bl[:, u, :], hot[:, u % 2, :], start=False, stop=(u % 2 == 1)).then_inc(expanded, 1)

            def body(it, b, live, past):
                if live(0):
                    pe.wait_ge(xn_ready, it + 1)
                    if past(0, 2):
                        pe.wait_ge(x_low, it - 1)
                    for k in range(KD):
                        mm = pe.transpose(pX[b][:, k, :], xn[:, b, k * P:(k + 1) * P], sh.ident[:, :])
                    mm.then_inc(turned, 1)
                if live(-1):
                    o = 1 - b
                    if not past(-1, 1):
                        pe.wait_ge(cents_copied, 1)
                        pe.wait_ge(w_copied, KD)
                    pe.wait_ge(x_high, it)
                    if past(-1, 2):
                        pe.wait_ge(dots_used, it - 2)
                        pe.wait_ge(product_used, it - 2)
                    for k in range(KD):
                        mm = pe.matmul(pDot[o][:, :], xT[:, o, k, :], cT[:, k, :], start=(k == 0), stop=(k == KD - 1))
                    mm.then_inc(dots_done, 1)
                    for k in range(KD):
                        pe.matmul(pW[o][:, :], xh[:, o, k, :], Wh[:, k, :], start=(k == 0), stop=False)
                        pe.matmul(pW[o][:, :], xh[:, o, k, :], Wl[:, k, :], start=False, stop=False)
                    pe.wait_ge(x_low, it)
                    for k in range(KD):
                        mm = pe.matmul(pW[o][:, :], xl[:, o, k, :], Wh[:, k, :], start=False, stop=(k == KD - 1))
                    mm.then_inc(product, 1)
            over_tiles(pe, body, 0, 1)
            pe.wait_ge(used_ready, 1)
            pe.matmul(pCW[:, 0, :], sh.ones[:, :], used[:, :], start=True, stop=True).then_inc(counted, 1)

        @block.scalar
        def _(act):
            for k in range(KD):
                act.wait_ge(expanded, 2 * k + 2)
                act.activation(Wh[:, k, :], pW[k % 2][:, :], ACT.Copy).then_inc(w_high, 1)

            def body(it, b, live, past):
                if live(0):
                    act.wait_ge(turned, it + 1)
                    if past(0, 2):
                        act.wait_ge(product, it - 1)
                    act.activation(xT[:, b, :, :], pX[b][:, :, :], ACT.Copy)
                    act.activation(xh[:, b, :, :], pX[b][:, :, :], ACT.Copy).then_inc(x_high, 1)
            over_tiles(act, body, 0, 0)
            act.wait_ge(step, VAR_STEPS)
            act.activation(std[:, :], var[:, :], ACT.Sqrt, bias=sh.eps[:, :], scale=1.0 / NCL).then_inc(std_ready, 1)
            act.wait_ge(z_ready, 1)
            act.activation(z[:, :, :], cen[:, :, :], ACT.Exp).then_inc(exp_ready, 1)

        @block.vector
        def _(dve):
            dve.wait_ge(zeroed, 1)
            dve.wait_ge(w_in.loaded, w_in.loads)
            for q in range(CG):
                rows = slice(q * CODES, (q + 1) * CODES)
                for half in range(2):
                    at = half * CG * SUB + q * SUB
                    i = dve.tensor_copy(books[rows, half::2, at:at + SUB], books_in[rows, half::2, :])
            i.then_inc(books_ready, 1)
            dve.wait_ge(ids, CG)
            dve.tensor_copy(code_idf[:, :], code_id[:, :]).then_inc(ids_float, 1)
            dve.wait_ge(books_ready, 1)
            dve.tensor_copy(bh[:, :, :], books[:, :, :]).then_inc(books_split, 1)
            dve.wait_ge(ids_float, 1)
            dve.tensor_scalar(hotc[:, :, :], cents[:, :, :], code_idf[:, :], None, ALU.is_equal).then_inc(hotc_ready, 1)
            dve.wait_ge(books_split, 1)
            dve.tensor_tensor(bl[:, :, :], books[:, :, :], bh[:, :, :], ALU.subtract)

            def low_part(k):
                dve.wait_ge(w_high, k + 1)
                dve.tensor_tensor(Wl[:, k, :], pW[k % 2][:, :], Wh[:, k, :], ALU.subtract).then_inc(w_copied, 1)

            def normalize(t, u):
                if not (isinstance(t, int) and t < 2):
                    dve.wait_ge(turned, t - 1)
                dve.tensor_scalar(xn[:, u, :], sh.x[:, t, :], sh.rstd[:, bass.ds(t, 1)], sh.nmr[:, bass.ds(t, 1)],
                                  ALU.mult, ALU.add).then_inc(xn_ready, 1)

            for u in range(NU):
                if u >= 2:
                    dve.wait_ge(expanded, u - 1)
                dve.tensor_scalar(hot[:, u % 2, :], codes[:, u, :], code_idf[:, :], None, ALU.is_equal).then_inc(hot_ready, 1)
                if u == 2:
                    dve.wait_ge(cents_expanded, 1)
                    dve.tensor_copy(cT[:, :, :], pCW[:, :, :]).then_inc(cents_copied, 1)
                if u % 2 == 1 and u >= 3:
                    low_part(u // 2 - 1)
            normalize(0, 0)
            low_part(KD - 1)

            def body(it, b, live, past):
                if live(1):
                    normalize(it + 1, 1 - b)
                if live(0):
                    dve.wait_ge(x_high, it + 1)
                    if past(0, 2):
                        dve.wait_ge(product, it - 1)
                    dve.tensor_tensor(xl[:, b, :, :], pX[b][:, :, :], xh[:, b, :, :], ALU.subtract).then_inc(x_low, 1)
                if live(-1):
                    t, o = it - 1, 1 - b
                    dve.wait_ge(dots_done, it)
                    dve.tensor_scalar(dots[:, t, :], pDot[o][:, :], 1.0, None, ALU.mult).then_inc(dots_used, 1)
                    dve.wait_ge(product, it)
                    dve.tensor_tensor(y[:, t, :], pW[o][:, :], bias[:, :], ALU.add).then_inc(product_used, 1)
            over_tiles(dve, body, 0, 1)

            st = Steps(dve, step, 0, 0)
            over = lambda a: a[:, :].rearrange("p (n a) -> p n a", a=1).broadcast_to([P, N, NCL])
            dve.wait_ge(dots_used, N)
            st.done(dve.tensor_reduce(mean[:, :], dots[:, :, :], AX.X, ALU.add))
            st.done(dve.tensor_scalar(rs[:, :], mean[:, :], 1.0 / NCL, None, ALU.mult))
            st.done(dve.tensor_tensor(cen[:, :, :], dots[:, :, :], over(rs), ALU.subtract))
            st.done(dve.tensor_tensor(z[:, :, :], cen[:, :, :], cen[:, :, :], ALU.mult))
            st.done(dve.tensor_reduce(var[:, :], z[:, :, :], AX.X, ALU.add))
            assert st.n == VAR_STEPS
            dve.wait_ge(std_ready, 1)
            st.done(dve.reciprocal(rs[:, :], std[:, :]))
            st.mark(dve.tensor_scalar(std[:, :], var[:, :], 1.0 / NCL, EPS, ALU.mult, ALU.add))
            st.done(dve.tensor_tensor(rs2[:, :], rs[:, :], rs[:, :], ALU.mult))
            st.done(dve.tensor_tensor(mean[:, :], std[:, :], rs2[:, :], ALU.mult))
            st.done(dve.tensor_scalar(rs2[:, :], mean[:, :], -0.5, 1.5, ALU.mult, ALU.add))
            st.done(dve.tensor_tensor(mean[:, :], rs[:, :], rs2[:, :], ALU.mult))
            st.done(dve.tensor_tensor(z[:, :, :], cen[:, :, :], over(mean), ALU.mult))
            st.done(dve.tensor_tensor(dots[:, :, :], z[:, :, :],
                                      lnw[:, :].rearrange("p (a c) -> p a c", a=1).broadcast_to([P, N, NCL]), ALU.mult))
            st.done(dve.tensor_reduce(top[:, :], dots[:, :, :], AX.X, ALU.max))
            dve.tensor_tensor(cen[:, :, :], dots[:, :, :], over(top), ALU.subtract).then_inc(z_ready, 1)
            dve.wait_ge(exp_ready, 1)
            st.done(dve.tensor_reduce(total[:, :], z[:, :, :], AX.X, ALU.add))
            st.done(dve.tensor_scalar(rs[:, :], total[:, :], 0.5, None, ALU.mult))
            st.done(dve.tensor_tensor(dots[:, :, :], z[:, :, :], over(rs), ALU.is_gt))
            st.done(dve.tensor_reduce(kept[:, :], dots[:, :, :], AX.X, ALU.max))
            dve.tensor_reduce(used[:, :], dots[:, :, :].rearrange("p n c -> p c n"), AX.X, ALU.max).then_inc(used_ready, 1)
            st.done(dve.tensor_scalar(keep_t[:, :], kept[:, :], sh.tanh_g[:, 3:4], None, ALU.mult))
            dve.wait_ge(counted, 1)
            dve.tensor_scalar(keep_c[:, :], pCW[:, 0, :], 0.5, None, ALU.is_gt).then_inc(cols_ready, 1)
            dve.wait_ge(cols_ready, 1)
            dve.wait_ge(product_used, N)

            def mask(t):
                yt = by_cluster(t)
                dve.tensor_tensor(yt, yt, columns(), ALU.mult).then_inc(masked, 1)

            def finish(t):
                dve.scalar_tensor_tensor(sh.x[:, t, :], y[:, t, :], keep_t[:, bass.ds(t, 1)], sh.x[:, t, :], ALU.mult, ALU.add).then_inc(finished, 1)

            mask(0)
            with dve.Fori(0, ON_V - 1, 1) as t:
                mask(t + 1)
                dve.wait_ge(masked, t + 1)
                finish(t)
            dve.wait_ge(masked, ON_V)
            finish(ON_V - 1)
            with dve.Fori(ON_V, N, 1) as t:
                dve.wait_ge(masked_pool, t - (ON_V - 1))
                finish(t)


class Shared:
    pass


def flamingo(nc, io, out):
    sh = Shared()
    with ExitStack() as c:
        sb = lambda n, s, dt=F32: c.enter_context(nc.sbuf_tensor(n, s, dt))
        sh.x = sb("x", [P, N, D])
        sh.ident, sh.identb, sh.ones = sb("ident", [P, P]), sb("identb", [P, P], BF16), sb("ones", [P, P])
        sh.odd = sb("odd", [P, 2])
        sh.tanh_g, sh.scales = sb("tanh_g", [P, 4]), sb("scales", [P, 3])
        sh.wmean, sh.wscale = sb("wmean", [P, 3]), sb("wscale", [P, 3])
        sh.eps, sh.round = sb("eps", [P, 1]), sb("round", [P, 1])
        sh.stats = sb("stats", [P, N, 6])
        sh.rstd, sh.nmr = sb("rstd_all", [P, N]), sb("nmr_all", [P, N])
        sh.gateT, sh.upT = sb("gateT", [P, KD, FF], BF16), sb("upT", [P, KD, FF], BF16)
        sh.downT = sb("downT", [P, FJ, D], BF16)
        x_loaded = [c.enter_context(nc.semaphore(f"x_loaded{k}")) for k in range(N // XT)]
        consts_set = c.enter_context(nc.semaphore("consts_set"))
        a0 = FirstAttentionConstants(nc, c)
        with ExitStack() as raw_stack:
            raw = FirstFfnRaw(nc, raw_stack)
            with nc.Block() as block:
                @block.vector
                def _(dve):
                    dve.memset(a0.wnat[:, :, :], 0.0).then_inc(a0.zeroed, 1)
                    dve.memset(sh.eps[:, :], EPS).then_inc(consts_set, 1)
                    dve.memset(sh.round[:, :], ROUND).then_inc(consts_set, 1)
                    dve.wait_ge(consts_set, 2)

            def loads(sp):
                x_in = io["x"].rearrange("(n i b) s d -> n (b s) i d", b=BPT, i=XT)
                for n in range(N // XT):
                    sp.dma_start(sh.x[:, n * XT:(n + 1) * XT, :], x_in[n]).then_inc(x_loaded[n], 16)
                raw.load(sp, io)
                a0.load(sp, io)

            layer_norms(nc, sh, "n0_", loads, x_loaded)
            setup(nc, io, sh, raw, a0)
        first_attention(nc, io, sh, a0)
        w1, w2 = SecondAttentionWeights(nc, c), SecondFfnWeights(nc, c)
        first_ffn(nc, io, sh, w1)
        layer_norms(nc, sh, "n2_")
        second_attention(nc, io, sh, w1, w2)
        layer_norms(nc, sh, "n3_")
        second_ffn(nc, io, out, sh, w2)


def kernel(**inputs):
    import numpy as _np
    import concourse.bacc as _bacc
    from concourse import mybir as _mybir
    from concourse.bass_utils import run_bass_kernel_spmd as _run

    nc = _bacc.Bacc("TRN2", target_bir_lowering=False, num_devices=1)
    arrays, io = {}, {}
    for name, value in inputs.items():
        a = _np.ascontiguousarray(value)
        arrays[f"in_{name}"] = a
        io[name] = nc.dram_tensor(f"in_{name}", a.shape, _mybir.dt.from_np(a.dtype), kind="ExternalInput").ap()
    out = nc.dram_tensor("out_0", (B, S, D), F32, kind="ExternalOutput").ap()
    flamingo(nc, io, out)
    r = _run(nc, [arrays], core_ids=[0])
    return r.results[0]["out_0"]
```
